# Optimizing a Trainium2 kernel written in Bass

```python
import numpy as np
import jax
import jax.numpy as jnp

def _softmax(x, axis=-1):
    return jax.nn.softmax(x, axis=axis)

def _gelu(x):
    return jax.nn.gelu(x, approximate=True)

def _silu(x):
    return jax.nn.silu(x)

def _sigmoid(x):
    return jax.nn.sigmoid(x)

def _layernorm(x, axis=-1, eps=1e-05):
    m = jnp.mean(x, axis=axis, keepdims=True)
    v = jnp.var(x, axis=axis, keepdims=True)
    return (x - m) / jnp.sqrt(v + eps)

def _scatter_add(tgt, idx, src, axis=0):
    return tgt.at[idx].add(src)

def _segment_sum(src, seg, n):
    return jax.ops.segment_sum(src, seg, n)
kernel_name = 'mk_seq_postln_d2_jaxref_r8_05439e'

def setup_inputs(seed: int=0):
    np.random.seed(seed)
    _w = jnp.asarray

    def _L0_attn_setup():
        import jax, jax.numpy as jnp
        import numpy as np
        from jax import lax
        D_MODEL = 128
        D_STATE = 128
        D_CONV = 4
        EXPAND = 2
        HEADDIM = 64
        D_INNER = EXPAND * D_MODEL
        NHEADS = D_INNER // HEADDIM
        CONV_DIM = D_INNER + 2 * D_STATE
        D_IN_PROJ = 2 * D_INNER + 2 * D_STATE + NHEADS
        B_SZ, L_SEQ = (4, 256)
        EPS = 1e-05

        def _mamba_block(x, in_proj_w, conv_w, conv_b, dt_bias, A_log, D, norm_w, out_proj_w, ln_w, ln_b):
            b, l, _ = x.shape
            zxbcdt = jnp.einsum('bld,ed->ble', x, in_proj_w)
            z = zxbcdt[..., :D_INNER]
            xBC = zxbcdt[..., D_INNER:D_INNER + CONV_DIM]
            dt = jax.nn.softplus(zxbcdt[..., D_INNER + CONV_DIM:] + dt_bias)
            xBC_t = xBC.transpose(0, 2, 1)
            conv = lax.conv_general_dilated(xBC_t, conv_w[:, None, :], (1,), [(D_CONV - 1, 0)], feature_group_count=CONV_DIM, dimension_numbers=('NCW', 'OIW', 'NCW'))
            xBC = jax.nn.silu(conv + conv_b[:, None]).transpose(0, 2, 1)
            x_ssm = xBC[..., :D_INNER].reshape(b, l, NHEADS, HEADDIM)
            Bm = xBC[..., D_INNER:D_INNER + D_STATE]
            Cm = xBC[..., D_INNER + D_STATE:]
            A = -jnp.exp(A_log)
            dA = jnp.exp(dt * A)

            def step(h, inp):
                dA_t, x_t, B_t, C_t, dt_t = inp
                dBx = dt_t[:, :, None, None] * x_t[..., None] * B_t[:, None, None, :]
                h = h * dA_t[:, :, None, None] + dBx
                y = jnp.einsum('bhpn,bn->bhp', h, C_t)
                return (h, y)
            h0 = jnp.zeros((b, NHEADS, HEADDIM, D_STATE), dtype=x.dtype)
            inputs = (dA.transpose(1, 0, 2), x_ssm.transpose(1, 0, 2, 3), Bm.transpose(1, 0, 2), Cm.transpose(1, 0, 2), dt.transpose(1, 0, 2))
            _, ys = lax.scan(step, h0, inputs)
            y = ys.transpose(1, 0, 2, 3) + D[None, None, :, None] * x_ssm
            y = y.reshape(b, l, D_INNER)
            y = y * jax.nn.silu(z)
            y = y * lax.rsqrt(jnp.mean(y * y, axis=-1, keepdims=True) + EPS) * norm_w
            y = jnp.einsum('bld,ed->ble', y, out_proj_w) + x
            mu = jnp.mean(y, axis=-1, keepdims=True)
            var = jnp.mean((y - mu) ** 2, axis=-1, keepdims=True)
            return (y - mu) * lax.rsqrt(var + EPS) * ln_w + ln_b
        key = jax.random.key(seed)
        ks = jax.random.split(key, 10)
        x = jax.random.normal(ks[0], (B_SZ, L_SEQ, D_MODEL), dtype=jnp.float32)
        in_proj_w = jax.random.normal(ks[1], (D_IN_PROJ, D_MODEL), dtype=jnp.float32) * 0.02
        conv_w = jax.random.normal(ks[2], (CONV_DIM, D_CONV), dtype=jnp.float32) * 0.2
        conv_b = jax.random.normal(ks[3], (CONV_DIM,), dtype=jnp.float32) * 0.02
        dt_bias = jax.random.normal(ks[4], (NHEADS,), dtype=jnp.float32) * 0.5
        A_log = jnp.log(jax.random.uniform(ks[5], (NHEADS,), minval=1.0, maxval=16.0, dtype=jnp.float32))
        D = 1.0 + 0.1 * jax.random.normal(ks[6], (NHEADS,), dtype=jnp.float32)
        norm_w = jnp.ones((D_INNER,), dtype=jnp.float32)
        out_proj_w = jax.random.normal(ks[7], (D_MODEL, D_INNER), dtype=jnp.float32) * 0.02
        ln_w = jnp.ones((D_MODEL,), dtype=jnp.float32)
        ln_b = jnp.zeros((D_MODEL,), dtype=jnp.float32)
        return {'x': x, 'in_proj_w': in_proj_w, 'conv_w': conv_w, 'conv_b': conv_b, 'dt_bias': dt_bias, 'A_log': A_log, 'D': D, 'norm_w': norm_w, 'out_proj_w': out_proj_w, 'ln_w': ln_w, 'ln_b': ln_b}
    _L0_attn_in = _L0_attn_setup()

    def _L0_ffn_setup():
        import jax, jax.numpy as jnp
        import numpy as np
        B, N, DIM = (2, 256, 128)
        HEADS, DIM_HEAD, EXPERTS = (8, 64, 8)
        SCALE = DIM_HEAD ** (-0.5)
        key = jax.random.key(seed)
        ks = jax.random.split(key, 6)
        dim_inner = HEADS * DIM_HEAD
        return {'x': jax.random.normal(ks[0], (B, N, DIM), jnp.float32), 'w_q': jax.random.normal(ks[1], (DIM, dim_inner), jnp.float32) * 0.02, 'w_k': jax.random.normal(ks[2], (DIM, dim_inner), jnp.float32) * 0.02, 'w_gate': jax.random.normal(ks[3], (DIM, HEADS * EXPERTS), jnp.float32) * 0.02, 'value_experts': jax.random.normal(ks[4], (EXPERTS, HEADS, DIM, DIM_HEAD), jnp.float32) * 0.02, 'output_experts': jax.random.normal(ks[5], (EXPERTS, HEADS, DIM_HEAD, DIM), jnp.float32) * 0.02}
    _L0_ffn_in = _L0_ffn_setup()

    def _L1_attn_setup():
        import jax, jax.numpy as jnp
        import numpy as np
        HEADS = 16
        THETA = 10000.0

        def _rope(x):
            b, n, d = x.shape
            half = d // 2
            inv_freq = 1.0 / THETA ** (jnp.arange(0, d, 2, dtype=jnp.float32) / d)
            ang = jnp.arange(n, dtype=jnp.float32)[:, None] * inv_freq
            cos, sin = (jnp.cos(ang), jnp.sin(ang))
            xp = x.reshape(b, n, half, 2)
            x1, x2 = (xp[..., 0], xp[..., 1])
            out = jnp.stack([x1 * cos - x2 * sin, x2 * cos + x1 * sin], axis=-1)
            return out.reshape(b, n, d)
        key = jax.random.key(seed)
        ks = jax.random.split(key, 8)
        B, N, C = (8, 256, 128)
        s = C ** (-0.5)
        return {'x': jax.random.normal(ks[0], (B, N, C), jnp.float32), 'Wq': jax.random.normal(ks[1], (C, C), jnp.float32) * s, 'bq': jax.random.normal(ks[2], (C,), jnp.float32) * 0.01, 'Wk': jax.random.normal(ks[3], (C, C), jnp.float32) * s, 'bk': jax.random.normal(ks[4], (C,), jnp.float32) * 0.01, 'Wv': jax.random.normal(ks[5], (C, C), jnp.float32) * s, 'bv': jax.random.normal(ks[6], (C,), jnp.float32) * 0.01, 'gamma': jnp.ones((C,), jnp.float32), 'beta': jnp.zeros((C,), jnp.float32)}
    _L1_attn_in = _L1_attn_setup()

    def _L1_ffn_setup():
        import jax, jax.numpy as jnp
        import numpy as np
        B, M, D = (4, 256, 128)
        N, P = (64, 32)
        key = jax.random.key(seed)
        k1, k2, k3, k4 = jax.random.split(key, 4)
        x = jax.random.normal(k1, (B, M, D), dtype=jnp.float32)
        phi = jax.random.normal(k2, (D, N, P), dtype=jnp.float32) * (1.0 / np.sqrt(D))
        W = jax.random.normal(k3, (N, D, D), dtype=jnp.float32) * (1.0 / np.sqrt(D))
        b = jax.random.normal(k4, (N, D), dtype=jnp.float32) * 0.01
        return {'x': x, 'phi': phi, 'W': W, 'b': b}
    _L1_ffn_in = _L1_ffn_setup()
    _d = {'L0_attn_x': _L0_attn_in['x'], 'L0_attn_in_proj_w': _L0_attn_in['in_proj_w'], 'L0_attn_conv_w': _L0_attn_in['conv_w'], 'L0_attn_conv_b': _L0_attn_in['conv_b'], 'L0_attn_dt_bias': _L0_attn_in['dt_bias'], 'L0_attn_A_log': _L0_attn_in['A_log'], 'L0_attn_D': _L0_attn_in['D'], 'L0_attn_norm_w': _L0_attn_in['norm_w'], 'L0_attn_out_proj_w': _L0_attn_in['out_proj_w'], 'L0_attn_ln_w': _L0_attn_in['ln_w'], 'L0_attn_ln_b': _L0_attn_in['ln_b'], 'L0_ffn_w_q': _L0_ffn_in['w_q'], 'L0_ffn_w_k': _L0_ffn_in['w_k'], 'L0_ffn_w_gate': _L0_ffn_in['w_gate'], 'L0_ffn_value_experts': _L0_ffn_in['value_experts'], 'L0_ffn_output_experts': _L0_ffn_in['output_experts'], 'L1_attn_Wq': _L1_attn_in['Wq'], 'L1_attn_bq': _L1_attn_in['bq'], 'L1_attn_Wk': _L1_attn_in['Wk'], 'L1_attn_bk': _L1_attn_in['bk'], 'L1_attn_Wv': _L1_attn_in['Wv'], 'L1_attn_bv': _L1_attn_in['bv'], 'L1_attn_gamma': _L1_attn_in['gamma'], 'L1_attn_beta': _L1_attn_in['beta'], 'L1_ffn_phi': _L1_ffn_in['phi'], 'L1_ffn_W': _L1_ffn_in['W'], 'L1_ffn_b': _L1_ffn_in['b']}
    _x0 = _d['L0_attn_x']
    _d['L0_attn_x'] = jax.random.normal(jax.random.fold_in(jax.random.key(seed), 1), (16, 256, 128), dtype=_x0.dtype)
    del _x0
    return _d

def reference(L0_attn_x, L0_attn_in_proj_w, L0_attn_conv_w, L0_attn_conv_b, L0_attn_dt_bias, L0_attn_A_log, L0_attn_D, L0_attn_norm_w, L0_attn_out_proj_w, L0_attn_ln_w, L0_attn_ln_b, L0_ffn_w_q, L0_ffn_w_k, L0_ffn_w_gate, L0_ffn_value_experts, L0_ffn_output_experts, L1_attn_Wq, L1_attn_bq, L1_attn_Wk, L1_attn_bk, L1_attn_Wv, L1_attn_bv, L1_attn_gamma, L1_attn_beta, L1_ffn_phi, L1_ffn_W, L1_ffn_b):

    def _L0_attn_ref(x, in_proj_w, conv_w, conv_b, dt_bias, A_log, D, norm_w, out_proj_w, ln_w, ln_b):
        import jax, jax.numpy as jnp
        import numpy as np
        from jax import lax
        D_MODEL = 128
        D_STATE = 128
        D_CONV = 4
        EXPAND = 2
        HEADDIM = 64
        D_INNER = EXPAND * D_MODEL
        NHEADS = D_INNER // HEADDIM
        CONV_DIM = D_INNER + 2 * D_STATE
        D_IN_PROJ = 2 * D_INNER + 2 * D_STATE + NHEADS
        B_SZ, L_SEQ = (4, 256)
        EPS = 1e-05

        def _mamba_block(x, in_proj_w, conv_w, conv_b, dt_bias, A_log, D, norm_w, out_proj_w, ln_w, ln_b):
            b, l, _ = x.shape
            zxbcdt = jnp.einsum('bld,ed->ble', x, in_proj_w)
            z = zxbcdt[..., :D_INNER]
            xBC = zxbcdt[..., D_INNER:D_INNER + CONV_DIM]
            dt = jax.nn.softplus(zxbcdt[..., D_INNER + CONV_DIM:] + dt_bias)
            xBC_t = xBC.transpose(0, 2, 1)
            conv = lax.conv_general_dilated(xBC_t, conv_w[:, None, :], (1,), [(D_CONV - 1, 0)], feature_group_count=CONV_DIM, dimension_numbers=('NCW', 'OIW', 'NCW'))
            xBC = jax.nn.silu(conv + conv_b[:, None]).transpose(0, 2, 1)
            x_ssm = xBC[..., :D_INNER].reshape(b, l, NHEADS, HEADDIM)
            Bm = xBC[..., D_INNER:D_INNER + D_STATE]
            Cm = xBC[..., D_INNER + D_STATE:]
            A = -jnp.exp(A_log)
            dA = jnp.exp(dt * A)

            def step(h, inp):
                dA_t, x_t, B_t, C_t, dt_t = inp
                dBx = dt_t[:, :, None, None] * x_t[..., None] * B_t[:, None, None, :]
                h = h * dA_t[:, :, None, None] + dBx
                y = jnp.einsum('bhpn,bn->bhp', h, C_t)
                return (h, y)
            h0 = jnp.zeros((b, NHEADS, HEADDIM, D_STATE), dtype=x.dtype)
            inputs = (dA.transpose(1, 0, 2), x_ssm.transpose(1, 0, 2, 3), Bm.transpose(1, 0, 2), Cm.transpose(1, 0, 2), dt.transpose(1, 0, 2))
            _, ys = lax.scan(step, h0, inputs)
            y = ys.transpose(1, 0, 2, 3) + D[None, None, :, None] * x_ssm
            y = y.reshape(b, l, D_INNER)
            y = y * jax.nn.silu(z)
            y = y * lax.rsqrt(jnp.mean(y * y, axis=-1, keepdims=True) + EPS) * norm_w
            y = jnp.einsum('bld,ed->ble', y, out_proj_w) + x
            mu = jnp.mean(y, axis=-1, keepdims=True)
            var = jnp.mean((y - mu) ** 2, axis=-1, keepdims=True)
            return (y - mu) * lax.rsqrt(var + EPS) * ln_w + ln_b
        return _mamba_block(x, in_proj_w, conv_w, conv_b, dt_bias, A_log, D, norm_w, out_proj_w, ln_w, ln_b)

    def _L0_ffn_ref(x, w_q, w_k, w_gate, value_experts, output_experts):
        import jax, jax.numpy as jnp
        import numpy as np
        B, N, DIM = (2, 256, 128)
        HEADS, DIM_HEAD, EXPERTS = (8, 64, 8)
        SCALE = DIM_HEAD ** (-0.5)
        b, n, _ = x.shape
        q = (x @ w_q).reshape(b, n, HEADS, DIM_HEAD).transpose(0, 2, 1, 3)
        k = (x @ w_k).reshape(b, n, HEADS, DIM_HEAD).transpose(0, 2, 1, 3)
        gates = jax.nn.sigmoid((x @ w_gate).reshape(b, n, HEADS, EXPERTS).transpose(0, 2, 1, 3))
        sel = jnp.argmax(gates, axis=-1)
        gm = jax.nn.one_hot(sel, EXPERTS, dtype=x.dtype) * gates
        values = jnp.einsum('bhne,ehdk,bnd->bhnk', gm, value_experts, x)
        sim = jnp.einsum('bhid,bhjd->bhij', q * SCALE, k)
        causal_mask = jnp.triu(jnp.ones((n, n), dtype=bool), 1)
        sim = jnp.where(causal_mask, jnp.finfo(sim.dtype).min, sim)
        attn = jax.nn.softmax(sim, axis=-1)
        out = jnp.einsum('bhij,bhjk->bhik', attn, values)
        out = jnp.einsum('bhne,ehkd,bhnk->bhnd', gm, output_experts, out)
        return out.sum(axis=1)

    def _L1_attn_ref(x, Wq, bq, Wk, bk, Wv, bv, gamma, beta):
        import jax, jax.numpy as jnp
        import numpy as np
        HEADS = 16
        THETA = 10000.0

        def _rope(x):
            b, n, d = x.shape
            half = d // 2
            inv_freq = 1.0 / THETA ** (jnp.arange(0, d, 2, dtype=jnp.float32) / d)
            ang = jnp.arange(n, dtype=jnp.float32)[:, None] * inv_freq
            cos, sin = (jnp.cos(ang), jnp.sin(ang))
            xp = x.reshape(b, n, half, 2)
            x1, x2 = (xp[..., 0], xp[..., 1])
            out = jnp.stack([x1 * cos - x2 * sin, x2 * cos + x1 * sin], axis=-1)
            return out.reshape(b, n, d)
        b, n, c = x.shape
        h = HEADS
        d = c // h
        gelu = lambda t: jax.nn.gelu(t, approximate=False)
        q = gelu(x @ Wq.T + bq) + 0.21
        k = gelu(x @ Wk.T + bk) + 0.21
        v = x @ Wv.T + bv
        q_r = _rope(q)
        k_r = _rope(k)
        split = lambda t: t.reshape(b, n, h, d).transpose(0, 2, 1, 3)
        qh, kh, vh, qrh, krh = (split(q), split(k), split(v), split(q_r), split(k_r))
        z = 1.0 / (jnp.einsum('bhnd,bhd->bhn', qh, kh.mean(axis=2)) + 1e-06)
        scale = n ** (-0.5)
        kv = jnp.einsum('bhnd,bhne->bhde', krh * scale, vh * scale)
        out = jnp.einsum('bhnd,bhde->bhne', qrh, kv) * z[..., None]
        out = out.transpose(0, 2, 1, 3).reshape(b, n, c)
        res = out + x
        mu = res.mean(-1, keepdims=True)
        var = res.var(-1, keepdims=True)
        return (res - mu) / jnp.sqrt(var + 1e-12) * gamma + beta

    def _L1_ffn_ref(x, phi, W, b):
        import jax, jax.numpy as jnp
        import numpy as np
        B, M, D = (4, 256, 128)
        N, P = (64, 32)
        logits = jnp.einsum('bmd,dnp->bmnp', x, phi)
        dispatch = jax.nn.softmax(logits, axis=0)
        bsz, m, n, p = logits.shape
        combine = jax.nn.softmax(logits.reshape(bsz, m, n * p), axis=-1).reshape(bsz, m, n, p)
        slots = jnp.einsum('bmd,bmnp->bnpd', x, dispatch)
        y = jnp.einsum('bnpd,nde->bnpe', slots, W) + b[None, :, None, :]
        out = jnp.einsum('bnpd,bmnp->bmd', y, combine)
        return out
    x = L0_attn_x
    x = _layernorm(x + _L0_attn_ref(x, L0_attn_in_proj_w, L0_attn_conv_w, L0_attn_conv_b, L0_attn_dt_bias, L0_attn_A_log, L0_attn_D, L0_attn_norm_w, L0_attn_out_proj_w, L0_attn_ln_w, L0_attn_ln_b), axis=-1)
    x = _layernorm(x + _L0_ffn_ref(x, L0_ffn_w_q, L0_ffn_w_k, L0_ffn_w_gate, L0_ffn_value_experts, L0_ffn_output_experts), axis=-1)
    x = _layernorm(x + _L1_attn_ref(x, L1_attn_Wq, L1_attn_bq, L1_attn_Wk, L1_attn_bk, L1_attn_Wv, L1_attn_bv, L1_attn_gamma, L1_attn_beta), axis=-1)
    x = _layernorm(x + _L1_ffn_ref(x, L1_ffn_phi, L1_ffn_W, L1_ffn_b), axis=-1)
    return x

_drawn_inputs = setup_inputs


def setup_inputs(seed=0):
    import zlib

    import numpy as np

    out = dict(_drawn_inputs(seed))
    spreads = {'L0_attn_norm_w': (1.0, 0.584),
     'L0_attn_ln_w': (1.0, 0.2),
     'L0_attn_ln_b': (0.0, 0.1),
     'L1_attn_gamma': (1.0, 0.2),
     'L1_attn_beta': (0.0, 0.1)}
    factors = {'L0_attn_dt_bias': 8.0,
     'L0_attn_A_log': 8.0,
     'L0_attn_D': 4.747,
     'L0_ffn_w_q': 8.0,
     'L0_ffn_w_k': 8.0,
     'L0_ffn_w_gate': 8.0,
     'L0_ffn_value_experts': 8.0,
     'L0_ffn_output_experts': 8.0,
     'L1_attn_bq': 170.902,
     'L1_attn_bk': 195.035,
     'L1_attn_bv': 6.645,
     'L1_ffn_b': 43.814,
     'L1_attn_Wq': 2.865}
    for name, (base, spread) in spreads.items():
        noise = np.random.default_rng([zlib.crc32(name.encode()), seed]).standard_normal(out[name].shape)
        drawn = base * np.exp(spread * noise) if base else spread * noise
        out[name] = jnp.asarray(drawn.astype(out[name].dtype))
    for name, factor in factors.items():
        out[name] = (out[name] * factor).astype(out[name].dtype)
    return out
```

```python
from contextlib import ExitStack

import concourse.bass as bass
from concourse import mybir

F32 = mybir.dt.float32
F32R = mybir.dt.float32r
BF16 = mybir.dt.bfloat16
I32 = mybir.dt.int32
ALU = mybir.AluOpType
ACT = mybir.ActivationFunctionType
AX = mybir.AxisListType

NB, L, D = 16, 256, 128
P = 128
C = L // P
NH, HD = 4, 64
DI = NH * HD
NCH = (DI + 2 * D) // P
TAPS = 4
EPS = 1e-5
HB, DH, NE = 8, 64, 8
HP = HB // 2
SCALE = DH ** -0.5
NEG = -3.0e38
HL = 16
WL = D // HL
SHIFT = 0.21
NX, NS = 64, 32
S = NX * NS
SB = S // P
XB = P // NS
TT = NB * C

RSQRT_SEED = float(0x5F3759DF)
RSQRT_STEPS = 3
RSQRT_OPS = 3 + 4 * RSQRT_STEPS
LOG1P_TERMS = 7


def wait(eng, sem, value):
    if not isinstance(value, int) or value > 0:
        eng.wait_ge(sem, value)


def newton(pool, wait_apart, done, k, source, var, scale, eps, v, h, y, t):
    wait_apart(pool, source)
    pool.tensor_scalar(v[:], var, scale, eps, ALU.mult, ALU.add).then_inc(done, 1)
    wait_apart(pool, (done, k + 1))
    pool.tensor_scalar(h[:], v[:], -0.5, None, ALU.mult).then_inc(done, 1)
    pool.tensor_scalar(y[:].bitcast(I32), v[:].bitcast(I32), -0.5, RSQRT_SEED,
                       ALU.mult, ALU.add).then_inc(done, 1)
    for s in range(RSQRT_STEPS):
        wait(pool, done, k + 3 + 4 * s)
        pool.tensor_tensor(t[:], y[:], y[:], ALU.mult).then_inc(done, 1)
        wait(pool, done, k + 4 + 4 * s)
        pool.tensor_tensor(t[:], t[:], h[:], ALU.mult).then_inc(done, 1)
        wait_apart(pool, (done, k + 5 + 4 * s))
        pool.tensor_scalar(t[:], t[:], 1.5, None, ALU.add).then_inc(done, 1)
        wait(pool, done, k + 6 + 4 * s)
        pool.tensor_tensor(y[:], y[:], t[:], ALU.mult).then_inc(done, 1)


def build(nc, x, xT, in_wT, conv_w, conv_b, dt_bias, A_log, Dh, norm_w, out_wT, ln_w, ln_b,
          w_q, w_k, w_gate, v_exp, o_exp, WqkvT, bq, bk, bv, gamma, beta, phi, W, b_exp,
          ident, causal, neg_blocks, strict_low, upper, head_of, rot, cosT, sinT, w8,
          out):
    x3_dram = nc.dram_tensor("x3_tok", (NB * L, D), F32, kind="Internal").ap()
    x3T_dram = nc.dram_tensor("x3_T", (D, NB * L), F32, kind="Internal").ap()
    ctx = ExitStack()
    with ctx:
        x3_stored = ctx.enter_context(nc.semaphore("x3_stored"))
        token_blocks(nc, ctx, x, xT, in_wT, conv_w, conv_b, dt_bias, A_log, Dh, norm_w, out_wT, ln_w, ln_b,
                     w_q, w_k, w_gate, v_exp, o_exp, WqkvT, bq, bk, bv, gamma, beta,
                     ident, causal, neg_blocks, strict_low, upper, head_of, rot, cosT, sinT, w8,
                     x3_dram, x3T_dram, x3_stored)
        soft_experts(nc, ctx, x3_dram, x3T_dram, x3_stored, phi, W, b_exp, ident, out)


def row(ap, n):
    return ap.rearrange("(a n) -> a n", a=1).to_broadcast([P, n])


def token_blocks(nc, kept, x, xT, in_wT, conv_w, conv_b, dt_bias, A_log, Dh, norm_w, out_wT, ln_w, ln_b,
                 w_q, w_k, w_gate, v_exp, o_exp, WqkvT, bq, bk, bv, gamma, beta,
                 ident, causal, neg_blocks, strict_low, upper, head_of, rot, cosT, sinT, w8,
                 x3_dram, x3T_dram, x3_stored):
    with ExitStack() as ctx:
        def sb(name, shape, dt=F32):
            return ctx.enter_context(nc.sbuf_tensor(name, [P] + shape, dt))

        def sem(name):
            return kept.enter_context(nc.semaphore(name))

        id_f = sb("id_f", [P])
        id_b = sb("id_b", [P], BF16)
        causal_s = sb("causal_s", [P])
        negb_f = sb("negb_f", [3, P])
        negb = sb("negb", [3, P], BF16)
        low_s = sb("low_s", [P])
        upp_s = sb("upp_s", [P])
        hof = sb("hof", [P])
        hof_n = sb("hof_n", [P])
        h16 = sb("h16", [HL])
        rot_s = sb("rot_s", [P])
        cos_s = sb("cos_s", [L])
        sin_s = sb("sin_s", [L])
        w8_s = sb("w8_s", [NE])
        in_w = sb("in_w", [2 * DI + 2 * D + NH])
        out_w0 = sb("out_w0", [2, D])
        out_w = sb("out_w", [2, D])
        cw0 = sb("cw0", [NCH, TAPS])
        cb0 = sb("cb0", [NCH])
        cw = sb("cw", [NCH, TAPS])
        cb = sb("cb", [NCH])
        nw = sb("nw", [2])
        dtb = sb("dtb", [NH])
        alog = sb("alog", [NH])
        d_h = sb("d_h", [NH])
        lnw = sb("lnw", [D])
        lnb = sb("lnb", [D])
        wq_f = sb("wq_f", [HB * DH])
        wk_f = sb("wk_f", [HB * DH])
        wg_f = sb("wg_f", [HB * NE])
        wqH = sb("wqH", [HB * DH], F32R)
        wqL = sb("wqL", [HB * DH], F32R)
        wkH = sb("wkH", [HB * DH], F32R)
        wkL = sb("wkL", [HB * DH], F32R)
        wgH = sb("wgH", [HB * NE], F32R)
        wgL = sb("wgL", [HB * NE], F32R)
        ve_f = sb("ve_f", [NE * HB * DH])
        veH = sb("veH", [NE, HB * DH], F32R)
        veL = sb("veL", [NE, HB * DH], F32R)
        oe = sb("oe", [HP, NE, D])
        x_all = oe[:, :, :, :].rearrange("p a e d -> p (a e d)")
        idfold = sb("idfold", [HB * NE])
        pick = sb("pick", [HP, NE, 2, DH], BF16)
        wl = sb("wl", [3 * D])
        bq_s = sb("bq_s", [1])
        bk_s = sb("bk_s", [1])
        bv_s = sb("bv_s", [D])
        gam = sb("gam", [D])
        bet = sb("bet", [D])

        sv = sb("sv", [TT, NH])
        sa = sb("sa", [TT, NH])
        su = sb("su", [TT, NH])
        sd = sb("sd", [TT, NH])
        s2 = sb("s2", [TT, NH])
        sp = sb("sp", [TT, NH])
        ea = sb("ea", [NH])
        dt_all = sb("dt_all", [TT, NH])
        a_all = sb("a_all", [TT, NH])

        xt_in = sb("xt_in", [2, L])
        x_in = sb("x_in", [2, C, D])
        dt_b = sb("dt_b", [C, NH])
        a_b = sb("a_b", [C, NH])
        cin = sb("cin", [NCH, L + TAPS - 1])
        cacc = sb("cacc", [NCH, L])
        xbc = sb("xbc", [NCH, L])
        xd = sb("xd", [C, NH, HD])
        xD = sb("xD", [C, NH, HD])
        btok = sb("btok", [P])
        gm = sb("gm", [C, P])
        am = sb("am", [C, NH, P])
        lx = sb("lx", [C, NH, P])
        mx = sb("mx", [C, NH, P])
        ep = sb("ep", [NH])
        xst = sb("xst", [NH, HD])
        st = sb("st", [DI])
        inter = sb("inter", [NH, HD])
        tz = sb("tz", [C, DI])
        sz = sb("sz", [C, DI])
        ya = sb("ya", [C, DI])
        yg = sb("yg", [C, DI])
        sq = sb("sq", [DI])
        ssq = sb("ssq", [C])
        yT = sb("yT", [2, L])
        ra = sb("ra", [C, D])
        na = sb("na", [C, D])
        xb = sb("xb", [C, D])
        x1 = sb("x1", [2, C, D])
        x1H = sb("x1H", [2, L], F32R)
        x1L = sb("x1L", [2, L], F32R)

        eg = sb("eg", [C, HB, NE])
        g = sb("g", [C, HB, NE])
        gx = sb("gx", [C, HB])
        geq = sb("geq", [C, HB, NE])
        g2 = sb("g2", [C, HB])
        oh = sb("oh", [C, HB, NE])
        ohT = sb("ohT", [P], BF16)
        qk = sb("qk", [HP, 2, L])
        vals = sb("vals", [C, HB, DH])
        r3 = sb("r3", [2, 3])
        n3 = sb("n3", [2, 3])
        pr = ve_f[:, 2048:2816].rearrange("p (s a n) -> p s a n", s=2, a=3)
        pt = ve_f[:, 2816:3584].rearrange("p (s a n) -> p s a n", s=2, a=3)
        rs = sb("rs", [C, HB])
        rg = sb("rg", [C, HB])
        on = sb("on", [C, HB * DH])
        oT = sb("oT", [HP, L])
        mo = ve_f[:, 0:2 * HP * L].rearrange("p (s a n) -> p s a n", s=2, a=HP)
        oa = sb("oa", [L])
        rb = sb("rb", [C, D])
        x2 = sb("x2", [2, C, D])
        x2T = sb("x2T", [2, L])

        gl = wk_f[:, :].rearrange("p (a n) -> p a n", a=2)
        ks = sb("ks", [1])
        km = sb("km", [1])
        kmh = sb("kmh", [HL])
        ql = sb("ql", [2, L])
        t1 = ve_f[:, 3584:4096].rearrange("p (a n) -> p a n", a=2)
        t2 = wq_f[:, :].rearrange("p (a n) -> p a n", a=2)
        qr = sb("qr", [2, L])
        vl = sb("vl", [C, D])
        kr = sb("kr", [C, D])
        kv = sb("kv", [D])
        zd = sb("zd", [C, HL])
        zr = sb("zr", [C, HL])
        rc = sb("rc", [C, HL, WL])
        rc2 = sb("rc2", [C, D])
        ncn = sb("ncn", [C, D])
        n2 = sb("n2", [C, D])
        xc = sb("xc", [C, D])
        x3 = sb("x3", [C, D])
        x3T = sb("x3T", [L])

        bank = [ctx.enter_context(nc.psum_tensor(f"bk{i}", [P, C, 512], F32)) for i in (0, 2)]
        ps_v = bank
        ps_o = ctx.enter_context(nc.psum_tensor("ps_o", [P, C, 512], F32))
        ps_a = ctx.enter_context(nc.psum_tensor("ps_a", [P, 512], F32))
        ps_c = ctx.enter_context(nc.psum_tensor("ps_c", [P, 512], F32))

        ready = sem("ready")
        x_all_in = sem("x_all_in")
        oe_in = sem("oe_in")
        prep = sem("prep")
        prep_act = sem("prep_act")
        dt_ps = sem("dt_ps")
        soft = sem("soft")
        soft_act = sem("soft_act")
        x_in_sem = [sem(f"x_in_sem{u}") for u in range(2)]

        names = """a_step a_xbc_ps a_cin a_conv a_th a_xbc a_z_ps a_tz a_sz a_am a_seg_ps a_lx a_mx a_xt_ps a_xd
            a_bg_ps a_btok a_ep a_gm a_xst a_st_ps a_st a_int_ps a_int a_y_ps a_y a_yg a_sq a_yt_ps a_yt
            a_op_ps a_r a_xb a_n a_x1t_ps a_x1h a_x1l a_x1
            b_g_ps b_eg b_gate b_oht_ps b_oht b_qk_ps b_qk b_v_ps b_v0 b_v b_vg b_s_ps b_max b_p b_pt_ps b_pt
            b_pv b_rg b_on b_ot_ps b_ot b_m_ps b_mo b_oe b_oa b_oat_ps b_r b_x2t_ps b_x2t
            c_qk_ps c_g c_km c_q c_v_ps c_v c_rot_ps c_qr c_krt_ps c_kr c_kv_ps c_kv c_out_ps c_z c_res c_n
            c_x3t_ps c_x3t c_x3""".split()
        q = {n: sem(n) for n in names}
        norms = {n: {k: sem(f"{n}_{k}") for k in ("moments", "rstd", "rows")}
                 for n in ("rms", "ln1", "ln2", "lnB", "lnC", "lnD")}
        nbuf = {n: (sb(f"{n}_st", [C, 6]), sb(f"{n}_mv", [C, 2]), sb(f"{n}_v", [C]), sb(f"{n}_h", [C]),
                    sb(f"{n}_y", [C]), sb(f"{n}_t", [C])) for n in norms}

        CONSTS = [(id_f, ident), (causal_s, causal), (negb_f, neg_blocks), (low_s, strict_low), (upp_s, upper),
                  (hof, head_of), (rot_s, rot), (cos_s, cosT), (sin_s, sinT), (w8_s, w8), (in_w, in_wT),
                  (out_w0, out_wT), (cw0, conv_w), (cb0, conv_b), (nw, norm_w),
                  (wq_f, w_q), (wk_f, w_k), (wg_f, w_gate), (ve_f, v_exp), (wl, WqkvT)]
        ROWS = [(dtb, dt_bias, NH), (alog, A_log, NH), (d_h, Dh, NH), (lnw, ln_w, D), (lnb, ln_b, D),
                (bv_s, bv, D), (gam, gamma, D), (bet, beta, D)]
        COLS = [(bq_s, bq), (bk_s, bk)]
        READY = 16 * (len(CONSTS) + len(ROWS) + len(COLS))
        PREP = 15
        PREP_ACT = 5

        def wait_apart(eng, *waits):
            for _, v in waits:
                eng.compute_val(v)
            eng.wait_ge(ready, READY)
            for s, v in waits:
                wait(eng, s, v)

        def var_of(n):
            return nbuf[n][1][:, :, 1] if n != "rms" else ssq[:]

        def rstd_of(n):
            return nbuf[n][4]

        def stats(dve, n, src, b):
            stt, mv = nbuf[n][0], nbuf[n][1]
            for c in range(C):
                dve.bn_stats(stt[:, c, :], src[:, c, :]).then_inc(norms[n]["moments"], 1)
            for c in range(C):
                wait_apart(dve, (norms[n]["moments"], 2 * C * b + c + 1))
                dve.bn_aggr(mv[:, c, :], stt[:, c, :]).then_inc(norms[n]["moments"], 1)

        def rsqrt(pool, n, b, scale, eps, source, per):
            _, _, v, h, y, t = nbuf[n]
            newton(pool, wait_apart, norms[n]["rstd"], RSQRT_OPS * b, (source, per * b + per), var_of(n), scale, eps,
                   v, h, y, t)

        def scale_rows(dve, n, src, dst, b):
            wait(dve, norms[n]["rstd"], RSQRT_OPS * (b + 1))
            for c in range(C):
                dve.tensor_scalar(dst[:, c, :], src[:, c, :], nbuf[n][1][:, c, 0:1], rstd_of(n)[:, c:c + 1],
                                  ALU.subtract, ALU.mult).then_inc(norms[n]["rows"], 1)

        block = ctx.enter_context(nc.Block())

        @block.sync
        def _(sp):
            sp.dma_start(x_all, xT).then_inc(x_all_in, 16)
            for dst, src in CONSTS:
                sp.dma_start(dst[:], src).then_inc(ready, 16)
            for dst, src, n in ROWS:
                sp.dma_start(dst[:], row(src, n)).then_inc(ready, 16)
            for dst, src in COLS:
                sp.dma_start(dst[:], src.rearrange("(p a) -> p a", a=1)).then_inc(ready, 16)
            sp.wait_ge(dt_ps, 1)
            sp.dma_start(oe[:], o_exp).then_inc(oe_in, 16)

            def load(b, u):
                for v in (b - 1, C * (b - 1), b * L):
                    sp.compute_val(v)
                sp.wait_ge(x_all_in, 16)
                wait(sp, q["a_xb"], b - 1)
                wait(sp, q["a_z_ps"], b - 1)
                wait(sp, q["a_r"], C * (b - 1))
                sp.dma_start(xt_in[:, u, :], xT[:, bass.ds(b * L, L)]).then_inc(x_in_sem[u], 16)
                sp.dma_start(x_in[:, u, :, :], x[bass.ds(b * L, L), :].rearrange("(c p) d -> p c d", p=P)
                             ).then_inc(x_in_sem[u], 16)

            def store(b):
                for v in (b + 1, b * L):
                    sp.compute_val(v)
                sp.wait_ge(x_all_in, 16)
                wait(sp, q["c_x3"], b + 1)
                sp.dma_start(x3_dram[bass.ds(b * L, L), :].rearrange("(c p) d -> p c d", p=P), x3[:]
                             ).then_inc(x3_stored, 16)
                sp.wait_ge(x_all_in, 16)
                wait(sp, q["c_x3t"], b + 1)
                sp.dma_start(x3T_dram[:, bass.ds(b * L, L)], x3T[:]).then_inc(x3_stored, 16)

            load(0, 0)
            load(1, 1)
            with sp.Fori(1, NB // 2) as pair:
                for u in range(2):
                    load(2 * pair + u, u)
                    store(2 * pair + u - 2)
            store(NB - 2)
            store(NB - 1)
            sp.wait_ge(x3_stored, 32 * NB)

        @block.tensor
        def _(pe):
            def mm3(ps, lh, ll, rh, rl, first=True, last=True):
                pe.matmul(ps, lh, rh, start=first, stop=False, skip_group_check=True)
                pe.matmul(ps, lh, rl, start=False, stop=False, skip_group_check=True)
                return pe.matmul(ps, ll, rh, start=False, stop=last, skip_group_check=True)

            def a_xbc(b, u, r, half):
                if half == 0:
                    wait(pe, x_in_sem[u], 32 * (r + 1))
                    wait(pe, q["a_x1h"], b)
                    wait(pe, q["a_x1l"], b)
                else:
                    wait(pe, q["a_cin"], 2 * b + 1)
                for j in range(2):
                    ch = DI + (2 * half + j) * P
                    last = pe.matmul(ps_a[:, j * L:(j + 1) * L], in_w[:, ch:ch + P], xt_in[:, u, :],
                                     start=True, stop=True, skip_group_check=True)
                last.then_inc(q["a_xbc_ps"], 1)

            def a_z(b, u):
                wait(pe, q["a_cin"], 2 * b + 2)
                for c in range(C):
                    last = pe.matmul(ps_a[:, c * DI:(c + 1) * DI], xt_in[:, u, c * P:(c + 1) * P], in_w[:, 0:DI],
                                     start=True, stop=True, skip_group_check=True)
                last.then_inc(q["a_z_ps"], 1)

            def a_seg(b, c):
                if c == 0:
                    wait(pe, q["a_sz"], b + 1)
                else:
                    wait(pe, q["a_lx"], C * b + 1)
                wait(pe, q["a_am"], C * b + c + 1)
                pe.matmul(ps_a[:, :], low_s[:], am[:, c, :, :].rearrange("p h t -> p (h t)"),
                          start=True, stop=True, skip_group_check=True).then_inc(q["a_seg_ps"], 1)

            def a_xt(b):
                wait(pe, q["a_xbc"], b + 1)
                wait(pe, q["a_lx"], C * b + 2)
                for c in range(C):
                    for j in range(2):
                        last = pe.transpose(ps_a[:, c * DI + j * P:c * DI + (j + 1) * P],
                                            xbc[:, j, c * P:(c + 1) * P], id_f[:])
                last.then_inc(q["a_xt_ps"], 1)

            def a_bg(b):
                wait(pe, q["a_xd"], 2 * b + 2)
                pe.transpose(ps_a[:, 0:P], xbc[:, 2, 0:P], id_f[:])
                for c in range(C):
                    pe.matmul(ps_a[:, (c + 1) * P:(c + 2) * P], xbc[:, 2, c * P:(c + 1) * P],
                              xbc[:, 3, c * P:(c + 1) * P], start=True, stop=True, skip_group_check=True)
                pe.matmul(ps_a[:, 3 * P:3 * P + NH], upp_s[:], a_b[:, 1, :], start=True, stop=True,
                          skip_group_check=True).then_inc(q["a_bg_ps"], 1)

            def a_state(b):
                wait(pe, q["a_gm"], b + 1)
                wait(pe, q["a_ep"], b + 1)
                wait(pe, q["a_btok"], b + 1)
                wait(pe, q["a_xst"], b + 1)
                pe.matmul(ps_a[:, 0:DI], btok[:], xst[:].rearrange("p h d -> p (h d)"),
                          start=True, stop=True, skip_group_check=True).then_inc(q["a_st_ps"], 1)

            def a_inter(b):
                wait(pe, q["a_st"], b + 1)
                pe.matmul(ps_a[:, DI:2 * DI], xbc[:, 3, P:2 * P], st[:],
                          start=True, stop=True, skip_group_check=True).then_inc(q["a_int_ps"], 1)

            def a_y(b):
                wait(pe, q["a_mx"], C * b + C)
                wait(pe, q["a_int"], 2 * b + 1)
                for c in range(C):
                    for h in range(NH):
                        last = pe.matmul(ps_a[:, c * DI + h * HD:c * DI + (h + 1) * HD], mx[:, c, h, :],
                                         xd[:, c, h, :], start=True, stop=True, skip_group_check=True)
                last.then_inc(q["a_y_ps"], 1)

            def a_yt(b):
                wait(pe, q["a_yg"], b + 1)
                for j in range(2):
                    for c in range(C):
                        last = pe.transpose(ps_a[:, j * L + c * P:j * L + (c + 1) * P],
                                            yg[:, c, j * P:(j + 1) * P], id_f[:])
                last.then_inc(q["a_yt_ps"], 1)

            def a_op(b):
                wait(pe, q["a_yt"], b + 1)
                for c in range(C):
                    for j in range(2):
                        last = pe.matmul(ps_a[:, c * D:(c + 1) * D], yT[:, j, c * P:(c + 1) * P], out_w[:, j, :],
                                         start=(j == 0), stop=(j == 1), skip_group_check=True)
                last.then_inc(q["a_op_ps"], 1)

            def a_x1t(b, u):
                wait(pe, q["a_x1"], b + 1)
                for c in range(C):
                    last = pe.transpose(ps_a[:, c * P:(c + 1) * P], x1[:, u, c, :], id_f[:])
                last.then_inc(q["a_x1t_ps"], 1)

            def b_gates(b, u):
                wait(pe, q["a_x1h"], b + 1)
                wait(pe, q["a_x1l"], b + 1)
                wait(pe, q["b_x2t"], b)
                for c in range(C):
                    cols = slice(c * P, (c + 1) * P)
                    last = mm3(ps_o[:, 1, c * 64:c * 64 + 64], x1H[:, u, cols], x1L[:, u, cols], wgH[:], wgL[:])
                last.then_inc(q["b_g_ps"], 1)

            def b_qk(b, u, hp):
                wait(pe, q["b_mo"], NE * b)
                bankq = ps_v[hp // 2][:, hp % 2, :]
                pe_cols = slice(hp * P, (hp + 1) * P)
                mm3(bankq[:, 0:L], wqH[:, pe_cols], wqL[:, pe_cols], x1H[:, u, :], x1L[:, u, :])
                mm3(bankq[:, L:2 * L], wkH[:, pe_cols], wkL[:, pe_cols], x1H[:, u, :], x1L[:, u, :]
                    ).then_inc(q["b_qk_ps"], 1)

            def b_values(b, u, e):
                if e < 2:
                    wait(pe, q["b_qk"], HP * b + 2 * e + 2)
                elif e == 2:
                    wait(pe, q["b_v0"], b + 1)
                else:
                    wait(pe, q["b_v"], (NE - 1) * b + e - 2)
                for c in range(C):
                    cols = slice(c * P, (c + 1) * P)
                    last = mm3(ps_v[e % 2][:, c, :], x1H[:, u, cols], x1L[:, u, cols], veH[:, e, :], veL[:, e, :])
                last.then_inc(q["b_v_ps"], 1)

            def b_oht(b):
                wait(pe, q["b_gate"], 7 * b + 7)
                pe.transpose(ps_o[:, 1, P:2 * P], oh[:].rearrange("p c h e -> p (c h e)"), id_f[:]
                             ).then_inc(q["b_oht_ps"], 1)

            def b_scores(b, h):
                if h < 2:
                    wait(pe, q["b_v"], (NE - 1) * (b + 1))
                else:
                    wait(pe, q["b_p"], 2 * HB * b + 2 * (h - 1))
                sc = ps_v[0][:, h % 2, :]
                half = slice(64 * (h % 2), 64 * (h % 2) + 64)
                pe.matmul(sc[:, 0:3 * P], id_b[:], negb[:].rearrange("p a b -> p (a b)"),
                          start=True, stop=False, skip_group_check=True)
                pe.matmul(sc[:, 0:P], qk[half, h // 2, 0, 0:P], qk[half, h // 2, 1, 0:P],
                          start=False, stop=False, skip_group_check=True)
                pe.matmul(sc[:, P:3 * P], qk[half, h // 2, 0, P:L], qk[half, h // 2, 1, :],
                          start=False, stop=True, skip_group_check=True).then_inc(q["b_s_ps"], 1)

            def b_turn(b, h):
                wait(pe, q["b_p"], 2 * HB * b + 2 * h + 2)
                if h >= 2:
                    wait(pe, q["b_pt"], HB * b + h - 1)
                for k in range(3):
                    last = pe.transpose(ps_v[1][:, h % 2, k * P:(k + 1) * P], pr[:, h % 2, k, :], id_f[:])
                last.then_inc(q["b_pt_ps"], 1)

            def b_pv(b, h):
                wait(pe, q["b_pt"], HB * b + h + 1)
                if h == 0:
                    wait(pe, q["b_vg"], C * (b + 1))
                    wait(pe, q["b_oht"], b + 1)
                cols = slice(h * DH, (h + 1) * DH)
                pe.matmul(ps_o[:, 0, cols], pt[:, h % 2, 0, :], vals[:, 0, h, :],
                          start=True, stop=True, skip_group_check=True)
                pe.matmul(ps_o[:, 1, cols], pt[:, h % 2, 1, :], vals[:, 0, h, :],
                          start=True, stop=False, skip_group_check=True)
                pe.matmul(ps_o[:, 1, cols], pt[:, h % 2, 2, :], vals[:, 1, h, :],
                          start=False, stop=True, skip_group_check=True).then_inc(q["b_pv"], 1)

            def b_ot(b):
                wait(pe, q["b_on"], C * (b + 1))
                for hp in range(HP):
                    for c in range(C):
                        last = pe.transpose(ps_v[0][:, hp // 2, (hp % 2) * L + c * P:(hp % 2) * L + (c + 1) * P],
                                            on[:, c, hp * P:(hp + 1) * P], id_f[:])
                last.then_inc(q["b_ot_ps"], 1)

            def b_mask(b, e):
                k = (e + 1) % 2
                if e == 0:
                    wait(pe, q["b_pt"], HB * (b + 1))
                elif e == 1:
                    wait(pe, q["b_ot"], b + 1)
                else:
                    wait(pe, q["b_mo"], NE * b + e - 1)
                for hp in range(HP):
                    for c in range(C):
                        rows = slice(64 * c, 64 * c + 64)
                        last = pe.matmul(ps_v[k][:, c, hp * P:(hp + 1) * P],
                                         pick[rows, hp, e, :, :].rearrange("p a k -> p (a k)"), ohT[rows, :],
                                         start=True, stop=True, skip_group_check=True)
                last.then_inc(q["b_m_ps"], 1)

            def b_out(b, e):
                wait(pe, q["b_mo"], NE * b + e + 1)
                for hp in range(HP):
                    last = pe.matmul(ps_o[:, 0, 0:L], oe[:, hp, e, :], mo[:, e % 2, hp, :],
                                     start=(e == 0 and hp == 0), stop=(e == NE - 1 and hp == HP - 1),
                                     skip_group_check=True)
                last.then_inc(q["b_oe"], 1)

            def b_oat(b):
                wait(pe, q["b_oa"], b + 1)
                for c in range(C):
                    last = pe.transpose(ps_o[:, 1, c * P:(c + 1) * P], oa[:, c * P:(c + 1) * P], id_f[:])
                last.then_inc(q["b_oat_ps"], 1)

            def b_x2t(b, u):
                wait(pe, norms["lnB"]["rows"], C * (b + 1))
                for c in range(C):
                    last = pe.transpose(ps_o[:, 1, L + c * P:L + (c + 1) * P], x2[:, u, c, :], id_f[:])
                last.then_inc(q["b_x2t_ps"], 1)

            def c_qk(b, u):
                wait(pe, q["b_x2t"], b + 1)
                wait(pe, q["c_x3t"], b)
                for j in range(2):
                    last = pe.matmul(ps_c[:, j * L:(j + 1) * L], wl[:, j * D:(j + 1) * D], x2T[:, u, :],
                                     start=True, stop=True, skip_group_check=True)
                last.then_inc(q["c_qk_ps"], 1)

            def c_v(b, u):
                wait(pe, q["c_g"], 2 * (b + 1))
                for c in range(C):
                    last = pe.matmul(ps_c[:, c * D:(c + 1) * D], x2T[:, u, c * P:(c + 1) * P], wl[:, 2 * D:3 * D],
                                     start=True, stop=True, skip_group_check=True)
                last.then_inc(q["c_v_ps"], 1)

            def c_rot(b):
                wait(pe, q["c_q"], b + 1)
                wait(pe, q["c_v"], b + 1)
                pe.matmul(ps_c[:, :], rot_s[:], ql[:].rearrange("p a n -> p (a n)"),
                          start=True, stop=True, skip_group_check=True).then_inc(q["c_rot_ps"], 1)

            def c_krt(b):
                wait(pe, q["c_qr"], 3 * b + 3)
                for c in range(C):
                    last = pe.transpose(ps_c[:, c * P:(c + 1) * P], qr[:, 1, c * P:(c + 1) * P], id_f[:])
                last.then_inc(q["c_krt_ps"], 1)

            def c_kv(b):
                wait(pe, q["c_kr"], b + 1)
                for c in range(C):
                    last = pe.matmul(ps_c[:, L:L + D], kr[:, c, :], vl[:, c, :], start=(c == 0), stop=(c == C - 1),
                                     skip_group_check=True)
                last.then_inc(q["c_kv_ps"], 1)

            def c_out(b):
                wait(pe, q["c_kv"], b + 1)
                wait(pe, q["c_km"], 2 * (b + 1))
                for c in range(C):
                    pe.matmul(ps_c[:, c * D:(c + 1) * D], qr[:, 0, c * P:(c + 1) * P], kv[:],
                              start=True, stop=True, skip_group_check=True)
                    last = pe.matmul(ps_c[:, 2 * D + c * HL:2 * D + (c + 1) * HL], ql[:, 0, c * P:(c + 1) * P], kmh[:],
                                     start=True, stop=True, skip_group_check=True)
                last.then_inc(q["c_out_ps"], 1)

            def c_x3t(b):
                wait(pe, q["c_x3"], b + 1)
                for c in range(C):
                    last = pe.transpose(ps_c[:, c * P:(c + 1) * P], x3[:, c, :], id_f[:])
                last.then_inc(q["c_x3t_ps"], 1)

            pe.wait_ge(x_all_in, 16)
            pe.wait_ge(ready, READY)
            for n in range(TT):
                last = pe.matmul(ps_a[:, n * NH:(n + 1) * NH], x_all[:, n * P:(n + 1) * P],
                                 in_w[:, 2 * DI + 2 * D:2 * DI + 2 * D + NH], start=True, stop=True,
                                 skip_group_check=True)
            last.then_inc(dt_ps, 1)
            pe.wait_ge(prep, PREP)
            pe.wait_ge(prep_act, PREP_ACT)
            pe.wait_ge(oe_in, 16)
            pe.wait_ge(soft, 1)

            def slot(r, u, a, b, c):
                t = 2 * r + u
                if b:
                    b_gates(t - 1, 1 - u)
                if c:
                    c_qk(t - 2, u)
                if a:
                    a_xbc(t, u, r, 0)
                for k in range(HP):
                    if b:
                        b_qk(t - 1, 1 - u, k)
                    if a and k == 1:
                        a_xbc(t, u, r, 1)
                    if c and k == 3:
                        c_v(t - 2, u)
                for e in range(NE):
                    if b:
                        b_values(t - 1, 1 - u, e)
                    if a and e == 0:
                        a_z(t, u)
                    if a and e in (2, 4):
                        a_seg(t, (e - 2) // 2)
                    if a and e == 6:
                        a_xt(t)
                    if c and e == 3:
                        c_rot(t - 2)
                    if c and e == 5:
                        c_krt(t - 2)
                    if c and e == 7:
                        c_kv(t - 2)
                if b:
                    b_oht(t - 1)
                    b_scores(t - 1, 0)
                for h in range(HB):
                    if b and h < HB - 1:
                        b_scores(t - 1, h + 1)
                    if a and h == 0:
                        a_bg(t)
                    if a and h == 2:
                        a_state(t)
                    if a and h == 4:
                        a_inter(t)
                    if a and h == 6:
                        a_y(t)
                    if c and h == 3:
                        c_out(t - 2)
                    if b:
                        b_turn(t - 1, h)
                        if h >= 1:
                            b_pv(t - 1, h - 1)
                if b:
                    b_pv(t - 1, HB - 1)
                if a:
                    a_yt(t)
                if b:
                    b_mask(t - 1, 0)
                    b_ot(t - 1)
                for e in range(NE):
                    if b and e < NE - 1:
                        b_mask(t - 1, e + 1)
                    if b:
                        b_out(t - 1, e)
                    if a and e == 0:
                        a_op(t)
                    if c and e == 2:
                        c_x3t(t - 2)
                    if a and e == 6:
                        a_x1t(t, u)
                if b:
                    b_oat(t - 1)
                    b_x2t(t - 1, 1 - u)

            slot(0, 0, True, False, False)
            slot(0, 1, True, True, False)
            with pe.Fori(1, NB // 2) as pair:
                for u in range(2):
                    slot(pair, u, True, True, True)
            slot(NB // 2, 0, False, True, True)
            slot(NB // 2, 1, False, False, True)

        @block.scalar
        def _(act):
            def copy(dst, src):
                return nc.scalar.activation(dst, src, ACT.Copy)

            def a_cin(b, half):
                wait(act, q["a_xbc_ps"], 2 * b + half + 1)
                wait(act, q["a_conv"], NCH * TAPS * b)
                copy(cin[:, 2 * half:2 * half + 2, TAPS - 1:], ps_a[:].rearrange("p (j n) -> p j n", j=2)
                     ).then_inc(q["a_cin"], 1)

            def a_tz(b):
                wait(act, q["a_z_ps"], b + 1)
                wait(act, q["a_sz"], b)
                nc.scalar.activation(tz[:].rearrange("p c n -> p (c n)"), ps_a[:], ACT.Tanh, scale=0.5
                                     ).then_inc(q["a_tz"], 1)

            def a_th(b):
                wait(act, q["a_conv"], NCH * TAPS * (b + 1))
                wait(act, q["a_y_ps"], b)
                nc.scalar.activation(xbc[:], cacc[:], ACT.Tanh).then_inc(q["a_th"], 1)

            def a_lx(b, c):
                wait(act, q["a_seg_ps"], C * b + c + 1)
                wait(act, q["a_mx"], C * b)
                wait(act, q["a_xst"], b)
                nc.scalar.activation(lx[:, c, :, :].rearrange("p h t -> p (h t)"), ps_a[:], ACT.Exp
                                     ).then_inc(q["a_lx"], 1)

            def a_btok(b):
                wait(act, q["a_bg_ps"], b + 1)
                wait(act, q["a_st_ps"], b)
                copy(btok[:], ps_a[:, 0:P]).then_inc(q["a_btok"], 1)
                wait(act, q["a_int"], 2 * b)
                nc.scalar.activation(ep[:], ps_a[:, 3 * P:3 * P + NH], ACT.Exp).then_inc(q["a_ep"], 1)

            def a_st(b):
                wait(act, q["a_st_ps"], b + 1)
                wait(act, q["a_int_ps"], b)
                copy(st[:], ps_a[:, 0:DI]).then_inc(q["a_st"], 1)

            def a_sq(b):
                wait(act, q["a_yg"], b + 1)
                for c in range(C):
                    if c == 1:
                        wait(act, q["a_sq"], C * b + 1)
                    nc.scalar.activation(sq[:], yg[:, c, :], ACT.Square, scale=0.5, accum_out=ssq[:, c:c + 1]
                                         ).then_inc(q["a_sq"], 1)

            def a_yt(b):
                wait(act, q["a_yt_ps"], b + 1)
                wait(act, q["a_op_ps"], b)
                copy(yT[:].rearrange("p j n -> p (j n)"), ps_a[:]).then_inc(q["a_yt"], 1)

            def a_x1h(b, u):
                wait(act, q["a_x1t_ps"], b + 1)
                wait(act, q["b_v_ps"], NE * (b - 1))
                copy(x1H[:, u, :], ps_a[:, 0:L]).then_inc(q["a_x1h"], 1)

            def b_eg(b):
                wait(act, q["b_g_ps"], b + 1)
                wait(act, q["b_gate"], 7 * b)
                nc.scalar.activation(eg[:].rearrange("p c h e -> p (c h e)"), ps_o[:, 1, 0:P], ACT.Exp, scale=-1.0
                                     ).then_inc(q["b_eg"], 1)

            def b_qk(b, hp):
                wait(act, q["b_qk_ps"], HP * b + hp + 1)
                wait(act, q["b_s_ps"], HB * b)
                copy(qk[:, hp, :, :].rearrange("p a n -> p (a n)"), ps_v[hp // 2][:, hp % 2, :]
                     ).then_inc(q["b_qk"], 1)

            def b_v0(b):
                wait(act, q["b_v_ps"], NE * b + 1)
                wait(act, q["b_pv"], HB * b)
                copy(vals[:].rearrange("p c h k -> p c (h k)"), ps_v[0][:]).then_inc(q["b_v0"], 1)

            def b_oht(b):
                wait(act, q["b_oht_ps"], b + 1)
                wait(act, q["b_m_ps"], NE * b)
                copy(ohT[:], ps_o[:, 1, P:2 * P]).then_inc(q["b_oht"], 1)

            def b_probs(b, h):
                wait(act, q["b_max"], 3 * HB * b + 3 * h + 3)
                if h >= 2:
                    wait(act, q["b_pt_ps"], HB * b + h - 1)
                else:
                    wait(act, q["b_rg"], 2 * b)
                sc = ps_v[0][:, h % 2, :]
                nc.scalar.activation(pr[:, h % 2, 0, :], sc[:, 0:P], ACT.Exp, bias=n3[:, h % 2, 0:1], scale=SCALE,
                                     accum_out=rs[:, 0, h:h + 1]).then_inc(q["b_p"], 1)
                nc.scalar.activation(pr[:, h % 2, 1:3, :].rearrange("p a b -> p (a b)"), sc[:, P:3 * P], ACT.Exp,
                                     bias=n3[:, h % 2, 1:2], scale=SCALE,
                                     accum_out=rs[:, 1, h:h + 1]).then_inc(q["b_p"], 1)

            def b_pt(b, h):
                wait(act, q["b_pt_ps"], HB * b + h + 1)
                if h >= 2:
                    wait(act, q["b_pv"], HB * b + h - 1)
                copy(pt[:, h % 2, :, :].rearrange("p a b -> p (a b)"), ps_v[1][:, h % 2, 0:3 * P]
                     ).then_inc(q["b_pt"], 1)

            def b_ot(b):
                wait(act, q["b_ot_ps"], b + 1)
                wait(act, q["b_mo"], NE * b)
                copy(oT[:].rearrange("p (a b) n -> p a (b n)", a=2), ps_v[0][:]).then_inc(q["b_ot"], 1)

            def b_oa(b):
                wait(act, q["b_oe"], NE * (b + 1))
                copy(oa[:], ps_o[:, 0, 0:L]).then_inc(q["b_oa"], 1)

            def b_x2t(b, u):
                wait(act, q["b_x2t_ps"], b + 1)
                wait(act, q["c_v_ps"], b - 1)
                copy(x2T[:, u, :], ps_o[:, 1, L:2 * L]).then_inc(q["b_x2t"], 1)

            def c_gelu(b):
                wait(act, q["c_qk_ps"], b + 1)
                wait(act, q["c_q"], b)
                wait(act, q["c_km"], 2 * b)
                nc.scalar.activation(gl[:, 0, :], ps_c[:, 0:L], ACT.Gelu, bias=bq_s[:]).then_inc(q["c_g"], 1)
                nc.scalar.activation(gl[:, 1, :], ps_c[:, L:2 * L], ACT.Gelu, bias=bk_s[:],
                                     accum_out=ks[:]).then_inc(q["c_g"], 1)

            def c_kr(b):
                wait(act, q["c_krt_ps"], b + 1)
                copy(kr[:].rearrange("p c d -> p (c d)"), ps_c[:, 0:L]).then_inc(q["c_kr"], 1)

            def c_x3t(b):
                wait(act, q["c_x3t_ps"], b + 1)
                wait(act, x3_stored, 32 * b)
                copy(x3T[:], ps_c[:, 0:L]).then_inc(q["c_x3t"], 1)

            act.wait_ge(ready, READY)
            copy(wqH[:], wq_f[:]).then_inc(prep_act, 1)
            copy(wkH[:], wk_f[:]).then_inc(prep_act, 1)
            copy(wgH[:], wg_f[:]).then_inc(prep_act, 1)
            copy(veH[:].rearrange("p e n -> p (e n)"), ve_f[:]).then_inc(prep_act, 1)
            nc.scalar.activation(ea[:], alog[:], ACT.Exp).then_inc(prep_act, 1)
            act.wait_ge(soft, 2)
            nc.scalar.activation(su[:], sa[:], ACT.Exp, scale=-1.0).then_inc(soft_act, 1)

            def slot(r, u, a, b, c):
                t = 2 * r + u
                if c:
                    c_gelu(t - 2)
                if b:
                    b_eg(t - 1)
                if a:
                    a_cin(t, 0)
                for k in range(HP):
                    if b:
                        b_qk(t - 1, k)
                    if a and k == 1:
                        a_cin(t, 1)
                for e in range(NE):
                    if b and e == 0:
                        b_v0(t - 1)
                    if a and e == 0:
                        a_tz(t)
                    if a and e in (2, 4):
                        a_lx(t, (e - 2) // 2)
                    if a and e == 5:
                        a_th(t)
                    if c and e == 5:
                        c_kr(t - 2)
                if b:
                    b_oht(t - 1)
                for h in range(HB):
                    if b:
                        b_probs(t - 1, h)
                        b_pt(t - 1, h)
                    if a and h == 0:
                        a_btok(t)
                    if a and h == 2:
                        a_st(t)
                if a:
                    a_sq(t)
                    a_yt(t)
                if b:
                    b_ot(t - 1)
                for e in range(NE):
                    if c and e == 2:
                        c_x3t(t - 2)
                    if a and e == 6:
                        a_x1h(t, u)
                if b:
                    b_oa(t - 1)
                    b_x2t(t - 1, 1 - u)

            slot(0, 0, True, False, False)
            slot(0, 1, True, True, False)
            with act.Fori(1, NB // 2) as pair:
                for u in range(2):
                    slot(pair, u, True, True, True)
            slot(NB // 2, 0, False, True, True)
            slot(NB // 2, 1, False, False, True)

        @block.vector
        def _(dve):
            V = nc.vector

            def a_steps(b):
                wait_apart(dve, (q["a_xd"], 2 * b), (q["a_bg_ps"], b), (q["a_am"], C * b))
                V.tensor_copy(dt_b[:], dt_all[:, bass.ds(b * C, C), :]).then_inc(q["a_step"], 1)
                V.tensor_copy(a_b[:], a_all[:, bass.ds(b * C, C), :]).then_inc(q["a_step"], 1)

            def a_conv(b, half):
                if half == 0:
                    wait(dve, q["a_th"], b)
                    wait(dve, q["a_xbc"], b)
                wait(dve, q["a_cin"], 2 * b + half + 1)
                n0 = NCH * TAPS * b + 2 * TAPS * half
                for k in range(TAPS):
                    for j in range(2):
                        ch = 2 * half + j
                        tap = TAPS - 1 - k
                        if k == 0:
                            ins = V.tensor_scalar(cacc[:, ch, :], cin[:, ch, tap:tap + L], cw[:, ch, tap:tap + 1],
                                                  cb[:, ch:ch + 1], ALU.mult, ALU.add)
                        else:
                            wait(dve, q["a_conv"], n0 + 2 * (k - 1) + j + 1)
                            ins = V.scalar_tensor_tensor(cacc[:, ch, :], cin[:, ch, tap:tap + L],
                                                         cw[:, ch, tap:tap + 1], cacc[:, ch, :], ALU.mult, ALU.add)
                        ins.then_inc(q["a_conv"], 1)

            def a_sz(b):
                wait(dve, q["a_tz"], b + 1)
                wait(dve, q["a_yg"], b)
                V.scalar_tensor_tensor(sz[:].rearrange("p c n -> p (c n)"), tz[:].rearrange("p c n -> p (c n)"), 1.0,
                                       ps_a[:], ALU.add, ALU.mult).then_inc(q["a_sz"], 1)

            def a_xbc(b):
                wait(dve, q["a_th"], b + 1)
                V.scalar_tensor_tensor(xbc[:], xbc[:], 1.0, cacc[:], ALU.add, ALU.mult).then_inc(q["a_xbc"], 1)

            def a_xd(b):
                wait(dve, q["a_xt_ps"], b + 1)
                wait(dve, q["a_step"], 2 * (b + 1))
                ps = ps_a[:].rearrange("p (c h d) -> p c h d", c=C, h=NH)
                V.tensor_tensor(xd[:], ps, dt_b[:].unsqueeze(3).to_broadcast([P, C, NH, HD]), ALU.mult
                                ).then_inc(q["a_xd"], 1)
                V.tensor_tensor(xD[:], ps, d_h[:].unsqueeze(1).unsqueeze(3).to_broadcast([P, C, NH, HD]), ALU.mult
                                ).then_inc(q["a_xd"], 1)

            def a_xst(b):
                wait(dve, q["a_lx"], C * b + 1)
                wait(dve, q["a_xd"], 2 * b + 2)
                wait(dve, q["a_st_ps"], b)
                V.tensor_tensor(xst[:], xd[:, 0, :, :], lx[:, 0, :, P - 1:P].to_broadcast([P, NH, HD]), ALU.mult
                                ).then_inc(q["a_xst"], 1)

            def a_gm(b):
                wait(dve, q["a_ep"], b + 1)
                wait(dve, q["a_mx"], C * b)
                V.tensor_tensor(gm[:], ps_a[:, P:3 * P].rearrange("p (c t) -> p c t", c=C),
                                causal_s[:].unsqueeze(1).to_broadcast([P, C, P]), ALU.mult).then_inc(q["a_gm"], 1)

            def a_mx(b):
                wait(dve, q["a_gm"], b + 1)
                wait(dve, q["a_lx"], C * (b + 1))
                wait(dve, q["a_y_ps"], b)
                for c in range(C):
                    V.tensor_tensor(mx[:, c, :, :], lx[:, c, :, :], gm[:, c, :].unsqueeze(1).to_broadcast([P, NH, P]),
                                    ALU.mult).then_inc(q["a_mx"], 1)

            def a_int(b):
                wait(dve, q["a_int_ps"], b + 1)
                wait(dve, q["a_ep"], b + 1)
                V.tensor_tensor(inter[:], ps_a[:, DI:2 * DI].rearrange("p (h d) -> p h d", h=NH),
                                ep[:].unsqueeze(2).to_broadcast([P, NH, HD]), ALU.mult).then_inc(q["a_int"], 1)
                wait(dve, q["a_int"], 2 * b + 1)
                V.tensor_tensor(xD[:, 1, :, :], xD[:, 1, :, :], inter[:], ALU.add).then_inc(q["a_int"], 1)

            def a_y(b):
                wait(dve, q["a_y_ps"], b + 1)
                wait(dve, q["a_int"], 2 * b + 2)
                V.tensor_tensor(ya[:].rearrange("p c n -> p (c n)"), ps_a[:], xD[:].rearrange("p c h d -> p (c h d)"),
                                ALU.add).then_inc(q["a_y"], 1)
                wait(dve, q["a_y"], b + 1)
                wait(dve, q["a_sq"], C * b)
                wait(dve, q["a_yt_ps"], b)
                V.tensor_tensor(yg[:], ya[:], sz[:], ALU.mult).then_inc(q["a_yg"], 1)

            def a_res(b, u):
                V_r = rstd_of("rms")
                wait(dve, norms["rms"]["rstd"], RSQRT_OPS * (b + 1))
                wait(dve, q["a_op_ps"], b + 1)
                V.tensor_scalar(V_r[:], V_r[:], 0.5, None, ALU.mult).then_inc(norms["rms"]["rows"], 1)
                wait(dve, norms["rms"]["rows"], b + 1)
                for c in range(C):
                    V.scalar_tensor_tensor(ra[:, c, :], ps_a[:, c * D:(c + 1) * D], V_r[:, c:c + 1], x_in[:, u, c, :],
                                           ALU.mult, ALU.add).then_inc(q["a_r"], 1)
                wait(dve, q["a_r"], C * (b + 1))
                stats(dve, "ln1", ra, b)
                V.tensor_tensor(xb[:], x_in[:, u, :, :], lnb[:].unsqueeze(1).to_broadcast([P, C, D]), ALU.add
                                ).then_inc(q["a_xb"], 1)

            def a_ln1(b):
                scale_rows(dve, "ln1", ra, na, b)
                wait(dve, norms["ln1"]["rows"], C * (b + 1))
                V.tensor_tensor(na[:], na[:], lnw[:].unsqueeze(1).to_broadcast([P, C, D]), ALU.mult
                                ).then_inc(q["a_n"], 1)
                wait(dve, q["a_n"], 2 * b + 1)
                wait(dve, q["a_xb"], b + 1)
                V.tensor_tensor(na[:], na[:], xb[:], ALU.add).then_inc(q["a_n"], 1)
                wait(dve, q["a_n"], 2 * b + 2)
                stats(dve, "ln2", na, b)

            def a_ln2(b, u):
                wait(dve, norms["lnB"]["rows"], C * (b - 1))
                wait(dve, norms["ln2"]["rstd"], RSQRT_OPS * (b + 1))
                for c in range(C):
                    ins = V.tensor_scalar(x1[:, u, c, :], na[:, c, :], nbuf["ln2"][1][:, c, 0:1],
                                          rstd_of("ln2")[:, c:c + 1], ALU.subtract, ALU.mult)
                ins.then_inc(q["a_x1"], 1)

            def a_x1l(b, u):
                wait(dve, q["a_x1h"], b + 1)
                V.tensor_tensor(x1L[:, u, :], ps_a[:, 0:L], x1H[:, u, :].bitcast(F32), ALU.subtract
                                ).then_inc(q["a_x1l"], 1)

            def b_gate(b):
                k = 7 * b
                n = q["b_gate"]
                wait(dve, q["b_eg"], b + 1)
                V.tensor_scalar(eg[:], eg[:], 1.0, None, ALU.add).then_inc(n, 1)
                wait(dve, n, k + 1)
                V.reciprocal(g[:], eg[:]).then_inc(n, 1)
                wait(dve, n, k + 2)
                V.tensor_reduce(gx[:], g[:], AX.X, ALU.max).then_inc(n, 1)
                wait(dve, n, k + 3)
                V.tensor_tensor(geq[:], g[:], gx[:].unsqueeze(3).to_broadcast([P, C, HB, NE]), ALU.is_equal
                                ).then_inc(n, 1)
                wait(dve, n, k + 4)
                V.tensor_tensor(geq[:], geq[:], w8_s[:].unsqueeze(1).unsqueeze(1).to_broadcast([P, C, HB, NE]),
                                ALU.mult).then_inc(n, 1)
                wait(dve, n, k + 5)
                V.tensor_reduce(g2[:], geq[:], AX.X, ALU.max).then_inc(n, 1)
                wait(dve, n, k + 6)
                V.tensor_tensor(oh[:], geq[:], g2[:].unsqueeze(3).to_broadcast([P, C, HB, NE]), ALU.is_equal
                                ).then_inc(n, 1)

            def b_v(b, e):
                if e == 1:
                    wait_apart(dve, (q["b_v_ps"], NE * b + 2), (q["b_v0"], b + 1), (q["b_gate"], 7 * b + 7))
                else:
                    wait_apart(dve, (q["b_v_ps"], NE * b + e + 1), (q["b_v"], (NE - 1) * b + e - 1))
                for c in range(C):
                    ins = V.copy_predicated(vals[:, c, :, :],
                                            oh[:, c, :, e:e + 1].bitcast(I32).to_broadcast([P, HB, DH]),
                                            ps_v[e % 2][:, c, :].rearrange("p (h k) -> p h k", h=HB))
                ins.then_inc(q["b_v"], 1)

            def b_vg(b):
                wait(dve, q["b_v"], (NE - 1) * (b + 1))
                for c in range(C):
                    V.tensor_tensor(vals[:, c, :, :], vals[:, c, :, :],
                                    gx[:, c, :].unsqueeze(2).to_broadcast([P, HB, DH]), ALU.mult
                                    ).then_inc(q["b_vg"], 1)

            def b_max(b, h):
                n, k = q["b_max"], 3 * HB * b + 3 * h
                wait(dve, q["b_s_ps"], HB * b + h + 1)
                if h >= 2:
                    wait(dve, q["b_p"], 2 * HB * b + 2 * (h - 1))
                V.tensor_reduce(r3[:, h % 2, :], ps_v[0][:, h % 2, 0:3 * P].rearrange("p (a b) -> p a b", a=3),
                                AX.X, ALU.max).then_inc(n, 1)
                wait(dve, n, k + 1)
                V.tensor_scalar(n3[:, h % 2, :], r3[:, h % 2, :], -SCALE, None, ALU.mult).then_inc(n, 1)
                wait(dve, n, k + 2)
                V.tensor_tensor(n3[:, h % 2, 1:2], n3[:, h % 2, 1:2], n3[:, h % 2, 2:3], ALU.min).then_inc(n, 1)

            def b_on(b):
                wait(dve, q["b_p"], 2 * HB * (b + 1))
                V.reciprocal(rg[:], rs[:]).then_inc(q["b_rg"], 1)
                wait(dve, q["b_rg"], 2 * b + 1)
                V.tensor_tensor(rg[:], rg[:], gx[:], ALU.mult).then_inc(q["b_rg"], 1)
                wait(dve, q["b_rg"], 2 * b + 2)
                wait(dve, q["b_pv"], HB * (b + 1))
                for c in range(C):
                    V.tensor_tensor(on[:, c, :].rearrange("p (h k) -> p h k", h=HB),
                                    ps_o[:, c, :].rearrange("p (h k) -> p h k", h=HB),
                                    rg[:, c, :].unsqueeze(2).to_broadcast([P, HB, DH]), ALU.mult
                                    ).then_inc(q["b_on"], 1)

            def b_mo(b, e):
                wait(dve, q["b_m_ps"], NE * b + e + 1)
                if e == 0:
                    wait(dve, q["b_ot"], b + 1)
                    wait(dve, q["b_oe"], NE * b)
                elif e >= 2:
                    wait(dve, q["b_oe"], NE * b + e - 1)
                V.tensor_tensor(mo[:, e % 2, :, :].rearrange("p a (c n) -> p c a n", c=C),
                                oT[:].rearrange("p a (c n) -> p c a n", c=C),
                                ps_v[(e + 1) % 2][:].rearrange("p c (a n) -> p c a n", a=HP), ALU.mult
                                ).then_inc(q["b_mo"], 1)

            def b_res(b, u):
                wait(dve, q["b_oat_ps"], b + 1)
                V.tensor_tensor(rb[:].rearrange("p c d -> p (c d)"), ps_o[:, 1, 0:L],
                                x1[:, u, :, :].rearrange("p c d -> p (c d)"), ALU.add).then_inc(q["b_r"], 1)
                wait(dve, q["b_r"], b + 1)
                stats(dve, "lnB", rb, b)
                wait(dve, norms["lnC"]["rows"], C * (b - 1))
                scale_rows(dve, "lnB", rb, x2[:, u, :, :], b)

            def c_q(b):
                wait(dve, q["c_g"], 2 * (b + 1))
                wait(dve, q["c_out_ps"], b)
                V.tensor_scalar(ql[:], gl[:], SHIFT, None, ALU.add).then_inc(q["c_q"], 1)

            def c_v(b):
                wait(dve, q["c_v_ps"], b + 1)
                wait(dve, q["c_kv_ps"], b)
                V.tensor_tensor(vl[:], ps_c[:, 0:L].rearrange("p (c d) -> p c d", c=C),
                                bv_s[:].unsqueeze(1).to_broadcast([P, C, D]), ALU.add).then_inc(q["c_v"], 1)

            def c_qr(b):
                n, k = q["c_qr"], 3 * b
                wait(dve, q["c_q"], b + 1)
                V.tensor_tensor(t2[:], ql[:], cos_s[:].unsqueeze(1).to_broadcast([P, 2, L]), ALU.mult).then_inc(n, 1)
                wait(dve, q["c_rot_ps"], b + 1)
                V.tensor_tensor(t1[:], ps_c[:].rearrange("p (a n) -> p a n", a=2),
                                sin_s[:].unsqueeze(1).to_broadcast([P, 2, L]), ALU.mult).then_inc(n, 1)
                wait(dve, n, k + 2)
                wait(dve, q["c_out_ps"], b)
                V.tensor_tensor(qr[:], t1[:], t2[:], ALU.add).then_inc(n, 1)

            def c_kv(b):
                wait(dve, q["c_kv_ps"], b + 1)
                wait(dve, q["c_out_ps"], b)
                V.tensor_tensor(kv[:], ps_c[:, L:L + D], hof_n[:], ALU.mult).then_inc(q["c_kv"], 1)

            def c_res(b, u):
                wait(dve, q["c_out_ps"], b + 1)
                V.tensor_scalar(zd[:].rearrange("p c h -> p (c h)"), ps_c[:, 2 * D:2 * D + C * HL], 1e-6, None, ALU.add
                                ).then_inc(q["c_z"], 1)
                wait(dve, q["c_z"], 2 * b + 1)
                V.reciprocal(zr[:], zd[:]).then_inc(q["c_z"], 1)
                wait(dve, q["c_z"], 2 * b + 2)
                V.tensor_tensor(rc[:], ps_c[:, 0:L].rearrange("p (c h e) -> p c h e", c=C, h=HL),
                                zr[:].unsqueeze(3).to_broadcast([P, C, HL, WL]), ALU.mult).then_inc(q["c_res"], 1)
                wait(dve, q["c_res"], 2 * b + 1)
                V.tensor_tensor(rc2[:], rc[:].rearrange("p c h e -> p c (h e)"), x2[:, u, :, :], ALU.add
                                ).then_inc(q["c_res"], 1)
                wait(dve, q["c_res"], 2 * b + 2)
                stats(dve, "lnC", rc2, b)
                V.tensor_tensor(xc[:], x2[:, u, :, :], bet[:].unsqueeze(1).to_broadcast([P, C, D]), ALU.add
                                ).then_inc(q["c_n"], 1)

            def c_ln(b):
                scale_rows(dve, "lnC", rc2, ncn, b)
                wait(dve, norms["lnC"]["rows"], C * (b + 1))
                V.tensor_tensor(n2[:], ncn[:], gam[:].unsqueeze(1).to_broadcast([P, C, D]), ALU.mult
                                ).then_inc(q["c_n"], 1)
                wait(dve, q["c_n"], 3 * b + 2)
                V.tensor_tensor(n2[:], n2[:], xc[:], ALU.add).then_inc(q["c_n"], 1)
                wait(dve, q["c_n"], 3 * b + 3)
                stats(dve, "lnD", n2, b)

            def c_x3(b):
                wait(dve, norms["lnD"]["rstd"], RSQRT_OPS * (b + 1))
                wait(dve, x3_stored, 32 * b)
                for c in range(C):
                    ins = V.tensor_scalar(x3[:, c, :], n2[:, c, :], nbuf["lnD"][1][:, c, 0:1],
                                          rstd_of("lnD")[:, c:c + 1], ALU.subtract, ALU.mult)
                ins.then_inc(q["c_x3"], 1)

            dve.wait_ge(ready, READY)
            V.tensor_copy(id_b[:], id_f[:]).then_inc(prep, 1)
            V.tensor_copy(negb[:], negb_f[:]).then_inc(prep, 1)
            V.tensor_scalar(hof_n[:], hof[:], 1.0 / L, None, ALU.mult).then_inc(prep, 1)
            V.tensor_copy(h16[:], hof[:].rearrange("p (h e) -> p h e", h=HL)[:, :, 0]).then_inc(prep, 1)
            V.tensor_scalar(cw[:], cw0[:], 0.5, None, ALU.mult).then_inc(prep, 1)
            V.tensor_scalar(cb[:], cb0[:], 0.5, None, ALU.mult).then_inc(prep, 1)
            for j in range(2):
                V.tensor_scalar(out_w[:, j, :], out_w0[:, j, :], nw[:, j:j + 1], None, ALU.mult).then_inc(prep, 1)
            V.memset(cin[:, :, 0:TAPS - 1], 0.0).then_inc(prep, 1)
            V.tensor_tensor(idfold[:], id_f[:, 0:64], id_f[:, 64:128], ALU.add).then_inc(prep, 1)
            dve.wait_ge(prep, 10)
            for hp in range(HP):
                ins = V.tensor_copy(pick[:, hp, :, :, :],
                                    idfold[:, 2 * hp * NE:2 * (hp + 1) * NE].rearrange("p (a e) -> p e a", a=2)
                                    .unsqueeze(3).to_broadcast([P, NE, 2, DH]))
            ins.then_inc(prep, 1)
            for n, (lo, full, hi) in enumerate(((wqL, wq_f, wqH), (wkL, wk_f, wkH), (wgL, wg_f, wgH))):
                dve.wait_ge(prep_act, n + 1)
                V.tensor_tensor(lo[:], full[:], hi[:].bitcast(F32), ALU.subtract).then_inc(prep, 1)
            dve.wait_ge(prep_act, 4)
            V.tensor_tensor(veL[:].rearrange("p e n -> p (e n)"), ve_f[:],
                            veH[:].rearrange("p e n -> p (e n)").bitcast(F32), ALU.subtract).then_inc(prep, 1)

            dve.wait_ge(dt_ps, 1)
            V.tensor_tensor(sv[:], ps_a[:, 0:TT * NH].rearrange("p (n h) -> p n h", h=NH),
                            dtb[:].unsqueeze(1).to_broadcast([P, TT, NH]), ALU.add).then_inc(soft, 1)
            dve.wait_ge(soft, 1)
            V.scalar_tensor_tensor(sa[:], sv[:], -1.0, sv[:], ALU.mult, ALU.max).then_inc(soft, 1)
            dve.wait_ge(soft_act, 1)
            V.tensor_scalar(sd[:], su[:], 2.0, None, ALU.add).then_inc(soft, 1)
            dve.wait_ge(soft, 3)
            V.reciprocal(sd[:], sd[:]).then_inc(soft, 1)
            dve.wait_ge(soft, 4)
            V.tensor_tensor(sd[:], sd[:], su[:], ALU.mult).then_inc(soft, 1)
            dve.wait_ge(soft, 5)
            V.tensor_tensor(s2[:], sd[:], sd[:], ALU.mult).then_inc(soft, 1)
            dve.wait_ge(soft, 6)
            V.tensor_scalar(sp[:], s2[:], 1.0 / (2 * LOG1P_TERMS + 1), None, ALU.mult).then_inc(soft, 1)
            at = 7
            for k in range(LOG1P_TERMS - 1, 0, -1):
                dve.wait_ge(soft, at)
                V.scalar_tensor_tensor(sp[:], sp[:], 1.0 / (2 * k + 1), s2[:], ALU.add, ALU.mult).then_inc(soft, 1)
                at += 1
            dve.wait_ge(soft, at)
            V.scalar_tensor_tensor(sp[:], sp[:], 1.0, sd[:], ALU.add, ALU.mult).then_inc(soft, 1)
            V.tensor_scalar(sv[:], sv[:], 0.0, None, ALU.max).then_inc(soft, 1)
            dve.wait_ge(soft, at + 2)
            V.scalar_tensor_tensor(dt_all[:], sp[:], 2.0, sv[:], ALU.mult, ALU.add).then_inc(soft, 1)
            dve.wait_ge(soft, at + 3)
            dve.wait_ge(prep_act, PREP_ACT)
            V.scalar_tensor_tensor(a_all[:], dt_all[:], -1.0, ea[:].unsqueeze(1).to_broadcast([P, TT, NH]),
                                   ALU.mult, ALU.mult).then_inc(soft, 1)
            dve.wait_ge(soft, at + 4)

            def slot(r, u, a, b, c):
                t = 2 * r + u
                if a:
                    a_steps(t)
                if c:
                    c_q(t - 2)
                if b:
                    b_gate(t - 1)
                if a:
                    a_conv(t, 0)
                if c:
                    c_v(t - 2)
                for e in range(NE):
                    if a and e == 0:
                        a_sz(t)
                    if b and e >= 1:
                        b_v(t - 1, e)
                    if a and e == 2:
                        a_conv(t, 1)
                    if a and e == 6:
                        a_xbc(t)
                    if a and e == 7:
                        a_xd(t)
                        a_xst(t)
                    if c and e == 3:
                        c_qr(t - 2)
                    if c and e == 7:
                        c_kv(t - 2)
                if b:
                    b_vg(t - 1)
                    b_max(t - 1, 0)
                for h in range(HB):
                    if b and h < HB - 1:
                        b_max(t - 1, h + 1)
                    if a and h == 0:
                        a_gm(t)
                    if a and h == 2:
                        a_mx(t)
                    if a and h == 4:
                        a_int(t)
                    if a and h == 6:
                        a_y(t)
                    if c and h == 3:
                        c_res(t - 2, u)
                    if c and h == 5:
                        c_ln(t - 2)
                    if c and h == 7:
                        c_x3(t - 2)
                if b:
                    b_on(t - 1)
                for e in range(NE):
                    if b:
                        b_mo(t - 1, e)
                    if a and e == 0:
                        a_res(t, u)
                    if a and e == 2:
                        a_ln1(t)
                    if a and e == 4:
                        a_ln2(t, u)
                    if a and e == 6:
                        a_x1l(t, u)
                if b:
                    b_res(t - 1, 1 - u)

            slot(0, 0, True, False, False)
            slot(0, 1, True, True, False)
            with dve.Fori(1, NB // 2) as pair:
                for u in range(2):
                    slot(pair, u, True, True, True)
            slot(NB // 2, 0, False, True, True)
            slot(NB // 2, 1, False, False, True)

        @block.gpsimd
        def _(pool):
            G = nc.gpsimd

            def a_am(b):
                for c in range(C):
                    wait_apart(pool, (q["a_step"], 2 * (b + 1)), (q["a_seg_ps"], C * b))
                    G.affine_select(out=am[:, c, :, :], in_=a_b[:, c, :].unsqueeze(2).to_broadcast([P, NH, P]),
                                    compare_op=ALU.is_ge, fill=0.0, base=0, pattern=[[0, NH], [1, P]],
                                    channel_multiplier=-1).then_inc(q["a_am"], 1)

            def c_km(b):
                wait_apart(pool, (q["c_g"], 2 * (b + 1)), (q["c_out_ps"], b))
                G.tensor_scalar(km[:], ks[:], 1.0 / L, SHIFT, ALU.mult, ALU.add).then_inc(q["c_km"], 1)
                wait_apart(pool, (q["c_km"], 2 * b + 1))
                G.tensor_scalar(kmh[:], h16[:], km[:], None, ALU.mult).then_inc(q["c_km"], 1)

            pool.wait_ge(ready, READY)
            pool.wait_ge(prep, PREP)

            def slot(r, u, a, b, c):
                t = 2 * r + u
                if a:
                    a_am(t)
                if c:
                    c_km(t - 2)
                    rsqrt(pool, "lnC", t - 2, 1.0, 1e-12, norms["lnC"]["moments"], 2 * C)
                    rsqrt(pool, "lnD", t - 2, 1.0, EPS, norms["lnD"]["moments"], 2 * C)
                if a:
                    rsqrt(pool, "rms", t, 1.0 / DI, EPS, q["a_sq"], C)
                    rsqrt(pool, "ln1", t, 1.0, EPS, norms["ln1"]["moments"], 2 * C)
                    rsqrt(pool, "ln2", t, 1.0, EPS, norms["ln2"]["moments"], 2 * C)
                if b:
                    rsqrt(pool, "lnB", t - 1, 1.0, EPS, norms["lnB"]["moments"], 2 * C)

            slot(0, 0, True, False, False)
            slot(0, 1, True, True, False)
            with pool.Fori(1, NB // 2) as pair:
                for u in range(2):
                    slot(pair, u, True, True, True)
            slot(NB // 2, 0, False, True, True)
            slot(NB // 2, 1, False, False, True)


def soft_experts(nc, kept, x3_dram, x3T_dram, x3_stored, phi, W, b_exp, ident, out):
    y_dram = nc.dram_tensor("y_slots", (P, SB, NB * D), F32, kind="Internal").ap()
    y_stored = [kept.enter_context(nc.semaphore(f"y_stored{u}")) for u in range(2)]
    with ExitStack() as ctx:
        dispatch(nc, ctx, kept, x3_dram, x3T_dram, phi, W, b_exp, ident, y_dram, y_stored)
    with ExitStack() as ctx:
        combine(nc, ctx, kept, x3_dram, x3T_dram, phi, ident, y_dram, out)


def dispatch(nc, ctx, kept, x3_dram, x3T_dram, phi, W, b_exp, ident, y_dram, y_stored):
    def sb(name, shape, dt=F32):
        return ctx.enter_context(nc.sbuf_tensor(name, [P] + shape, dt))

    def sem(name):
        return kept.enter_context(nc.semaphore(name))

    id_f = sb("d_id", [P])
    id_r = sb("d_idr", [P], F32R)
    xtf = sb("d_xtf", [TT * P])
    xtH = sb("d_xtH", [TT * P], F32R)
    xtL = sb("d_xtL", [TT * P], F32R)
    xs = sb("d_xs", [TT, D])
    phf = sb("d_phf", [S])
    phH = sb("d_phH", [S], F32R)
    phL = sb("d_phL", [S], F32R)
    w = sb("d_w", [2, XB, D])
    bx = sb("d_bx", [2, XB])
    mxb = sb("d_mxb", [P])
    nH = sb("d_nH", [P], F32R)
    nL = sb("d_nL", [P], F32R)
    ex = sb("d_ex", [C, NB, P])
    sm = sb("d_sm", [P])
    sr = sb("d_sr", [P])
    slot_s = sb("d_slot", [NB, P])
    yt = sb("d_yt", [NB, P])
    ys = sb("d_ys", [2, NB, D])

    lg = ctx.enter_context(nc.psum_tensor("d_lg", [P, NB, P], F32))
    sl = ctx.enter_context(nc.psum_tensor("d_sl", [P, NB, P], F32))
    sl4 = sl[:].rearrange("p (j a) s -> p j (a s)", j=XB)

    ready = sem("d_ready")
    halves = sem("d_halves")
    halves_act = sem("d_halves_act")
    w_in = [sem(f"d_w_in{u}") for u in range(2)]
    names = """lg_ps max sub_ps ex sum mult slot_ps slot yt_ps yt ys_ps ys""".split()
    q = {n: sem("d_" + n) for n in names}
    block = ctx.enter_context(nc.Block())
    READY = 16 * 4

    @block.sync
    def _(sp):
        sp.dma_start(xtf[:], x3T_dram).then_inc(ready, 16)
        sp.dma_start(phf[:], phi).then_inc(ready, 16)
        sp.dma_start(id_f[:], ident).then_inc(ready, 16)
        sp.dma_start(xs[:], x3_dram.rearrange("(n p) d -> p n d", p=P)).then_inc(ready, 16)

        def load(s, u):
            for v in (XB * (s - 1), s * XB):
                sp.compute_val(v)
            sp.wait_ge(ready, READY)
            wait(sp, q["yt"], XB * (s - 1))
            sp.dma_start(w[:, u, :, :], W[:, bass.ds(s * XB, XB), :]).then_inc(w_in[u], 16)
            sp.dma_start(bx[:, u, :], b_exp[:, bass.ds(s * XB, XB)]).then_inc(w_in[u], 16)

        def store(s, u):
            for v in (2 * (s + 1), s * NB * D):
                sp.compute_val(v)
            sp.wait_ge(ready, READY)
            wait(sp, q["ys"], 2 * (s + 1))
            sp.dma_start(y_dram.rearrange("p k n -> p (k n)")[:, bass.ds(s * NB * D, NB * D)],
                         ys[:, u, :, :].rearrange("p b e -> p (b e)")).then_inc(y_stored[u], 16)

        load(0, 0)
        load(1, 1)
        with sp.Fori(1, SB // 2) as pair:
            for u in range(2):
                load(2 * pair + u, u)
                store(2 * pair + u - 2, u)
        for u in range(2):
            store(SB - 2 + u, u)
        for u in range(2):
            sp.wait_ge(y_stored[u], 16 * (SB // 2))

    @block.tensor
    def _(pe):
        def logits(s, c):
            wait(pe, q["ex"], 2 * (C * s + c))
            cols = bass.ds(s * P, P)
            for b in range(NB):
                n = b * C + c
                tile = slice(n * P, (n + 1) * P)
                pe.matmul(lg[:, b, :], xtH[:, tile], phH[:, cols], start=(b % 4 == 0), stop=False,
                          skip_group_check=True)
                pe.matmul(lg[:, b, :], xtH[:, tile], phL[:, cols], start=False, stop=False, skip_group_check=True)
                last = pe.matmul(lg[:, b, :], xtL[:, tile], phH[:, cols], start=False, stop=False,
                                 skip_group_check=True)
            last.then_inc(q["lg_ps"], 1)

        def subtract(s, c):
            wait(pe, q["max"], 3 * (C * s + c) + 3)
            for k in range(4):
                part = lg[:, 4 * k:4 * k + 4, :]
                pe.matmul(part, id_r[:], nH[:].unsqueeze(1).to_broadcast([P, 4, P]), start=False, stop=False,
                          skip_group_check=True)
                last = pe.matmul(part, id_r[:], nL[:].unsqueeze(1).to_broadcast([P, 4, P]), start=False,
                                 stop=True, skip_group_check=True)
                if k % 2:
                    last.then_inc(q["sub_ps"], 1)

        def slots(s, c):
            wait(pe, q["mult"], C * s + c + 1)
            if c == 0:
                wait(pe, q["ys"], 2 * s)
            for b in range(NB):
                last = pe.matmul(sl[:, b, :], xs[:, b * C + c, :], ex[:, c, b, :],
                                 start=(c == 0 and b % 4 == 0), stop=(c == C - 1), skip_group_check=True)
            last.then_inc(q["slot_ps"], 1)

        def experts(s, u, r):
            wait(pe, w_in[u], 32 * (r + 1))
            wait(pe, q["slot"], 2 * (s + 1))
            for j in range(XB):
                pe.matmul(sl4[:, j, :].rearrange("p (b n) -> p b n", b=NB), w[:, u, j, :],
                          slot_s[:, :, j * NS:(j + 1) * NS], start=True, stop=True, skip_group_check=True
                          ).then_inc(q["yt_ps"], 1)

        def turn(s):
            wait(pe, q["yt"], XB * (s + 1))
            for b in range(NB):
                last = pe.transpose(sl[:, b, :], yt[:, b, :], id_f[:])
                if b % 8 == 7:
                    last.then_inc(q["ys_ps"], 1)

        pe.wait_ge(ready, READY)
        pe.wait_ge(halves, 2)
        pe.wait_ge(halves_act, 3)
        logits(0, 0)
        subtract(0, 0)
        logits(0, 1)
        slots(0, 0)
        subtract(0, 1)

        def later(r, u):
            s = 2 * r + u
            sp_, rp, up = s - 1, r if u else r - 1, 1 - u
            logits(s, 0)
            slots(sp_, 1)
            subtract(s, 0)
            experts(sp_, up, rp)
            turn(sp_)
            logits(s, 1)
            slots(s, 0)
            subtract(s, 1)

        later(0, 1)
        with pe.Fori(1, SB // 2) as pair:
            for u in range(2):
                later(pair, u)
        slots(SB - 1, 1)
        experts(SB - 1, 1, SB // 2 - 1)
        turn(SB - 1)

    @block.scalar
    def _(act):
        def exps(s, c):
            for k in range(2):
                wait(act, q["sub_ps"], 2 * (C * s + c) + k + 1)
                if k == 0:
                    wait(act, q["slot_ps"], C * (s - 1) + c + 1)
                nc.scalar.activation(ex[:, c, 8 * k:8 * k + 8, :], lg[:, 8 * k:8 * k + 8, :], ACT.Exp
                                     ).then_inc(q["ex"], 1)

        def slots(s):
            wait(act, q["slot_ps"], C * (s + 1))
            wait(act, q["yt_ps"], XB * s)
            for k in range(2):
                nc.scalar.activation(slot_s[:, 8 * k:8 * k + 8, :], sl[:, 8 * k:8 * k + 8, :], ACT.Copy
                                     ).then_inc(q["slot"], 1)

        def experts(s, u):
            wait(act, q["ys_ps"], 2 * s)
            for j in range(XB):
                wait(act, q["yt_ps"], XB * s + j + 1)
                nc.scalar.activation(yt[:, :, j * NS:(j + 1) * NS], sl4[:, j, :].rearrange("p (b n) -> p b n", b=NB),
                                     ACT.Identity, bias=bx[:, u, j:j + 1]).then_inc(q["yt"], 1)

        def outputs(s, u, r):
            for k in range(2):
                wait(act, q["ys_ps"], 2 * s + k + 1)
                if k == 0:
                    wait(act, y_stored[u], 16 * r)
                nc.scalar.activation(ys[:, u, 8 * k:8 * k + 8, :], sl[:, 8 * k:8 * k + 8, :], ACT.Copy
                                     ).then_inc(q["ys"], 1)

        act.wait_ge(ready, READY)
        for dst, src in ((xtH, xtf), (phH, phf), (id_r, id_f)):
            nc.scalar.activation(dst[:], src[:], ACT.Copy).then_inc(halves_act, 1)
        exps(0, 0)
        exps(0, 1)

        def later(r, u):
            s = 2 * r + u
            slots(s - 1)
            exps(s, 0)
            experts(s - 1, 1 - u)
            outputs(s - 1, 1 - u, r if u else r - 1)
            exps(s, 1)

        later(0, 1)
        with act.Fori(1, SB // 2) as pair:
            for u in range(2):
                later(pair, u)
        slots(SB - 1)
        experts(SB - 1, 1)
        outputs(SB - 1, 1, SB // 2 - 1)

    @block.vector
    def _(dve):
        V = nc.vector

        def greatest(s, c):
            k = 3 * (C * s + c)
            wait(dve, q["lg_ps"], C * s + c + 1)
            wait(dve, q["max"], k)
            V.tensor_reduce(mxb[:], lg[:].rearrange("p b s -> p s b"), AX.X, ALU.max).then_inc(q["max"], 1)
            wait(dve, q["max"], k + 1)
            wait(dve, q["sub_ps"], 2 * (C * s + c))
            V.tensor_scalar(nH[:], mxb[:], -1.0, None, ALU.mult).then_inc(q["max"], 1)
            wait(dve, q["max"], k + 2)
            V.scalar_tensor_tensor(nL[:], mxb[:], -1.0, nH[:].bitcast(F32), ALU.mult, ALU.subtract
                                   ).then_inc(q["max"], 1)

        def sums(s, c):
            k = 2 * (C * s + c)
            wait(dve, q["ex"], k + 2)
            V.tensor_reduce(sm[:], ex[:, c, :, :].rearrange("p b s -> p s b"), AX.X, ALU.add).then_inc(q["sum"], 1)
            wait(dve, q["sum"], k + 1)
            V.reciprocal(sr[:], sm[:]).then_inc(q["sum"], 1)

        def scaled(s, c):
            wait(dve, q["sum"], 2 * (C * s + c) + 2)
            V.tensor_tensor(ex[:, c, :, :], ex[:, c, :, :], sr[:].unsqueeze(1).to_broadcast([P, NB, P]), ALU.mult
                            ).then_inc(q["mult"], 1)

        dve.wait_ge(halves_act, 2)
        V.tensor_tensor(xtL[:], xtf[:], xtH[:].bitcast(F32), ALU.subtract).then_inc(halves, 1)
        V.tensor_tensor(phL[:], phf[:], phH[:].bitcast(F32), ALU.subtract).then_inc(halves, 1)
        greatest(0, 0)
        sums(0, 0)
        greatest(0, 1)
        scaled(0, 0)

        def later(s):
            sums(s - 1, 1)
            greatest(s, 0)
            scaled(s - 1, 1)
            sums(s, 0)
            greatest(s, 1)
            scaled(s, 0)

        later(1)
        with dve.Fori(1, SB // 2) as pair:
            for u in range(2):
                later(2 * pair + u)
        sums(SB - 1, 1)
        scaled(SB - 1, 1)


def combine(nc, ctx, kept, x3_dram, x3T_dram, phi, ident, y_dram, out):
    def sb(name, shape, dt=F32):
        return ctx.enter_context(nc.sbuf_tensor(name, [P] + shape, dt))

    def sem(name):
        return kept.enter_context(nc.semaphore(name))

    id_f = sb("e_id", [P])
    phf = sb("e_phf", [S])
    phH = sb("e_phH", [S], F32R)
    phL = sb("e_phL", [S], F32R)
    xtf = sb("e_xtf", [2, L])
    xtH = sb("e_xtH", [2, L], F32R)
    xtL = sb("e_xtL", [2, L], F32R)
    xs = sb("e_xs", [2, C, D])
    yb = sb("e_yb", [2, SB, D])
    mxt = sb("e_mxt", [1])
    nmx = sb("e_nmx", [1])
    pr = sb("e_pr", [2, SB, P])
    prT = sb("e_prT", [SB, P])
    rs = sb("e_rs", [2])
    rr = sb("e_rr", [2])
    rx = sb("e_rx", [C, D])
    stt = sb("e_st", [C, 6])
    mv = sb("e_mv", [C, 2])
    v, h, y, t = (sb(f"e_n{k}", [C]) for k in range(4))
    xo = sb("e_xo", [2, C, D])

    lg = ctx.enter_context(nc.psum_tensor("e_lg", [P, 4, 512], F32))
    tp = [ctx.enter_context(nc.psum_tensor(f"e_tp{k}", [P, 512], F32)) for k in range(3)]
    po = ctx.enter_context(nc.psum_tensor("e_po", [P, 512], F32))

    ready = sem("e_ready")
    halves = sem("e_halves")
    halves_act = sem("e_halves_act")
    b_in = [sem(f"e_b_in{u}") for u in range(2)]
    stored = [sem(f"e_stored{u}") for u in range(2)]
    q = {n: sem("e_" + n) for n in "xh xl lg_ps max pr tp_ps tp out_ps inv res moments rstd rows".split()}
    block = ctx.enter_context(nc.Block())
    READY = 32
    LOADS = 48

    def wait_apart(eng, *waits):
        for _, value in waits:
            eng.compute_val(value)
        eng.wait_ge(ready, READY)
        for s, value in waits:
            wait(eng, s, value)

    @block.sync
    def _(sp):
        sp.dma_start(phf[:], phi).then_inc(ready, 16)
        sp.dma_start(id_f[:], ident).then_inc(ready, 16)

        def load(b, u):
            for value in (C * (b - 1), b * L, b * D):
                sp.compute_val(value)
            sp.wait_ge(ready, READY)
            wait(sp, q["res"], C * (b - 1))
            sp.dma_start(xtf[:, u, :], x3T_dram[:, bass.ds(b * L, L)]).then_inc(b_in[u], 16)
            sp.dma_start(xs[:, u, :, :], x3_dram[bass.ds(b * L, L), :].rearrange("(c p) d -> p c d", p=P)
                         ).then_inc(b_in[u], 16)
            sp.dma_start(yb[:, u, :, :], y_dram[:, :, bass.ds(b * D, D)]
                         ).then_inc(b_in[u], 16)

        def store(b, u):
            for value in (C * (b + 1), b * L):
                sp.compute_val(value)
            sp.wait_ge(ready, READY)
            wait(sp, q["rows"], C * (b + 1))
            sp.dma_start(out[bass.ds(b * L, L), :].rearrange("(c p) d -> p c d", p=P), xo[:, u, :, :]
                         ).then_inc(stored[u], 16)

        load(0, 0)
        load(1, 1)
        with sp.Fori(1, NB // 2) as pair:
            for u in range(2):
                load(2 * pair + u, u)
                store(2 * pair + u - 2, u)
        for u in range(2):
            store(NB - 2 + u, u)
        for u in range(2):
            sp.wait_ge(stored[u], 16 * (NB // 2))

    @block.tensor
    def _(pe):
        def logits(b, u, c):
            n = C * b + c
            wait(pe, q["xl"], b + 1)
            wait(pe, q["pr"], n)
            cols = slice(c * P, (c + 1) * P)
            for k in range(4):
                part = slice(k * 512, (k + 1) * 512)
                pe.matmul(lg[:, k, :], xtH[:, u, cols], phH[:, part], start=True, stop=False, skip_group_check=True)
                pe.matmul(lg[:, k, :], xtH[:, u, cols], phL[:, part], start=False, stop=False,
                          skip_group_check=True)
                last = pe.matmul(lg[:, k, :], xtL[:, u, cols], phH[:, part], start=False, stop=True,
                                 skip_group_check=True)
            last.then_inc(q["lg_ps"], 1)

        def weigh(n, u, c):
            wait(pe, q["pr"], n + 1)
            for k in range(4):
                if k < 3:
                    wait(pe, q["tp"], 4 * (n - 1) + k + 2 if k < 2 else 4 * n)
                else:
                    wait(pe, q["tp"], 4 * n + 1)
                for j in range(4):
                    last = pe.transpose(tp[k % 3][:, j * P:(j + 1) * P], pr[:, c, 4 * k + j, :], id_f[:])
                last.then_inc(q["tp_ps"], 1)
            wait(pe, q["res"], n)
            for k in range(4):
                wait(pe, q["tp"], 4 * n + k + 1)
                for j in range(4):
                    s = 4 * k + j
                    last = pe.matmul(po[:, 0:D], prT[:, s, :], yb[:, u, s, :], start=(s == 0), stop=(s == SB - 1),
                                     skip_group_check=True)
            last.then_inc(q["out_ps"], 1)

        pe.wait_ge(ready, READY)
        pe.wait_ge(halves, 1)
        pe.wait_ge(halves_act, 1)

        def batch(r, u, first=False):
            b = 2 * r + u
            logits(b, u, 0)
            if not first:
                weigh(C * b - 1, 1 - u, 1)
            logits(b, u, 1)
            pe.wait_ge(b_in[u], LOADS * (r + 1))
            weigh(C * b, u, 0)

        batch(0, 0, True)
        batch(0, 1)
        with pe.Fori(1, NB // 2) as pair:
            for u in range(2):
                batch(pair, u)
        weigh(TT - 1, 1, 1)

    @block.scalar
    def _(act):
        def split(b, u, r):
            wait(act, b_in[u], LOADS * (r + 1))
            wait(act, q["lg_ps"], C * (b - 1))
            nc.scalar.activation(xtH[:, u, :], xtf[:, u, :], ACT.Copy).then_inc(q["xh"], 1)

        def exps(n, c):
            wait(act, q["max"], 2 * (n + 1))
            wait(act, q["tp_ps"], 4 * (n - 1))
            wait(act, q["inv"], n - 1)
            nc.scalar.activation(pr[:, c, :, :].rearrange("p a s -> p (a s)"), lg[:].rearrange("p a s -> p (a s)"),
                                 ACT.Exp, bias=nmx[:], accum_out=rs[:, c:c + 1]).then_inc(q["pr"], 1)

        def turned(n, ks):
            for k in ks:
                wait(act, q["tp_ps"], 4 * n + k + 1)
                wait(act, q["out_ps"], n)
                nc.scalar.activation(prT[:, 4 * k:4 * k + 4, :].rearrange("p a s -> p (a s)"), tp[k % 3][:],
                                     ACT.Copy).then_inc(q["tp"], 1)

        act.wait_ge(ready, READY)
        nc.scalar.activation(phH[:], phf[:], ACT.Copy).then_inc(halves_act, 1)

        def batch(r, u, first=False):
            b = 2 * r + u
            split(b, u, r)
            if not first:
                turned(C * b - 1, range(4))
            exps(C * b, 0)
            turned(C * b, range(4))
            exps(C * b + 1, 1)

        batch(0, 0, True)
        batch(0, 1)
        with act.Fori(1, NB // 2) as pair:
            for u in range(2):
                batch(pair, u)
        turned(TT - 1, range(4))

    @block.vector
    def _(dve):
        V = nc.vector

        def split(b, u):
            wait(dve, q["xh"], b + 1)
            wait(dve, q["lg_ps"], C * (b - 1))
            V.tensor_tensor(xtL[:, u, :], xtf[:, u, :], xtH[:, u, :].bitcast(F32), ALU.subtract
                            ).then_inc(q["xl"], 1)

        def greatest(n):
            wait(dve, q["lg_ps"], n + 1)
            wait(dve, q["max"], 2 * n)
            V.tensor_reduce(mxt[:], lg[:].rearrange("p a s -> p (a s)"), AX.X, ALU.max).then_inc(q["max"], 1)
            wait(dve, q["max"], 2 * n + 1)
            wait(dve, q["pr"], n)
            V.tensor_scalar(nmx[:], mxt[:], -1.0, None, ALU.mult).then_inc(q["max"], 1)

        def residual(n, u, c):
            wait(dve, q["pr"], n + 1)
            V.reciprocal(rr[:, c:c + 1], rs[:, c:c + 1]).then_inc(q["inv"], 1)
            wait(dve, q["inv"], n + 1)
            wait(dve, q["out_ps"], n + 1)
            V.scalar_tensor_tensor(rx[:, c, :], po[:, 0:D], rr[:, c:c + 1], xs[:, u, c, :], ALU.mult, ALU.add
                                   ).then_inc(q["res"], 1)
            wait(dve, q["res"], n + 1)
            V.bn_stats(stt[:, c, :], rx[:, c, :]).then_inc(q["moments"], 1)
            wait_apart(dve, (q["moments"], 2 * n + 1))
            V.bn_aggr(mv[:, c, :], stt[:, c, :]).then_inc(q["moments"], 1)

        def norm(b, u, r):
            wait(dve, q["rstd"], RSQRT_OPS * (b + 1))
            wait(dve, stored[u], 16 * r)
            for c in range(C):
                V.tensor_scalar(xo[:, u, c, :], rx[:, c, :], mv[:, c, 0:1], y[:, c:c + 1], ALU.subtract, ALU.mult
                                ).then_inc(q["rows"], 1)

        dve.wait_ge(halves_act, 1)
        V.tensor_tensor(phL[:], phf[:], phH[:].bitcast(F32), ALU.subtract).then_inc(halves, 1)

        def batch(r, u, first=False):
            b = 2 * r + u
            split(b, u)
            greatest(C * b)
            if not first:
                residual(C * b - 1, 1 - u, 1)
            greatest(C * b + 1)
            if not first:
                norm(b - 1, 1 - u, r if u else r - 1)
            residual(C * b, u, 0)

        batch(0, 0, True)
        batch(0, 1)
        with dve.Fori(1, NB // 2) as pair:
            for u in range(2):
                batch(pair, u)
        residual(TT - 1, 1, 1)
        norm(NB - 1, 1, NB // 2 - 1)

    @block.gpsimd
    def _(pool):
        pool.wait_ge(ready, READY)

        def batch(b):
            newton(pool, wait_apart, q["rstd"], RSQRT_OPS * b, (q["moments"], 2 * C * (b + 1)),
                   mv[:, :, 1], 1.0, EPS, v, h, y, t)

        batch(0)
        batch(1)
        with pool.Fori(1, NB // 2) as pair:
            for u in range(2):
                batch(2 * pair + u)


def constants():
    import numpy as np

    f = np.float32
    i = np.arange(P)
    ident = np.eye(P, dtype=f)
    causal = (i[:, None] <= i[None, :]).astype(f)
    neg = np.zeros((P, 3, P), f)
    later = i[None, :] > i[:, None]
    neg[:, 0][later] = NEG
    neg[:, 2][later] = NEG
    strict = (i[:, None] > i[None, :]).astype(f)
    head_of = (i[:, None] // WL == i[None, :] // WL).astype(f)
    rot = np.zeros((P, P), f)
    rot[i[1::2], i[0::2]] = -1.0
    rot[i[0::2], i[1::2]] = 1.0
    inv = (f(1.0) / np.power(f(10000.0), np.arange(0, D, 2, dtype=f) / f(D))).astype(f)
    ang = (np.arange(L, dtype=f)[:, None] * inv).astype(f)
    cosT = np.repeat(np.cos(ang.astype(np.float64)).astype(f).T, 2, axis=0)
    sinT = np.repeat(np.sin(ang.astype(np.float64)).astype(f).T, 2, axis=0)
    w8 = np.broadcast_to(np.arange(NE, 0, -1).astype(f), (P, NE))
    return dict(ident=ident, causal=causal, neg_blocks=neg, strict_low=strict, upper=causal, head_of=head_of,
                rot=rot, cosT=cosT, sinT=sinT, w8=w8)


def layout(d):
    import numpy as np

    x = np.asarray(d["L0_attn_x"]).reshape(NB * L, D)
    wq, wk, wv = (np.asarray(d[f"L1_attn_W{n}"]).T for n in "qkv")
    a = dict(
        x=x, xT=x.T, in_wT=np.asarray(d["L0_attn_in_proj_w"]).T,
        conv_w=np.asarray(d["L0_attn_conv_w"]).reshape(NCH, P, TAPS).transpose(1, 0, 2),
        conv_b=np.asarray(d["L0_attn_conv_b"]).reshape(NCH, P).T,
        dt_bias=d["L0_attn_dt_bias"], A_log=d["L0_attn_A_log"], Dh=d["L0_attn_D"],
        norm_w=np.asarray(d["L0_attn_norm_w"]).reshape(2, P).T,
        out_wT=np.asarray(d["L0_attn_out_proj_w"]).T.reshape(2, P, D).transpose(1, 0, 2),
        ln_w=d["L0_attn_ln_w"], ln_b=d["L0_attn_ln_b"],
        w_q=d["L0_ffn_w_q"], w_k=d["L0_ffn_w_k"], w_gate=d["L0_ffn_w_gate"],
        v_exp=np.asarray(d["L0_ffn_value_experts"]).transpose(2, 0, 1, 3).reshape(D, NE * HB * DH),
        o_exp=np.asarray(d["L0_ffn_output_experts"]).reshape(NE, HP, 2, DH, D).transpose(2, 3, 1, 0, 4)
        .reshape(P, HP, NE, D),
        WqkvT=np.concatenate([wq, wk, wv], axis=1),
        bq=d["L1_attn_bq"], bk=d["L1_attn_bk"], bv=d["L1_attn_bv"],
        gamma=d["L1_attn_gamma"], beta=d["L1_attn_beta"],
        phi=np.asarray(d["L1_ffn_phi"]).reshape(D, S),
        W=np.asarray(d["L1_ffn_W"]).transpose(1, 0, 2), b_exp=np.asarray(d["L1_ffn_b"]).T,
    )
    a.update(constants())
    return {k: np.ascontiguousarray(v) for k, v in a.items()}


def kernel(**inputs):
    import numpy as np
    import concourse.bacc as bacc
    from concourse.bass_utils import run_bass_kernel_spmd

    nc = bacc.Bacc("TRN2", target_bir_lowering=False, num_devices=1)
    arrays = layout(inputs)
    aps = {k: nc.dram_tensor(k, v.shape, mybir.dt.from_np(v.dtype), kind="ExternalInput").ap()
           for k, v in arrays.items()}
    out = nc.dram_tensor("out", (NB * L, D), F32, kind="ExternalOutput").ap()
    build(nc, out=out, **aps)
    r = run_bass_kernel_spmd(nc, [arrays], core_ids=[0])
    return np.asarray(r.results[0]["out"]).reshape(NB, L, D)
```

```python
from contextlib import ExitStack

import concourse.bass as bass
from concourse import mybir

F32 = mybir.dt.float32
F32R = mybir.dt.float32r
BF16 = mybir.dt.bfloat16
I32 = mybir.dt.int32
ALU = mybir.AluOpType
ACT = mybir.ActivationFunctionType
AX = mybir.AxisListType

NB, L, D = 16, 256, 128
P = 128
C = L // P
NH, HD = 4, 64
DI = NH * HD
NCH = (DI + 2 * D) // P
TAPS = 4
EPS = 1e-5
HB, DH, NE = 8, 64, 8
HP = HB // 2
SCALE = DH ** -0.5
NEG = -3.0e38
SCB = 3
HL = 16
WL = D // HL
SHIFT = 0.21
NX, NS = 64, 32
S = NX * NS
SB = S // P
XB = P // NS
TT = NB * C
BK, BB = 4, NB // 4

RSQRT_SEED = float(0x5F3759DF)
RSQRT_STEPS = 3
RSQRT_OPS = 3 + 4 * RSQRT_STEPS
LOG1P_TERMS = 7


def wait(eng, sem, value):
    if not isinstance(value, int) or value > 0:
        eng.wait_ge(sem, value)


def newton(pool, wait_apart, done, k, source, var, scale, eps, v, h, y, t):
    wait_apart(pool, source)
    pool.tensor_scalar(v[:], var, scale, eps, ALU.mult, ALU.add).then_inc(done, 1)
    wait_apart(pool, (done, k + 1))
    pool.tensor_scalar(h[:], v[:], -0.5, None, ALU.mult).then_inc(done, 1)
    pool.tensor_scalar(y[:].bitcast(I32), v[:].bitcast(I32), -0.5, RSQRT_SEED,
                       ALU.mult, ALU.add).then_inc(done, 1)
    for s in range(RSQRT_STEPS):
        wait(pool, done, k + 3 + 4 * s)
        pool.tensor_tensor(t[:], y[:], y[:], ALU.mult).then_inc(done, 1)
        wait(pool, done, k + 4 + 4 * s)
        pool.tensor_tensor(t[:], t[:], h[:], ALU.mult).then_inc(done, 1)
        wait_apart(pool, (done, k + 5 + 4 * s))
        pool.tensor_scalar(t[:], t[:], 1.5, None, ALU.add).then_inc(done, 1)
        wait(pool, done, k + 6 + 4 * s)
        pool.tensor_tensor(y[:], y[:], t[:], ALU.mult).then_inc(done, 1)


def build(nc, x, xT, in_wT, conv_w, conv_b, dt_bias, A_log, Dh, norm_w, out_wT, ln_w, ln_b,
          w_q, w_k, w_gate, v_exp, o_exp, WqkvT, bq, bk, bv, gamma, beta, phi, W, b_exp,
          ident, causal, neg_blocks, strict_low, upper, head_of, rot, cosT, sinT, w8,
          out):
    x3_dram = nc.dram_tensor("x3_tok", (NB * L, D), F32, kind="Internal").ap()
    x3T_dram = nc.dram_tensor("x3_T", (D, NB * L), F32, kind="Internal").ap()
    ctx = ExitStack()
    with ctx:
        x3_stored = ctx.enter_context(nc.semaphore("x3_stored"))
        token_blocks(nc, ctx, x, xT, in_wT, conv_w, conv_b, dt_bias, A_log, Dh, norm_w, out_wT, ln_w, ln_b,
                     w_q, w_k, w_gate, v_exp, o_exp, WqkvT, bq, bk, bv, gamma, beta,
                     ident, causal, neg_blocks, strict_low, upper, head_of, rot, cosT, sinT, w8,
                     x3_dram, x3T_dram, x3_stored)
        soft_experts(nc, ctx, x3_dram, x3T_dram, x3_stored, phi, W, b_exp, ident, out)


def row(ap, n):
    return ap.rearrange("(a n) -> a n", a=1).to_broadcast([P, n])


def token_blocks(nc, kept, x, xT, in_wT, conv_w, conv_b, dt_bias, A_log, Dh, norm_w, out_wT, ln_w, ln_b,
                 w_q, w_k, w_gate, v_exp, o_exp, WqkvT, bq, bk, bv, gamma, beta,
                 ident, causal, neg_blocks, strict_low, upper, head_of, rot, cosT, sinT, w8,
                 x3_dram, x3T_dram, x3_stored):
    with ExitStack() as ctx:
        def sb(name, shape, dt=F32):
            return ctx.enter_context(nc.sbuf_tensor(name, [P] + shape, dt))

        def sem(name):
            return kept.enter_context(nc.semaphore(name))

        id_f = sb("id_f", [P])
        id_b = sb("id_b", [P], BF16)
        causal_s = sb("causal_s", [P])
        negb_f = sb("negb_f", [3, P])
        negb = sb("negb", [3, P], BF16)
        low_s = sb("low_s", [P])
        upp_s = sb("upp_s", [P])
        hof = sb("hof", [P])
        hof_n = sb("hof_n", [P])
        h16 = sb("h16", [HL])
        rot_s = sb("rot_s", [P])
        cos_s = sb("cos_s", [L])
        sin_s = sb("sin_s", [L])
        w8_s = sb("w8_s", [NE])
        in_w = sb("in_w", [2 * DI + 2 * D + NH])
        out_w0 = sb("out_w0", [2, D])
        out_w = sb("out_w", [2, D])
        cw0 = sb("cw0", [NCH, TAPS])
        cb0 = sb("cb0", [NCH])
        cw = sb("cw", [NCH, TAPS])
        cb = sb("cb", [NCH])
        nw = sb("nw", [2])
        dtb = sb("dtb", [NH])
        alog = sb("alog", [NH])
        d_h = sb("d_h", [NH])
        lnw = sb("lnw", [D])
        lnb = sb("lnb", [D])
        wq_f = sb("wq_f", [HB * DH])
        wk_f = sb("wk_f", [HB * DH])
        wg_f = sb("wg_f", [HB * NE])
        wqH = sb("wqH", [HB * DH], F32R)
        wqL = sb("wqL", [HB * DH], F32R)
        wkH = sb("wkH", [HB * DH], F32R)
        wkL = sb("wkL", [HB * DH], F32R)
        wgH = sb("wgH", [HB * NE], F32R)
        wgL = sb("wgL", [HB * NE], F32R)
        ve_f = sb("ve_f", [NE * HB * DH])
        veH = sb("veH", [NE, HB * DH], F32R)
        veL = sb("veL", [NE, HB * DH], F32R)
        oe = sb("oe", [HP, NE, D])
        x_all = oe[:, :, :, :].rearrange("p a e d -> p (a e d)")
        idfold = sb("idfold", [HB * NE])
        pick = sb("pick", [HP, NE, 2, DH], BF16)
        wl = sb("wl", [3 * D])
        bq_s = sb("bq_s", [1])
        bk_s = sb("bk_s", [1])
        bv_s = sb("bv_s", [D])
        gam = sb("gam", [D])
        bet = sb("bet", [D])

        sv = sb("sv", [TT, NH])
        sa = sb("sa", [TT, NH])
        su = sb("su", [TT, NH])
        sd = sb("sd", [TT, NH])
        s2 = sb("s2", [TT, NH])
        sp = sb("sp", [TT, NH])
        ea = sb("ea", [NH])
        dt_all = sb("dt_all", [TT, NH])
        a_all = sb("a_all", [TT, NH])

        xt_in = sb("xt_in", [2, L])
        x_in = sb("x_in", [2, C, D])
        dt_b = sb("dt_b", [C, NH])
        a_b = sb("a_b", [C, NH])
        cin = sb("cin", [NCH, L + TAPS - 1])
        cacc = sb("cacc", [NCH, L])
        xbc = sb("xbc", [NCH, L])
        xd = sb("xd", [C, NH, HD])
        xD = sb("xD", [C, NH, HD])
        btok = sb("btok", [P])
        gm = sb("gm", [C, P])
        am = sb("am", [C, NH, P])
        lx = sb("lx", [C, NH, P])
        mx = sb("mx", [C, NH, P])
        ep = sb("ep", [NH])
        xst = sb("xst", [NH, HD])
        st = sb("st", [DI])
        inter = sb("inter", [NH, HD])
        tz = sb("tz", [C, DI])
        sz = sb("sz", [C, DI])
        ya = sb("ya", [C, DI])
        yg = sb("yg", [C, DI])
        sq = sb("sq", [DI])
        ssq = sb("ssq", [C])
        yT = sb("yT", [2, L])
        ra = sb("ra", [C, D])
        na = sb("na", [C, D])
        xb = sb("xb", [C, D])
        x1 = sb("x1", [2, C, D])
        x1H = sb("x1H", [2, L], F32R)
        x1L = sb("x1L", [2, L], F32R)

        eg = sb("eg", [C, HB, NE])
        g = sb("g", [C, HB, NE])
        gx = sb("gx", [C, HB])
        geq = sb("geq", [C, HB, NE])
        g2 = sb("g2", [C, HB])
        oh = sb("oh", [C, HB, NE])
        ohT = sb("ohT", [P], BF16)
        qk = sb("qk", [HP, 2, L])
        vals = sb("vals", [C, HB, DH])
        r3 = sb("r3", [SCB, 3])
        n3 = sb("n3", [SCB, 3])
        pr = ve_f[:, 2048:2816].rearrange("p (s a n) -> p s a n", s=2, a=3)
        pt = ve_f[:, 2816:3584].rearrange("p (s a n) -> p s a n", s=2, a=3)
        rs = sb("rs", [C, HB])
        rg = sb("rg", [C, HB])
        on = sb("on", [C, HB * DH])
        oT = sb("oT", [HP, L])
        mo = ve_f[:, 0:2 * HP * L].rearrange("p (s a n) -> p s a n", s=2, a=HP)
        oa = sb("oa", [L])
        rb = sb("rb", [C, D])
        x2 = sb("x2", [2, C, D])
        x2T = sb("x2T", [2, L])

        gl = wk_f[:, :].rearrange("p (a n) -> p a n", a=2)
        ks = sb("ks", [1])
        km = sb("km", [1])
        kmh = sb("kmh", [HL])
        ql = sb("ql", [2, L])
        t1 = ve_f[:, 3584:4096].rearrange("p (a n) -> p a n", a=2)
        t2 = wq_f[:, :].rearrange("p (a n) -> p a n", a=2)
        qr = sb("qr", [2, L])
        vl = sb("vl", [C, D])
        kr = sb("kr", [C, D])
        kv = sb("kv", [D])
        zd = sb("zd", [C, HL])
        zr = sb("zr", [C, HL])
        rc = sb("rc", [C, HL, WL])
        rc2 = sb("rc2", [C, D])
        ncn = sb("ncn", [C, D])
        n2 = sb("n2", [C, D])
        xc = sb("xc", [C, D])
        x3 = sb("x3", [C, D])
        x3T = sb("x3T", [L])

        bank = [ctx.enter_context(nc.psum_tensor(f"bk{i}", [P, C, 512], F32)) for i in (0, 2)]
        ps_v = bank
        ps_s = [bank[k // 2][:, k % 2, :] for k in range(SCB)]
        ps_o = ctx.enter_context(nc.psum_tensor("ps_o", [P, C, 512], F32))
        ps_a = ctx.enter_context(nc.psum_tensor("ps_a", [P, 512], F32))
        ps_c = ctx.enter_context(nc.psum_tensor("ps_c", [P, 512], F32))

        ready = sem("ready")
        x_all_in = sem("x_all_in")
        oe_in = sem("oe_in")
        prep = sem("prep")
        prep_act = sem("prep_act")
        dt_ps = sem("dt_ps")
        soft = sem("soft")
        soft_act = sem("soft_act")
        x_in_sem = [sem(f"x_in_sem{u}") for u in range(2)]

        names = """a_step a_xbc_ps a_cin a_conv a_th a_xbc a_z_ps a_tz a_sz a_am a_seg_ps a_lx a_mx a_xt_ps a_xd
            a_bg_ps a_btok a_ep a_gm a_xst a_st_ps a_st a_int_ps a_int a_y_ps a_y a_yg a_sq a_yt_ps a_yt
            a_op_ps a_r a_xb a_n a_x1t_ps a_x1h a_x1l a_x1
            b_g_ps b_eg b_gate b_oht_ps b_oht b_qk_ps b_qk b_v_ps b_v0 b_v b_vg b_s_ps b_max b_p b_pt_ps b_pt
            b_pv b_rg b_on b_ot_ps b_ot b_m_ps b_mo b_oe b_oa b_oat_ps b_r b_x2t_ps b_x2t
            c_qk_ps c_g c_km c_q c_v_ps c_v c_rot_ps c_qr c_krt_ps c_kr c_kv_ps c_kv c_out_ps c_z c_res c_n
            c_x3t_ps c_x3t c_x3""".split()
        q = {n: sem(n) for n in names}
        norms = {n: {k: sem(f"{n}_{k}") for k in ("moments", "rstd", "rows")}
                 for n in ("rms", "ln1", "ln2", "lnB", "lnC", "lnD")}
        nbuf = {n: (sb(f"{n}_st", [C, 6]), sb(f"{n}_mv", [C, 2]), sb(f"{n}_v", [C]), sb(f"{n}_h", [C]),
                    sb(f"{n}_y", [C]), sb(f"{n}_t", [C])) for n in norms}

        CONSTS = [(id_f, ident), (causal_s, causal), (negb_f, neg_blocks), (low_s, strict_low), (upp_s, upper),
                  (hof, head_of), (rot_s, rot), (cos_s, cosT), (sin_s, sinT), (w8_s, w8), (in_w, in_wT),
                  (out_w0, out_wT), (cw0, conv_w), (cb0, conv_b), (nw, norm_w),
                  (wq_f, w_q), (wk_f, w_k), (wg_f, w_gate), (ve_f, v_exp), (wl, WqkvT)]
        ROWS = [(dtb, dt_bias, NH), (alog, A_log, NH), (d_h, Dh, NH), (lnw, ln_w, D), (lnb, ln_b, D),
                (bv_s, bv, D), (gam, gamma, D), (bet, beta, D)]
        COLS = [(bq_s, bq), (bk_s, bk)]
        READY = 16 * (len(CONSTS) + len(ROWS) + len(COLS))
        PREP = 15
        PREP_ACT = 5

        def wait_apart(eng, *waits):
            for _, v in waits:
                eng.compute_val(v)
            eng.wait_ge(ready, READY)
            for s, v in waits:
                wait(eng, s, v)

        def var_of(n):
            return nbuf[n][1][:, :, 1] if n != "rms" else ssq[:]

        def rstd_of(n):
            return nbuf[n][4]

        def stats(dve, n, src, b):
            stt, mv = nbuf[n][0], nbuf[n][1]
            for c in range(C):
                dve.bn_stats(stt[:, c, :], src[:, c, :]).then_inc(norms[n]["moments"], 1)
            for c in range(C):
                wait_apart(dve, (norms[n]["moments"], 2 * C * b + c + 1))
                dve.bn_aggr(mv[:, c, :], stt[:, c, :]).then_inc(norms[n]["moments"], 1)

        def rsqrt(pool, n, b, scale, eps, source, per):
            _, _, v, h, y, t = nbuf[n]
            newton(pool, wait_apart, norms[n]["rstd"], RSQRT_OPS * b, (source, per * b + per), var_of(n), scale, eps,
                   v, h, y, t)

        def scale_rows(dve, n, src, dst, b):
            wait(dve, norms[n]["rstd"], RSQRT_OPS * (b + 1))
            for c in range(C):
                dve.tensor_scalar(dst[:, c, :], src[:, c, :], nbuf[n][1][:, c, 0:1], rstd_of(n)[:, c:c + 1],
                                  ALU.subtract, ALU.mult).then_inc(norms[n]["rows"], 1)

        block = ctx.enter_context(nc.Block())

        @block.sync
        def _(sp):
            sp.dma_start(x_all, xT).then_inc(x_all_in, 16)
            for dst, src in CONSTS:
                sp.dma_start(dst[:], src).then_inc(ready, 16)
            for dst, src, n in ROWS:
                sp.dma_start(dst[:], row(src, n)).then_inc(ready, 16)
            for dst, src in COLS:
                sp.dma_start(dst[:], src.rearrange("(p a) -> p a", a=1)).then_inc(ready, 16)
            sp.wait_ge(dt_ps, 1)
            sp.dma_start(oe[:], o_exp).then_inc(oe_in, 16)

            def load(b, u):
                for v in (b - 1, C * (b - 1), b * L):
                    sp.compute_val(v)
                sp.wait_ge(x_all_in, 16)
                wait(sp, q["a_xb"], b - 1)
                wait(sp, q["a_z_ps"], b - 1)
                wait(sp, q["a_r"], C * (b - 1))
                sp.dma_start(xt_in[:, u, :], xT[:, bass.ds(b * L, L)]).then_inc(x_in_sem[u], 16)
                sp.dma_start(x_in[:, u, :, :], x[bass.ds(b * L, L), :].rearrange("(c p) d -> p c d", p=P)
                             ).then_inc(x_in_sem[u], 16)

            def store(b):
                for v in (b + 1, b * L):
                    sp.compute_val(v)
                sp.wait_ge(x_all_in, 16)
                wait(sp, q["c_x3"], b + 1)
                sp.dma_start(x3_dram[bass.ds(b * L, L), :].rearrange("(c p) d -> p c d", p=P), x3[:]
                             ).then_inc(x3_stored, 16)
                sp.wait_ge(x_all_in, 16)
                wait(sp, q["c_x3t"], b + 1)
                sp.dma_start(x3T_dram[:, bass.ds(b * L, L)], x3T[:]).then_inc(x3_stored, 16)

            load(0, 0)
            load(1, 1)
            load(2, 0)
            with sp.Fori(1, NB // 2 - 1) as pair:
                for u in range(2):
                    load(2 * pair + u + 1, 1 - u)
                    store(2 * pair + u - 2)
            load(NB - 1, 1)
            for b in range(NB - 4, NB):
                store(b)
            sp.wait_ge(x3_stored, 32 * NB)

        @block.tensor
        def _(pe):
            def mm3(ps, lh, ll, rh, rl, first=True, last=True):
                pe.matmul(ps, lh, rh, start=first, stop=False, skip_group_check=True)
                pe.matmul(ps, lh, rl, start=False, stop=False, skip_group_check=True)
                return pe.matmul(ps, ll, rh, start=False, stop=last, skip_group_check=True)

            def a_xbc(b, u, r, half):
                if half == 0:
                    wait(pe, x_in_sem[u], 32 * (r + 1))
                    wait(pe, q["a_y"], b)
                else:
                    wait(pe, q["a_cin"], 2 * b + 1)
                for j in range(2):
                    ch = DI + (2 * half + j) * P
                    last = pe.matmul(ps_a[:, j * L:(j + 1) * L], in_w[:, ch:ch + P], xt_in[:, u, :],
                                     start=True, stop=True, skip_group_check=True)
                last.then_inc(q["a_xbc_ps"], 1)

            def a_z(b, u):
                wait(pe, q["a_cin"], 2 * b + 2)
                wait(pe, q["a_x1h"], b)
                wait(pe, q["a_x1l"], b)
                for c in range(C):
                    last = pe.matmul(ps_a[:, c * DI:(c + 1) * DI], xt_in[:, u, c * P:(c + 1) * P], in_w[:, 0:DI],
                                     start=True, stop=True, skip_group_check=True)
                last.then_inc(q["a_z_ps"], 1)

            def a_seg(b, c):
                if c == 0:
                    wait(pe, q["a_sz"], b + 1)
                else:
                    wait(pe, q["a_lx"], C * b + 1)
                wait(pe, q["a_am"], C * b + c + 1)
                pe.matmul(ps_a[:, :], low_s[:], am[:, c, :, :].rearrange("p h t -> p (h t)"),
                          start=True, stop=True, skip_group_check=True).then_inc(q["a_seg_ps"], 1)

            def a_xt(b):
                wait(pe, q["a_xbc"], b + 1)
                wait(pe, q["a_lx"], C * b + 2)
                for c in range(C):
                    for j in range(2):
                        last = pe.transpose(ps_a[:, c * DI + j * P:c * DI + (j + 1) * P],
                                            xbc[:, j, c * P:(c + 1) * P], id_f[:])
                last.then_inc(q["a_xt_ps"], 1)

            def a_bg(b):
                wait(pe, q["a_xd"], 2 * b + 2)
                pe.transpose(ps_a[:, 0:P], xbc[:, 2, 0:P], id_f[:])
                for c in range(C):
                    pe.matmul(ps_a[:, (c + 1) * P:(c + 2) * P], xbc[:, 2, c * P:(c + 1) * P],
                              xbc[:, 3, c * P:(c + 1) * P], start=True, stop=True, skip_group_check=True)
                pe.matmul(ps_a[:, 3 * P:3 * P + NH], upp_s[:], a_b[:, 1, :], start=True, stop=True,
                          skip_group_check=True).then_inc(q["a_bg_ps"], 1)

            def a_state(b):
                wait(pe, q["a_gm"], b + 1)
                wait(pe, q["a_ep"], b + 1)
                wait(pe, q["a_btok"], b + 1)
                wait(pe, q["a_xst"], b + 1)
                pe.matmul(ps_a[:, 0:DI], btok[:], xst[:].rearrange("p h d -> p (h d)"),
                          start=True, stop=True, skip_group_check=True).then_inc(q["a_st_ps"], 1)

            def a_inter(b):
                wait(pe, q["a_st"], b + 1)
                pe.matmul(ps_a[:, DI:2 * DI], xbc[:, 3, P:2 * P], st[:],
                          start=True, stop=True, skip_group_check=True).then_inc(q["a_int_ps"], 1)

            def a_y(b):
                wait(pe, q["a_mx"], C * b + C)
                wait(pe, q["a_int"], 2 * b + 1)
                for c in range(C):
                    for h in range(NH):
                        last = pe.matmul(ps_a[:, c * DI + h * HD:c * DI + (h + 1) * HD], mx[:, c, h, :],
                                         xd[:, c, h, :], start=True, stop=True, skip_group_check=True)
                last.then_inc(q["a_y_ps"], 1)

            def a_yt(b, more):
                wait(pe, q["a_yg"], b + 1)
                if more:
                    wait(pe, q["a_cin"], 2 * b + 4)
                for j in range(2):
                    for c in range(C):
                        last = pe.transpose(ps_a[:, j * L + c * P:j * L + (c + 1) * P],
                                            yg[:, c, j * P:(j + 1) * P], id_f[:])
                last.then_inc(q["a_yt_ps"], 1)

            def a_op(b):
                wait(pe, q["a_yt"], b + 1)
                for c in range(C):
                    for j in range(2):
                        last = pe.matmul(ps_a[:, c * D:(c + 1) * D], yT[:, j, c * P:(c + 1) * P], out_w[:, j, :],
                                         start=(j == 0), stop=(j == 1), skip_group_check=True)
                last.then_inc(q["a_op_ps"], 1)

            def a_x1t(b, u):
                wait(pe, q["a_x1"], b + 1)
                for c in range(C):
                    last = pe.transpose(ps_a[:, c * P:(c + 1) * P], x1[:, u, c, :], id_f[:])
                last.then_inc(q["a_x1t_ps"], 1)

            def b_gates(b, u):
                wait(pe, q["a_x1h"], b + 1)
                wait(pe, q["a_x1l"], b + 1)
                wait(pe, q["b_r"], b)
                for c in range(C):
                    cols = slice(c * P, (c + 1) * P)
                    last = mm3(ps_o[:, 1, c * 64:c * 64 + 64], x1H[:, u, cols], x1L[:, u, cols], wgH[:], wgL[:])
                last.then_inc(q["b_g_ps"], 1)

            def b_qk(b, u, hp):
                wait(pe, q["b_mo"], NE * b)
                bankq = ps_v[hp // 2][:, hp % 2, :]
                pe_cols = slice(hp * P, (hp + 1) * P)
                mm3(bankq[:, 0:L], wqH[:, pe_cols], wqL[:, pe_cols], x1H[:, u, :], x1L[:, u, :])
                mm3(bankq[:, L:2 * L], wkH[:, pe_cols], wkL[:, pe_cols], x1H[:, u, :], x1L[:, u, :]
                    ).then_inc(q["b_qk_ps"], 1)

            def b_values(b, u, e):
                if e < 2:
                    wait(pe, q["b_qk"], HP * b + 2 * e + 2)
                elif e == 2:
                    wait(pe, q["b_v0"], b + 1)
                else:
                    wait(pe, q["b_v"], (NE - 1) * b + e - 2)
                for c in range(C):
                    cols = slice(c * P, (c + 1) * P)
                    last = mm3(ps_v[e % 2][:, c, :], x1H[:, u, cols], x1L[:, u, cols], veH[:, e, :], veL[:, e, :])
                last.then_inc(q["b_v_ps"], 1)

            def b_oht(b):
                wait(pe, q["b_gate"], 7 * b + 7)
                wait(pe, q["b_x2t"], b)
                pe.transpose(ps_o[:, 1, P:2 * P], oh[:].rearrange("p c h e -> p (c h e)"), id_f[:]
                             ).then_inc(q["b_oht_ps"], 1)

            def b_scores(b, h):
                if h < SCB:
                    wait(pe, q["b_v"], (NE - 1) * (b + 1))
                else:
                    wait(pe, q["b_p"], 2 * HB * b + 2 * (h - SCB + 1))
                sc = ps_s[h % SCB]
                half = slice(64 * (h % 2), 64 * (h % 2) + 64)
                pe.matmul(sc[:, 0:3 * P], id_b[:], negb[:].rearrange("p a b -> p (a b)"),
                          start=True, stop=False, skip_group_check=True)
                pe.matmul(sc[:, 0:P], qk[half, h // 2, 0, 0:P], qk[half, h // 2, 1, 0:P],
                          start=False, stop=False, skip_group_check=True)
                pe.matmul(sc[:, P:3 * P], qk[half, h // 2, 0, P:L], qk[half, h // 2, 1, :],
                          start=False, stop=True, skip_group_check=True).then_inc(q["b_s_ps"], 1)

            def b_turn(b, h):
                wait(pe, q["b_p"], 2 * HB * b + 2 * h + 2)
                if h >= 1:
                    wait(pe, q["b_pt"], HB * b + h)
                for k in range(3):
                    last = pe.transpose(ps_v[1][:, 1, k * P:(k + 1) * P], pr[:, h % 2, k, :], id_f[:])
                last.then_inc(q["b_pt_ps"], 1)

            def b_pv(b, h):
                wait(pe, q["b_pt"], HB * b + h + 1)
                if h == 0:
                    wait(pe, q["b_vg"], C * (b + 1))
                    wait(pe, q["b_oht"], b + 1)
                cols = slice(h * DH, (h + 1) * DH)
                pe.matmul(ps_o[:, 0, cols], pt[:, h % 2, 0, :], vals[:, 0, h, :],
                          start=True, stop=True, skip_group_check=True)
                pe.matmul(ps_o[:, 1, cols], pt[:, h % 2, 1, :], vals[:, 0, h, :],
                          start=True, stop=False, skip_group_check=True)
                pe.matmul(ps_o[:, 1, cols], pt[:, h % 2, 2, :], vals[:, 1, h, :],
                          start=False, stop=True, skip_group_check=True).then_inc(q["b_pv"], 1)

            def b_ot(b):
                for c in range(C):
                    wait(pe, q["b_on"], C * b + c + 1)
                    for hp in range(HP):
                        last = pe.transpose(ps_v[0][:, hp // 2, (hp % 2) * L + c * P:(hp % 2) * L + (c + 1) * P],
                                            on[:, c, hp * P:(hp + 1) * P], id_f[:])
                last.then_inc(q["b_ot_ps"], 1)

            def b_mask(b, e):
                k = (e + 1) % 2
                if e == 0:
                    wait(pe, q["b_pt"], HB * (b + 1))
                elif e == 1:
                    wait(pe, q["b_ot"], b + 1)
                else:
                    wait(pe, q["b_mo"], NE * b + e - 1)
                for hp in range(HP):
                    for c in range(C):
                        rows = slice(64 * c, 64 * c + 64)
                        last = pe.matmul(ps_v[k][:, c, hp * P:(hp + 1) * P],
                                         pick[rows, hp, e, :, :].rearrange("p a k -> p (a k)"), ohT[rows, :],
                                         start=True, stop=True, skip_group_check=True)
                last.then_inc(q["b_m_ps"], 1)

            def b_out(b, e):
                wait(pe, q["b_mo"], NE * b + e + 1)
                for hp in range(HP):
                    last = pe.matmul(ps_o[:, 0, 0:L], oe[:, hp, e, :], mo[:, e % 2, hp, :],
                                     start=(e == 0 and hp == 0), stop=(e == NE - 1 and hp == HP - 1),
                                     skip_group_check=True)
                last.then_inc(q["b_oe"], 1)

            def b_oat(b):
                wait(pe, q["b_oa"], b + 1)
                for c in range(C):
                    last = pe.transpose(ps_o[:, 1, c * P:(c + 1) * P], oa[:, c * P:(c + 1) * P], id_f[:])
                last.then_inc(q["b_oat_ps"], 1)

            def b_x2t(b, u, more):
                wait(pe, norms["lnB"]["rows"], C * (b + 1))
                if more:
                    wait(pe, q["b_eg"], b + 2)
                for c in range(C):
                    last = pe.transpose(ps_o[:, 1, L + c * P:L + (c + 1) * P], x2[:, u, c, :], id_f[:])
                last.then_inc(q["b_x2t_ps"], 1)

            def c_qk(b, u):
                wait(pe, q["b_x2t"], b + 1)
                wait(pe, q["c_x3t"], b)
                for j in range(2):
                    last = pe.matmul(ps_c[:, j * L:(j + 1) * L], wl[:, j * D:(j + 1) * D], x2T[:, u, :],
                                     start=True, stop=True, skip_group_check=True)
                last.then_inc(q["c_qk_ps"], 1)

            def c_v(b, u):
                wait(pe, q["c_g"], 2 * (b + 1))
                for c in range(C):
                    last = pe.matmul(ps_c[:, c * D:(c + 1) * D], x2T[:, u, c * P:(c + 1) * P], wl[:, 2 * D:3 * D],
                                     start=True, stop=True, skip_group_check=True)
                last.then_inc(q["c_v_ps"], 1)

            def c_rot(b):
                wait(pe, q["c_q"], b + 1)
                wait(pe, q["c_v"], b + 1)
                pe.matmul(ps_c[:, :], rot_s[:], ql[:].rearrange("p a n -> p (a n)"),
                          start=True, stop=True, skip_group_check=True).then_inc(q["c_rot_ps"], 1)

            def c_krt(b):
                wait(pe, q["c_qr"], 3 * b + 3)
                for c in range(C):
                    last = pe.transpose(ps_c[:, c * P:(c + 1) * P], qr[:, 1, c * P:(c + 1) * P], id_f[:])
                last.then_inc(q["c_krt_ps"], 1)

            def c_kv(b):
                wait(pe, q["c_kr"], b + 1)
                for c in range(C):
                    last = pe.matmul(ps_c[:, L:L + D], kr[:, c, :], vl[:, c, :], start=(c == 0), stop=(c == C - 1),
                                     skip_group_check=True)
                last.then_inc(q["c_kv_ps"], 1)

            def c_out(b):
                wait(pe, q["c_kv"], b + 1)
                wait(pe, q["c_km"], 2 * (b + 1))
                for c in range(C):
                    pe.matmul(ps_c[:, c * D:(c + 1) * D], qr[:, 0, c * P:(c + 1) * P], kv[:],
                              start=True, stop=True, skip_group_check=True)
                    last = pe.matmul(ps_c[:, 2 * D + c * HL:2 * D + (c + 1) * HL], ql[:, 0, c * P:(c + 1) * P], kmh[:],
                                     start=True, stop=True, skip_group_check=True)
                last.then_inc(q["c_out_ps"], 1)

            def c_x3t(b):
                wait(pe, q["c_x3"], b + 1)
                for c in range(C):
                    last = pe.transpose(ps_c[:, c * P:(c + 1) * P], x3[:, c, :], id_f[:])
                last.then_inc(q["c_x3t_ps"], 1)

            pe.wait_ge(x_all_in, 16)
            pe.wait_ge(ready, READY)
            for n in range(TT):
                last = pe.matmul(ps_a[:, n * NH:(n + 1) * NH], x_all[:, n * P:(n + 1) * P],
                                 in_w[:, 2 * DI + 2 * D:2 * DI + 2 * D + NH], start=True, stop=True,
                                 skip_group_check=True)
            last.then_inc(dt_ps, 1)
            pe.wait_ge(prep, PREP)
            pe.wait_ge(prep_act, PREP_ACT)
            pe.wait_ge(oe_in, 16)
            pe.wait_ge(soft, 1)

            def slot(r, u, a, b, c, more):
                t = 2 * r + u
                r1 = r + u
                if c:
                    b_oat(t - 2)
                if b:
                    b_gates(t - 1, 1 - u)
                for k in range(HP):
                    if b:
                        b_qk(t - 1, 1 - u, k)
                    if a and k == 1:
                        a_z(t, u)
                for e in range(NE):
                    if b:
                        b_values(t - 1, 1 - u, e)
                    if c and e == 0:
                        b_x2t(t - 2, u, b)
                    if c and e == 1:
                        c_qk(t - 2, u)
                    if a and e in (1, 2):
                        a_seg(t, e - 1)
                    if a and e == 3:
                        a_xt(t)
                    if a and e == 5:
                        a_bg(t)
                    if a and e == 7:
                        a_state(t)
                    if c and e == 2:
                        c_v(t - 2, u)
                    if c and e == 4:
                        c_rot(t - 2)
                    if c and e == 6:
                        c_krt(t - 2)
                if b:
                    b_oht(t - 1)
                    b_scores(t - 1, 0)
                    b_scores(t - 1, 1)
                for h in range(HB):
                    if b and h < HB - 2:
                        b_scores(t - 1, h + 2)
                    if c and h == 0:
                        c_kv(t - 2)
                    if a and h == 1:
                        a_inter(t)
                    if a and h == 3:
                        a_y(t)
                    if more and h == 5:
                        a_xbc(t + 1, 1 - u, r1, 0)
                    if c and h == 3:
                        c_out(t - 2)
                    if b:
                        b_turn(t - 1, h)
                        if h >= 1:
                            b_pv(t - 1, h - 1)
                if b:
                    b_pv(t - 1, HB - 1)
                if more:
                    a_xbc(t + 1, 1 - u, r1, 1)
                if a:
                    a_yt(t, more)
                if b:
                    b_mask(t - 1, 0)
                    b_ot(t - 1)
                for e in range(NE):
                    if b and e < NE - 1:
                        b_mask(t - 1, e + 1)
                    if b:
                        b_out(t - 1, e)
                    if a and e == 0:
                        a_op(t)
                    if c and e == 2:
                        c_x3t(t - 2)
                    if a and e == 6:
                        a_x1t(t, u)

            for half in range(2):
                a_xbc(0, 0, 0, half)
            slot(0, 0, True, False, False, True)
            slot(0, 1, True, True, False, True)
            with pe.Fori(1, NB // 2 - 1) as pair:
                for u in range(2):
                    slot(pair, u, True, True, True, True)
            slot(NB // 2 - 1, 0, True, True, True, True)
            slot(NB // 2 - 1, 1, True, True, True, False)
            slot(NB // 2, 0, False, True, True, False)
            slot(NB // 2, 1, False, False, True, False)

        @block.scalar
        def _(act):
            def copy(dst, src):
                return nc.scalar.activation(dst, src, ACT.Copy)

            def a_cin(b, half):
                wait(act, q["a_xbc_ps"], 2 * b + half + 1)
                wait(act, q["a_conv"], NCH * TAPS * b)
                copy(cin[:, 2 * half:2 * half + 2, TAPS - 1:], ps_a[:].rearrange("p (j n) -> p j n", j=2)
                     ).then_inc(q["a_cin"], 1)

            def a_tz(b):
                wait(act, q["a_z_ps"], b + 1)
                wait(act, q["a_sz"], b)
                nc.scalar.activation(tz[:].rearrange("p c n -> p (c n)"), ps_a[:], ACT.Tanh, scale=0.5
                                     ).then_inc(q["a_tz"], 1)

            def a_th(b):
                wait(act, q["a_conv"], NCH * TAPS * (b + 1))
                wait(act, q["a_y_ps"], b)
                nc.scalar.activation(xbc[:], cacc[:], ACT.Tanh).then_inc(q["a_th"], 1)

            def a_lx(b, c):
                wait(act, q["a_seg_ps"], C * b + c + 1)
                wait(act, q["a_mx"], C * b)
                wait(act, q["a_xst"], b)
                nc.scalar.activation(lx[:, c, :, :].rearrange("p h t -> p (h t)"), ps_a[:], ACT.Exp
                                     ).then_inc(q["a_lx"], 1)

            def a_btok(b):
                wait(act, q["a_bg_ps"], b + 1)
                wait(act, q["a_st_ps"], b)
                copy(btok[:], ps_a[:, 0:P]).then_inc(q["a_btok"], 1)
                wait(act, q["a_int"], 2 * b)
                nc.scalar.activation(ep[:], ps_a[:, 3 * P:3 * P + NH], ACT.Exp).then_inc(q["a_ep"], 1)

            def a_st(b):
                wait(act, q["a_st_ps"], b + 1)
                wait(act, q["a_int_ps"], b)
                copy(st[:], ps_a[:, 0:DI]).then_inc(q["a_st"], 1)

            def a_sq(b):
                wait(act, q["a_yg"], b + 1)
                for c in range(C):
                    if c == 1:
                        wait(act, q["a_sq"], C * b + 1)
                    nc.scalar.activation(sq[:], yg[:, c, :], ACT.Square, scale=0.5, accum_out=ssq[:, c:c + 1]
                                         ).then_inc(q["a_sq"], 1)

            def a_yt(b):
                wait(act, q["a_yt_ps"], b + 1)
                wait(act, q["a_op_ps"], b)
                copy(yT[:].rearrange("p j n -> p (j n)"), ps_a[:]).then_inc(q["a_yt"], 1)

            def a_x1h(b, u):
                wait(act, q["a_x1t_ps"], b + 1)
                wait(act, q["b_v_ps"], NE * (b - 1))
                copy(x1H[:, u, :], ps_a[:, 0:L]).then_inc(q["a_x1h"], 1)

            def b_eg(b):
                wait(act, q["b_g_ps"], b + 1)
                wait(act, q["b_gate"], 7 * b)
                nc.scalar.activation(eg[:].rearrange("p c h e -> p (c h e)"), ps_o[:, 1, 0:P], ACT.Exp, scale=-1.0
                                     ).then_inc(q["b_eg"], 1)

            def b_qk(b, hp):
                wait(act, q["b_qk_ps"], HP * b + hp + 1)
                wait(act, q["b_s_ps"], HB * b)
                copy(qk[:, hp, :, :].rearrange("p a n -> p (a n)"), ps_v[hp // 2][:, hp % 2, :]
                     ).then_inc(q["b_qk"], 1)

            def b_v0(b):
                wait(act, q["b_v_ps"], NE * b + 1)
                wait(act, q["b_pv"], HB * b)
                copy(vals[:].rearrange("p c h k -> p c (h k)"), ps_v[0][:]).then_inc(q["b_v0"], 1)

            def b_oht(b):
                wait(act, q["b_oht_ps"], b + 1)
                wait(act, q["b_m_ps"], NE * b)
                copy(ohT[:], ps_o[:, 1, P:2 * P]).then_inc(q["b_oht"], 1)

            def b_probs(b, h):
                wait(act, q["b_max"], 3 * HB * b + 3 * h + 3)
                if h >= 2:
                    wait(act, q["b_pt_ps"], HB * b + h - 1)
                else:
                    wait(act, q["b_rg"], 2 * b)
                sc = ps_s[h % SCB]
                nc.scalar.activation(pr[:, h % 2, 0, :], sc[:, 0:P], ACT.Exp, bias=n3[:, h % SCB, 0:1], scale=SCALE,
                                     accum_out=rs[:, 0, h:h + 1]).then_inc(q["b_p"], 1)
                nc.scalar.activation(pr[:, h % 2, 1:3, :].rearrange("p a b -> p (a b)"), sc[:, P:3 * P], ACT.Exp,
                                     bias=n3[:, h % SCB, 1:2], scale=SCALE,
                                     accum_out=rs[:, 1, h:h + 1]).then_inc(q["b_p"], 1)

            def b_pt(b, h):
                wait(act, q["b_pt_ps"], HB * b + h + 1)
                if h >= 2:
                    wait(act, q["b_pv"], HB * b + h - 1)
                copy(pt[:, h % 2, :, :].rearrange("p a b -> p (a b)"), ps_v[1][:, 1, 0:3 * P]
                     ).then_inc(q["b_pt"], 1)

            def b_ot(b):
                wait(act, q["b_ot_ps"], b + 1)
                wait(act, q["b_mo"], NE * b)
                copy(oT[:].rearrange("p (a b) n -> p a (b n)", a=2), ps_v[0][:]).then_inc(q["b_ot"], 1)

            def b_oa(b):
                wait(act, q["b_oe"], NE * (b + 1))
                copy(oa[:], ps_o[:, 0, 0:L]).then_inc(q["b_oa"], 1)

            def b_x2t(b, u):
                wait(act, q["b_x2t_ps"], b + 1)
                copy(x2T[:, u, :], ps_o[:, 1, L:2 * L]).then_inc(q["b_x2t"], 1)

            def c_gelu(b):
                wait(act, q["c_qk_ps"], b + 1)
                wait(act, q["c_q"], b)
                wait(act, q["c_km"], 2 * b)
                nc.scalar.activation(gl[:, 0, :], ps_c[:, 0:L], ACT.Gelu, bias=bq_s[:]).then_inc(q["c_g"], 1)
                nc.scalar.activation(gl[:, 1, :], ps_c[:, L:2 * L], ACT.Gelu, bias=bk_s[:],
                                     accum_out=ks[:]).then_inc(q["c_g"], 1)

            def c_kr(b):
                wait(act, q["c_krt_ps"], b + 1)
                copy(kr[:].rearrange("p c d -> p (c d)"), ps_c[:, 0:L]).then_inc(q["c_kr"], 1)

            def c_x3t(b):
                wait(act, q["c_x3t_ps"], b + 1)
                wait(act, x3_stored, 32 * b)
                copy(x3T[:], ps_c[:, 0:L]).then_inc(q["c_x3t"], 1)

            act.wait_ge(ready, READY)
            copy(wqH[:], wq_f[:]).then_inc(prep_act, 1)
            copy(wkH[:], wk_f[:]).then_inc(prep_act, 1)
            copy(wgH[:], wg_f[:]).then_inc(prep_act, 1)
            copy(veH[:].rearrange("p e n -> p (e n)"), ve_f[:]).then_inc(prep_act, 1)
            nc.scalar.activation(ea[:], alog[:], ACT.Exp).then_inc(prep_act, 1)
            act.wait_ge(soft, 2)
            nc.scalar.activation(su[:], sa[:], ACT.Exp, scale=-1.0).then_inc(soft_act, 1)

            def slot(r, u, a, b, c, more):
                t = 2 * r + u
                if c:
                    b_oa(t - 2)
                if b:
                    b_eg(t - 1)
                for k in range(HP):
                    if b:
                        b_qk(t - 1, k)
                    if a and k == 1:
                        a_tz(t)
                if c:
                    b_x2t(t - 2, u)
                for e in range(NE):
                    if b and e == 0:
                        b_v0(t - 1)
                    if c and e == 0:
                        c_gelu(t - 2)
                    if a and e in (2, 3):
                        a_lx(t, e - 2)
                    if a and e == 5:
                        a_btok(t)
                    if c and e == 6:
                        c_kr(t - 2)
                if b:
                    b_oht(t - 1)
                if b:
                    b_probs(t - 1, 0)
                for h in range(HB):
                    if b and h < HB - 1:
                        b_probs(t - 1, h + 1)
                    if b:
                        b_pt(t - 1, h)
                    if a and h == 0:
                        a_st(t)
                    if more and h == 5:
                        a_cin(t + 1, 0)
                    if a and h == 6:
                        a_sq(t)
                if more:
                    a_cin(t + 1, 1)
                if a:
                    a_yt(t)
                if b:
                    b_ot(t - 1)
                if c:
                    c_x3t(t - 2)
                if more:
                    a_th(t + 1)
                if a:
                    a_x1h(t, u)

            for half in range(2):
                a_cin(0, half)
            a_th(0)
            slot(0, 0, True, False, False, True)
            slot(0, 1, True, True, False, True)
            with act.Fori(1, NB // 2 - 1) as pair:
                for u in range(2):
                    slot(pair, u, True, True, True, True)
            slot(NB // 2 - 1, 0, True, True, True, True)
            slot(NB // 2 - 1, 1, True, True, True, False)
            slot(NB // 2, 0, False, True, True, False)
            slot(NB // 2, 1, False, False, True, False)

        @block.vector
        def _(dve):
            V = nc.vector

            def a_steps(b):
                wait_apart(dve, (q["a_xd"], 2 * b), (q["a_bg_ps"], b), (q["a_am"], C * b))
                V.tensor_copy(dt_b[:], dt_all[:, bass.ds(b * C, C), :]).then_inc(q["a_step"], 1)
                V.tensor_copy(a_b[:], a_all[:, bass.ds(b * C, C), :]).then_inc(q["a_step"], 1)

            def a_conv(b, half, taps=range(TAPS)):
                if half == 0:
                    wait(dve, q["a_th"], b)
                    wait(dve, q["a_xbc"], b)
                wait(dve, q["a_cin"], 2 * b + half + 1)
                n0 = NCH * TAPS * b + 2 * TAPS * half
                for k in taps:
                    for j in range(2):
                        ch = 2 * half + j
                        tap = TAPS - 1 - k
                        if k == 0:
                            ins = V.tensor_scalar(cacc[:, ch, :], cin[:, ch, tap:tap + L], cw[:, ch, tap:tap + 1],
                                                  cb[:, ch:ch + 1], ALU.mult, ALU.add)
                        else:
                            wait(dve, q["a_conv"], n0 + 2 * (k - 1) + j + 1)
                            ins = V.scalar_tensor_tensor(cacc[:, ch, :], cin[:, ch, tap:tap + L],
                                                         cw[:, ch, tap:tap + 1], cacc[:, ch, :], ALU.mult, ALU.add)
                        ins.then_inc(q["a_conv"], 1)

            def a_sz(b):
                wait(dve, q["a_tz"], b + 1)
                wait(dve, q["a_yg"], b)
                V.scalar_tensor_tensor(sz[:].rearrange("p c n -> p (c n)"), tz[:].rearrange("p c n -> p (c n)"), 1.0,
                                       ps_a[:], ALU.add, ALU.mult).then_inc(q["a_sz"], 1)

            def a_xbc(b):
                wait(dve, q["a_th"], b + 1)
                V.scalar_tensor_tensor(xbc[:], xbc[:], 1.0, cacc[:], ALU.add, ALU.mult).then_inc(q["a_xbc"], 1)

            def a_xd(b):
                wait(dve, q["a_xt_ps"], b + 1)
                wait(dve, q["a_step"], 2 * (b + 1))
                ps = ps_a[:].rearrange("p (c h d) -> p c h d", c=C, h=NH)
                V.tensor_tensor(xd[:], ps, dt_b[:].unsqueeze(3).to_broadcast([P, C, NH, HD]), ALU.mult
                                ).then_inc(q["a_xd"], 1)
                V.tensor_tensor(xD[:], ps, d_h[:].unsqueeze(1).unsqueeze(3).to_broadcast([P, C, NH, HD]), ALU.mult
                                ).then_inc(q["a_xd"], 1)

            def a_xst(b):
                wait(dve, q["a_lx"], C * b + 1)
                wait(dve, q["a_xd"], 2 * b + 2)
                wait(dve, q["a_st_ps"], b)
                V.tensor_tensor(xst[:], xd[:, 0, :, :], lx[:, 0, :, P - 1:P].to_broadcast([P, NH, HD]), ALU.mult
                                ).then_inc(q["a_xst"], 1)

            def a_gm(b):
                wait(dve, q["a_ep"], b + 1)
                wait(dve, q["a_mx"], C * b)
                V.tensor_tensor(gm[:], ps_a[:, P:3 * P].rearrange("p (c t) -> p c t", c=C),
                                causal_s[:].unsqueeze(1).to_broadcast([P, C, P]), ALU.mult).then_inc(q["a_gm"], 1)

            def a_mx(b):
                wait(dve, q["a_gm"], b + 1)
                wait(dve, q["a_lx"], C * (b + 1))
                wait(dve, q["a_y_ps"], b)
                for c in range(C):
                    V.tensor_tensor(mx[:, c, :, :], lx[:, c, :, :], gm[:, c, :].unsqueeze(1).to_broadcast([P, NH, P]),
                                    ALU.mult).then_inc(q["a_mx"], 1)

            def a_int(b):
                wait(dve, q["a_int_ps"], b + 1)
                wait(dve, q["a_ep"], b + 1)
                V.tensor_tensor(inter[:], ps_a[:, DI:2 * DI].rearrange("p (h d) -> p h d", h=NH),
                                ep[:].unsqueeze(2).to_broadcast([P, NH, HD]), ALU.mult).then_inc(q["a_int"], 1)
                wait(dve, q["a_int"], 2 * b + 1)
                V.tensor_tensor(xD[:, 1, :, :], xD[:, 1, :, :], inter[:], ALU.add).then_inc(q["a_int"], 1)

            def a_y(b):
                wait(dve, q["a_y_ps"], b + 1)
                wait(dve, q["a_int"], 2 * b + 2)
                V.tensor_tensor(ya[:].rearrange("p c n -> p (c n)"), ps_a[:], xD[:].rearrange("p c h d -> p (c h d)"),
                                ALU.add).then_inc(q["a_y"], 1)
                wait(dve, q["a_y"], b + 1)
                wait(dve, q["a_sq"], C * b)
                wait(dve, q["a_yt_ps"], b)
                V.tensor_tensor(yg[:], ya[:], sz[:], ALU.mult).then_inc(q["a_yg"], 1)

            def a_res(b, u):
                V_r = rstd_of("rms")
                wait(dve, norms["rms"]["rstd"], RSQRT_OPS * (b + 1))
                wait(dve, q["a_op_ps"], b + 1)
                V.tensor_scalar(V_r[:], V_r[:], 0.5, None, ALU.mult).then_inc(norms["rms"]["rows"], 1)
                wait(dve, norms["rms"]["rows"], b + 1)
                for c in range(C):
                    V.scalar_tensor_tensor(ra[:, c, :], ps_a[:, c * D:(c + 1) * D], V_r[:, c:c + 1], x_in[:, u, c, :],
                                           ALU.mult, ALU.add).then_inc(q["a_r"], 1)
                wait(dve, q["a_r"], C * (b + 1))
                stats(dve, "ln1", ra, b)
                V.tensor_tensor(xb[:], x_in[:, u, :, :], lnb[:].unsqueeze(1).to_broadcast([P, C, D]), ALU.add
                                ).then_inc(q["a_xb"], 1)

            def a_ln1(b):
                scale_rows(dve, "ln1", ra, na, b)
                wait(dve, norms["ln1"]["rows"], C * (b + 1))
                V.tensor_tensor(na[:], na[:], lnw[:].unsqueeze(1).to_broadcast([P, C, D]), ALU.mult
                                ).then_inc(q["a_n"], 1)
                wait(dve, q["a_n"], 2 * b + 1)
                wait(dve, q["a_xb"], b + 1)
                V.tensor_tensor(na[:], na[:], xb[:], ALU.add).then_inc(q["a_n"], 1)
                wait(dve, q["a_n"], 2 * b + 2)
                stats(dve, "ln2", na, b)

            def a_ln2(b, u):
                wait(dve, norms["lnB"]["rows"], C * (b - 1))
                wait(dve, norms["ln2"]["rstd"], RSQRT_OPS * (b + 1))
                for c in range(C):
                    ins = V.tensor_scalar(x1[:, u, c, :], na[:, c, :], nbuf["ln2"][1][:, c, 0:1],
                                          rstd_of("ln2")[:, c:c + 1], ALU.subtract, ALU.mult)
                ins.then_inc(q["a_x1"], 1)

            def a_x1l(b, u):
                wait(dve, q["a_x1h"], b + 1)
                V.tensor_tensor(x1L[:, u, :], ps_a[:, 0:L], x1H[:, u, :].bitcast(F32), ALU.subtract
                                ).then_inc(q["a_x1l"], 1)

            def b_gate(b):
                k = 7 * b
                n = q["b_gate"]
                wait(dve, q["b_eg"], b + 1)
                V.tensor_scalar(eg[:], eg[:], 1.0, None, ALU.add).then_inc(n, 1)
                wait(dve, n, k + 1)
                V.reciprocal(g[:], eg[:]).then_inc(n, 1)
                wait(dve, n, k + 2)
                V.tensor_reduce(gx[:], g[:], AX.X, ALU.max).then_inc(n, 1)
                wait(dve, n, k + 3)
                V.tensor_tensor(geq[:], g[:], gx[:].unsqueeze(3).to_broadcast([P, C, HB, NE]), ALU.is_equal
                                ).then_inc(n, 1)
                wait(dve, n, k + 4)
                V.tensor_tensor(geq[:], geq[:], w8_s[:].unsqueeze(1).unsqueeze(1).to_broadcast([P, C, HB, NE]),
                                ALU.mult).then_inc(n, 1)
                wait(dve, n, k + 5)
                V.tensor_reduce(g2[:], geq[:], AX.X, ALU.max).then_inc(n, 1)
                wait(dve, n, k + 6)
                V.tensor_tensor(oh[:], geq[:], g2[:].unsqueeze(3).to_broadcast([P, C, HB, NE]), ALU.is_equal
                                ).then_inc(n, 1)

            def b_v(b, e):
                if e == 1:
                    wait_apart(dve, (q["b_v_ps"], NE * b + 2), (q["b_v0"], b + 1), (q["b_gate"], 7 * b + 7))
                else:
                    wait_apart(dve, (q["b_v_ps"], NE * b + e + 1), (q["b_v"], (NE - 1) * b + e - 1))
                for c in range(C):
                    ins = V.copy_predicated(vals[:, c, :, :],
                                            oh[:, c, :, e:e + 1].bitcast(I32).to_broadcast([P, HB, DH]),
                                            ps_v[e % 2][:, c, :].rearrange("p (h k) -> p h k", h=HB))
                ins.then_inc(q["b_v"], 1)

            def b_vg(b):
                wait(dve, q["b_v"], (NE - 1) * (b + 1))
                for c in range(C):
                    V.tensor_tensor(vals[:, c, :, :], vals[:, c, :, :],
                                    gx[:, c, :].unsqueeze(2).to_broadcast([P, HB, DH]), ALU.mult
                                    ).then_inc(q["b_vg"], 1)

            def b_max(b, h):
                n, k = q["b_max"], 3 * HB * b + 3 * h
                wait(dve, q["b_s_ps"], HB * b + h + 1)
                if h >= SCB:
                    wait(dve, q["b_p"], 2 * HB * b + 2 * (h - SCB + 1))
                V.tensor_reduce(r3[:, h % SCB, :], ps_s[h % SCB][:, 0:3 * P].rearrange("p (a b) -> p a b", a=3),
                                AX.X, ALU.max).then_inc(n, 1)
                wait(dve, n, k + 1)
                V.tensor_scalar(n3[:, h % SCB, :], r3[:, h % SCB, :], -SCALE, None, ALU.mult).then_inc(n, 1)
                wait(dve, n, k + 2)
                V.tensor_tensor(n3[:, h % SCB, 1:2], n3[:, h % SCB, 1:2], n3[:, h % SCB, 2:3], ALU.min).then_inc(n, 1)

            def b_on(b):
                wait(dve, q["b_p"], 2 * HB * (b + 1))
                V.reciprocal(rg[:], rs[:]).then_inc(q["b_rg"], 1)
                wait(dve, q["b_rg"], 2 * b + 1)
                V.tensor_tensor(rg[:], rg[:], gx[:], ALU.mult).then_inc(q["b_rg"], 1)
                wait(dve, q["b_rg"], 2 * b + 2)
                wait(dve, q["b_pv"], HB * (b + 1))
                for c in range(C):
                    V.tensor_tensor(on[:, c, :].rearrange("p (h k) -> p h k", h=HB),
                                    ps_o[:, c, :].rearrange("p (h k) -> p h k", h=HB),
                                    rg[:, c, :].unsqueeze(2).to_broadcast([P, HB, DH]), ALU.mult
                                    ).then_inc(q["b_on"], 1)

            def b_mo(b, e):
                wait(dve, q["b_m_ps"], NE * b + e + 1)
                if e == 0:
                    wait(dve, q["b_ot"], b + 1)
                    wait(dve, q["b_oe"], NE * b)
                elif e >= 2:
                    wait(dve, q["b_oe"], NE * b + e - 1)
                V.tensor_tensor(mo[:, e % 2, :, :].rearrange("p a (c n) -> p c a n", c=C),
                                oT[:].rearrange("p a (c n) -> p c a n", c=C),
                                ps_v[(e + 1) % 2][:].rearrange("p c (a n) -> p c a n", a=HP), ALU.mult
                                ).then_inc(q["b_mo"], 1)

            def b_res(b, u):
                wait(dve, q["b_oat_ps"], b + 1)
                V.tensor_tensor(rb[:].rearrange("p c d -> p (c d)"), ps_o[:, 1, 0:L],
                                x1[:, u, :, :].rearrange("p c d -> p (c d)"), ALU.add).then_inc(q["b_r"], 1)
                wait(dve, q["b_r"], b + 1)
                stats(dve, "lnB", rb, b)

            def b_x2(b, u):
                scale_rows(dve, "lnB", rb, x2[:, u, :, :], b)

            def c_q(b):
                wait(dve, q["c_g"], 2 * (b + 1))
                wait(dve, q["c_out_ps"], b)
                V.tensor_scalar(ql[:], gl[:], SHIFT, None, ALU.add).then_inc(q["c_q"], 1)

            def c_v(b):
                wait(dve, q["c_v_ps"], b + 1)
                wait(dve, q["c_kv_ps"], b)
                V.tensor_tensor(vl[:], ps_c[:, 0:L].rearrange("p (c d) -> p c d", c=C),
                                bv_s[:].unsqueeze(1).to_broadcast([P, C, D]), ALU.add).then_inc(q["c_v"], 1)

            def c_qr(b):
                n, k = q["c_qr"], 3 * b
                wait(dve, q["c_q"], b + 1)
                V.tensor_tensor(t2[:], ql[:], cos_s[:].unsqueeze(1).to_broadcast([P, 2, L]), ALU.mult).then_inc(n, 1)
                wait(dve, q["c_rot_ps"], b + 1)
                V.tensor_tensor(t1[:], ps_c[:].rearrange("p (a n) -> p a n", a=2),
                                sin_s[:].unsqueeze(1).to_broadcast([P, 2, L]), ALU.mult).then_inc(n, 1)
                wait(dve, n, k + 2)
                wait(dve, q["c_out_ps"], b)
                V.tensor_tensor(qr[:], t1[:], t2[:], ALU.add).then_inc(n, 1)

            def c_kv(b):
                wait(dve, q["c_kv_ps"], b + 1)
                wait(dve, q["c_out_ps"], b)
                V.tensor_tensor(kv[:], ps_c[:, L:L + D], hof_n[:], ALU.mult).then_inc(q["c_kv"], 1)

            def c_res(b, u):
                wait(dve, q["c_out_ps"], b + 1)
                V.tensor_scalar(zd[:].rearrange("p c h -> p (c h)"), ps_c[:, 2 * D:2 * D + C * HL], 1e-6, None, ALU.add
                                ).then_inc(q["c_z"], 1)
                wait(dve, q["c_z"], 2 * b + 1)
                V.reciprocal(zr[:], zd[:]).then_inc(q["c_z"], 1)
                wait(dve, q["c_z"], 2 * b + 2)
                V.tensor_tensor(rc[:], ps_c[:, 0:L].rearrange("p (c h e) -> p c h e", c=C, h=HL),
                                zr[:].unsqueeze(3).to_broadcast([P, C, HL, WL]), ALU.mult).then_inc(q["c_res"], 1)
                wait(dve, q["c_res"], 2 * b + 1)
                V.tensor_tensor(rc2[:], rc[:].rearrange("p c h e -> p c (h e)"), x2[:, u, :, :], ALU.add
                                ).then_inc(q["c_res"], 1)
                wait(dve, q["c_res"], 2 * b + 2)
                stats(dve, "lnC", rc2, b)
                V.tensor_tensor(xc[:], x2[:, u, :, :], bet[:].unsqueeze(1).to_broadcast([P, C, D]), ALU.add
                                ).then_inc(q["c_n"], 1)

            def c_ln(b):
                scale_rows(dve, "lnC", rc2, ncn, b)
                wait(dve, norms["lnC"]["rows"], C * (b + 1))
                V.tensor_tensor(n2[:], ncn[:], gam[:].unsqueeze(1).to_broadcast([P, C, D]), ALU.mult
                                ).then_inc(q["c_n"], 1)
                wait(dve, q["c_n"], 3 * b + 2)
                V.tensor_tensor(n2[:], n2[:], xc[:], ALU.add).then_inc(q["c_n"], 1)
                wait(dve, q["c_n"], 3 * b + 3)
                stats(dve, "lnD", n2, b)

            def c_x3(b):
                wait(dve, norms["lnD"]["rstd"], RSQRT_OPS * (b + 1))
                wait(dve, x3_stored, 32 * b)
                for c in range(C):
                    ins = V.tensor_scalar(x3[:, c, :], n2[:, c, :], nbuf["lnD"][1][:, c, 0:1],
                                          rstd_of("lnD")[:, c:c + 1], ALU.subtract, ALU.mult)
                ins.then_inc(q["c_x3"], 1)

            dve.wait_ge(ready, READY)
            V.tensor_copy(id_b[:], id_f[:]).then_inc(prep, 1)
            V.tensor_copy(negb[:], negb_f[:]).then_inc(prep, 1)
            V.tensor_scalar(hof_n[:], hof[:], 1.0 / L, None, ALU.mult).then_inc(prep, 1)
            V.tensor_copy(h16[:], hof[:].rearrange("p (h e) -> p h e", h=HL)[:, :, 0]).then_inc(prep, 1)
            V.tensor_scalar(cw[:], cw0[:], 0.5, None, ALU.mult).then_inc(prep, 1)
            V.tensor_scalar(cb[:], cb0[:], 0.5, None, ALU.mult).then_inc(prep, 1)
            for j in range(2):
                V.tensor_scalar(out_w[:, j, :], out_w0[:, j, :], nw[:, j:j + 1], None, ALU.mult).then_inc(prep, 1)
            V.memset(cin[:, :, 0:TAPS - 1], 0.0).then_inc(prep, 1)
            V.tensor_tensor(idfold[:], id_f[:, 0:64], id_f[:, 64:128], ALU.add).then_inc(prep, 1)
            dve.wait_ge(prep, 10)
            for hp in range(HP):
                ins = V.tensor_copy(pick[:, hp, :, :, :],
                                    idfold[:, 2 * hp * NE:2 * (hp + 1) * NE].rearrange("p (a e) -> p e a", a=2)
                                    .unsqueeze(3).to_broadcast([P, NE, 2, DH]))
            ins.then_inc(prep, 1)
            for n, (lo, full, hi) in enumerate(((wqL, wq_f, wqH), (wkL, wk_f, wkH), (wgL, wg_f, wgH))):
                dve.wait_ge(prep_act, n + 1)
                V.tensor_tensor(lo[:], full[:], hi[:].bitcast(F32), ALU.subtract).then_inc(prep, 1)
            dve.wait_ge(prep_act, 4)
            V.tensor_tensor(veL[:].rearrange("p e n -> p (e n)"), ve_f[:],
                            veH[:].rearrange("p e n -> p (e n)").bitcast(F32), ALU.subtract).then_inc(prep, 1)

            dve.wait_ge(dt_ps, 1)
            V.tensor_tensor(sv[:], ps_a[:, 0:TT * NH].rearrange("p (n h) -> p n h", h=NH),
                            dtb[:].unsqueeze(1).to_broadcast([P, TT, NH]), ALU.add).then_inc(soft, 1)
            dve.wait_ge(soft, 1)
            V.scalar_tensor_tensor(sa[:], sv[:], -1.0, sv[:], ALU.mult, ALU.max).then_inc(soft, 1)
            dve.wait_ge(soft_act, 1)
            V.tensor_scalar(sd[:], su[:], 2.0, None, ALU.add).then_inc(soft, 1)
            dve.wait_ge(soft, 3)
            V.reciprocal(sd[:], sd[:]).then_inc(soft, 1)
            dve.wait_ge(soft, 4)
            V.tensor_tensor(sd[:], sd[:], su[:], ALU.mult).then_inc(soft, 1)
            dve.wait_ge(soft, 5)
            V.tensor_tensor(s2[:], sd[:], sd[:], ALU.mult).then_inc(soft, 1)
            dve.wait_ge(soft, 6)
            V.tensor_scalar(sp[:], s2[:], 1.0 / (2 * LOG1P_TERMS + 1), None, ALU.mult).then_inc(soft, 1)
            at = 7
            for k in range(LOG1P_TERMS - 1, 0, -1):
                dve.wait_ge(soft, at)
                V.scalar_tensor_tensor(sp[:], sp[:], 1.0 / (2 * k + 1), s2[:], ALU.add, ALU.mult).then_inc(soft, 1)
                at += 1
            dve.wait_ge(soft, at)
            V.scalar_tensor_tensor(sp[:], sp[:], 1.0, sd[:], ALU.add, ALU.mult).then_inc(soft, 1)
            V.tensor_scalar(sv[:], sv[:], 0.0, None, ALU.max).then_inc(soft, 1)
            dve.wait_ge(soft, at + 2)
            V.scalar_tensor_tensor(dt_all[:], sp[:], 2.0, sv[:], ALU.mult, ALU.add).then_inc(soft, 1)
            dve.wait_ge(soft, at + 3)
            dve.wait_ge(prep_act, PREP_ACT)
            V.scalar_tensor_tensor(a_all[:], dt_all[:], -1.0, ea[:].unsqueeze(1).to_broadcast([P, TT, NH]),
                                   ALU.mult, ALU.mult).then_inc(soft, 1)
            dve.wait_ge(soft, at + 4)

            def slot(r, u, a, b, c, more):
                t = 2 * r + u
                if c:
                    b_res(t - 2, u)
                if a:
                    a_steps(t)
                if b:
                    b_gate(t - 1)
                if a:
                    a_sz(t)
                if c:
                    b_x2(t - 2, u)
                for e in range(NE):
                    if b and e >= 1:
                        b_v(t - 1, e)
                    if a and e == 4:
                        a_xd(t)
                        a_xst(t)
                    if a and e == 6:
                        a_gm(t)
                    if c and e == 1:
                        c_q(t - 2)
                    if c and e == 3:
                        c_v(t - 2)
                    if c and e == 5:
                        c_qr(t - 2)
                if b:
                    b_max(t - 1, 0)
                    b_vg(t - 1)
                    b_max(t - 1, 1)
                for h in range(HB):
                    if b and h < HB - 2:
                        b_max(t - 1, h + 2)
                    if a and h == 0:
                        a_mx(t)
                    if c and h == 0:
                        c_kv(t - 2)
                    if a and h == 1:
                        a_int(t)
                    if c and h == 3:
                        c_res(t - 2, u)
                    if a and h == 4:
                        a_y(t)
                    if c and h == 5:
                        c_ln(t - 2)
                    if more and h == 7:
                        a_conv(t + 1, 0)
                if b:
                    b_on(t - 1)
                for e in range(NE):
                    if b:
                        b_mo(t - 1, e)
                    if c and e == 0:
                        c_x3(t - 2)
                    if a and e == 1:
                        a_res(t, u)
                    if a and e == 2:
                        a_ln1(t)
                    if more and e == 3:
                        a_conv(t + 1, 1, (0, 1))
                    if more and e == 4:
                        a_conv(t + 1, 1, (2, 3))
                    if a and e == 5:
                        a_ln2(t, u)
                if a:
                    a_x1l(t, u)
                if more:
                    a_xbc(t + 1)

            for half in range(2):
                a_conv(0, half)
            a_xbc(0)
            slot(0, 0, True, False, False, True)
            slot(0, 1, True, True, False, True)
            with dve.Fori(1, NB // 2 - 1) as pair:
                for u in range(2):
                    slot(pair, u, True, True, True, True)
            slot(NB // 2 - 1, 0, True, True, True, True)
            slot(NB // 2 - 1, 1, True, True, True, False)
            slot(NB // 2, 0, False, True, True, False)
            slot(NB // 2, 1, False, False, True, False)

        @block.gpsimd
        def _(pool):
            G = nc.gpsimd

            def a_am(b):
                for c in range(C):
                    wait_apart(pool, (q["a_step"], 2 * (b + 1)), (q["a_seg_ps"], C * b))
                    G.affine_select(out=am[:, c, :, :], in_=a_b[:, c, :].unsqueeze(2).to_broadcast([P, NH, P]),
                                    compare_op=ALU.is_ge, fill=0.0, base=0, pattern=[[0, NH], [1, P]],
                                    channel_multiplier=-1).then_inc(q["a_am"], 1)

            def c_km(b):
                wait_apart(pool, (q["c_g"], 2 * (b + 1)), (q["c_out_ps"], b))
                G.tensor_scalar(km[:], ks[:], 1.0 / L, SHIFT, ALU.mult, ALU.add).then_inc(q["c_km"], 1)
                wait_apart(pool, (q["c_km"], 2 * b + 1))
                G.tensor_scalar(kmh[:], h16[:], km[:], None, ALU.mult).then_inc(q["c_km"], 1)

            pool.wait_ge(ready, READY)
            pool.wait_ge(prep, PREP)

            def slot(r, u, a, b, c):
                t = 2 * r + u
                if c:
                    rsqrt(pool, "lnB", t - 2, 1.0, EPS, norms["lnB"]["moments"], 2 * C)
                if a:
                    a_am(t)
                if c:
                    c_km(t - 2)
                    rsqrt(pool, "lnC", t - 2, 1.0, 1e-12, norms["lnC"]["moments"], 2 * C)
                    rsqrt(pool, "lnD", t - 2, 1.0, EPS, norms["lnD"]["moments"], 2 * C)
                if a:
                    rsqrt(pool, "rms", t, 1.0 / DI, EPS, q["a_sq"], C)
                    rsqrt(pool, "ln1", t, 1.0, EPS, norms["ln1"]["moments"], 2 * C)
                    rsqrt(pool, "ln2", t, 1.0, EPS, norms["ln2"]["moments"], 2 * C)

            slot(0, 0, True, False, False)
            slot(0, 1, True, True, False)
            with pool.Fori(1, NB // 2) as pair:
                for u in range(2):
                    slot(pair, u, True, True, True)
            slot(NB // 2, 0, False, True, True)
            slot(NB // 2, 1, False, False, True)


def soft_experts(nc, kept, x3_dram, x3T_dram, x3_stored, phi, W, b_exp, ident, out):
    y_dram = nc.dram_tensor("y_slots", (SB * NS, NB * XB * D), F32, kind="Internal").ap()
    y_stored = [kept.enter_context(nc.semaphore(f"y_stored{u}")) for u in range(2)]
    with ExitStack() as ctx:
        dispatch(nc, ctx, kept, x3_dram, x3T_dram, phi, W, b_exp, ident, y_dram, y_stored)
    with ExitStack() as ctx:
        combine(nc, ctx, kept, x3_dram, x3T_dram, phi, ident, y_dram, out)


def dispatch(nc, ctx, kept, x3_dram, x3T_dram, phi, W, b_exp, ident, y_dram, y_stored):
    def sb(name, shape, dt=F32):
        return ctx.enter_context(nc.sbuf_tensor(name, [P] + shape, dt))

    def sem(name):
        return kept.enter_context(nc.semaphore(name))

    id_f = sb("d_id", [P])
    id_r = sb("d_idr", [P], F32R)
    xtf = sb("d_xtf", [NB, C, P])
    xs = sb("d_xs", [TT, D])
    phf = sb("d_phf", [S])
    w = sb("d_w", [2, XB, D])
    bx = sb("d_bx", [SB * XB * D])
    mp = sb("d_mp", [BK, P])
    mxb = sb("d_mxb", [P])
    nH = sb("d_nH", [P], F32R)
    nL = sb("d_nL", [P], F32R)
    ex = sb("d_ex", [2, C, BK, BB, P])
    sm = sb("d_sm", [P])
    sr = sb("d_sr", [P])
    slot_s = sb("d_slot", [XB, BK, BB, NS])
    ys = sb("d_ys", [2, BK, XB, D])

    lg = ctx.enter_context(nc.psum_tensor("d_lg", [P, BK, BB, P], F32))
    sl = ctx.enter_context(nc.psum_tensor("d_sl", [P, BK, BB, P], F32))

    ready = sem("d_ready")
    late = sem("d_late")
    x_in = [sem(f"d_x_in{c}") for c in range(C)]
    id_half = sem("d_id_half")
    w_in = [sem(f"d_w_in{u}") for u in range(2)]
    names = "lg_ps part max sub_ps ex sum mult slot_ps slot ys_ps ys y".split()
    q = {n: sem("d_" + n) for n in names}
    block = ctx.enter_context(nc.Block())
    READY = 16 * 2

    @block.sync
    def _(sp):
        sp.dma_start(phf[:], phi).then_inc(ready, 16)
        for c in range(C):
            sp.dma_start(xtf[:, :, c, :], x3T_dram.rearrange("p (b c t) -> p b c t", c=C, t=P)[:, :, c, :]
                         ).then_inc(x_in[c], 16)
        sp.dma_start(id_f[:], ident).then_inc(ready, 16)

        def load(s, u):
            for v in (BK * (s - 1), s * XB):
                sp.compute_val(v)
            sp.wait_ge(ready, READY)
            wait(sp, q["ys_ps"], BK * (s - 1))
            sp.dma_start(w[:, u, :, :], W[:, bass.ds(s * XB, XB), :]).then_inc(w_in[u], 16)

        def store(s, u):
            for v in (BK * (s + 1), s * NS):
                sp.compute_val(v)
            sp.wait_ge(ready, READY)
            wait(sp, q["y"], BK * (s + 1))
            for i in range(BB):
                batches = slice(i * BK * XB * D, (i + 1) * BK * XB * D)
                sp.dma_start(y_dram[bass.ds(s * NS, NS), batches],
                             ys[i * NS:(i + 1) * NS, u, :, :, :].rearrange("n k j e -> n (k j e)")
                             ).then_inc(y_stored[u], 16)

        load(0, 0)
        load(1, 1)
        sp.dma_start(xs[:], x3_dram.rearrange("(n p) d -> p n d", p=P)).then_inc(late, 16)
        sp.dma_start(bx[:], row(b_exp, S * D // NS)).then_inc(late, 16)
        with sp.Fori(1, SB // 2) as pair:
            for u in range(2):
                load(2 * pair + u, u)
                store(2 * pair + u - 2, u)
        for u in range(2):
            store(SB - 2 + u, u)
        for u in range(2):
            sp.wait_ge(y_stored[u], 16 * BB * (SB // 2))

    @block.tensor
    def _(pe):
        def logits(s, c):
            g = C * s + c
            cols = bass.ds(s * P, P)
            for k in range(BK):
                wait(pe, q["ex"], BK * (g - 1) + k + 1 if not isinstance(g, int) or g else 0)
                for i in range(BB):
                    b = BK * i + k
                    last = pe.matmul(lg[:, k, i, :], xtf[:, b, c, :], phf[:, cols], start=(i == 0), stop=False,
                                     skip_group_check=True)
                last.then_inc(q["lg_ps"], 1)

        def subtract(s, c):
            wait(pe, q["max"], 3 * (C * s + c) + 3)
            for k in range(BK):
                pe.matmul(lg[:, k, :, :], id_r[:], nH[:].unsqueeze(1).to_broadcast([P, BB, P]), start=False,
                          stop=False, skip_group_check=True)
                pe.matmul(lg[:, k, :, :], id_r[:], nL[:].unsqueeze(1).to_broadcast([P, BB, P]), start=False,
                          stop=True, skip_group_check=True).then_inc(q["sub_ps"], 1)

        def slots(s, u, c, ks):
            wait(pe, q["mult"], C * s + c + 1)
            for k in ks:
                if c == 0:
                    wait(pe, q["ys"], BK * (s - 1) + k + 1 if not isinstance(s, int) or s else 0)
                for i in range(BB):
                    last = pe.matmul(sl[:, k, i, :], xs[:, (BK * i + k) * C + c, :], ex[:, u, c, k, i, :],
                                     start=(c == 0 and i == 0), stop=(c == C - 1), skip_group_check=True)
                last.then_inc(q["slot_ps"], 1)

        def experts(s, u, r, ks):
            wait(pe, w_in[u], 16 * (r + 1))
            for k in ks:
                wait(pe, q["slot"], BK * s + k + 1)
                for j in range(XB):
                    last = pe.matmul(sl[:, k, j, :], slot_s[:, j, k, :, :], w[:, u, j, :], start=(j == 0), stop=True,
                                     skip_group_check=True)
                last.then_inc(q["ys_ps"], 1)

        def block_of(r, u):
            s = 2 * r + u
            known = isinstance(s, int)
            logits(s, 0)
            if not known or s >= 2:
                experts(s - 2, u, r - 1, (0, 1))
                slots(s - 2, u, 1, (2, 3))
            subtract(s, 0)
            if not known or s >= 2:
                experts(s - 2, u, r - 1, (2, 3))
            if not known or s >= 1:
                slots(s - 1, 1 - u, 0, (0, 1))
            if known and s == 0:
                pe.wait_ge(x_in[1], 16)
            logits(s, 1)
            if not known or s >= 1:
                slots(s - 1, 1 - u, 0, (2, 3))
            subtract(s, 1)
            if not known or s >= 1:
                slots(s - 1, 1 - u, 1, (0, 1))

        pe.wait_ge(ready, READY)
        pe.wait_ge(id_half, 1)
        pe.wait_ge(x_in[0], 16)
        block_of(0, 0)
        pe.wait_ge(late, 32)
        block_of(0, 1)
        with pe.Fori(1, SB // 2) as pair:
            for u in range(2):
                block_of(pair, u)
        r = SB // 2 - 1
        experts(SB - 2, 0, r, (0, 1))
        slots(SB - 2, 0, 1, (2, 3))
        experts(SB - 2, 0, r, (2, 3))
        slots(SB - 1, 1, 0, range(BK))
        slots(SB - 1, 1, 1, range(BK))
        experts(SB - 1, 1, r, range(BK))

    @block.scalar
    def _(act):
        def exps(s, u, c):
            g = C * s + c
            for k in range(BK):
                wait(act, q["sub_ps"], BK * g + k + 1)
                if k == 0:
                    wait(act, q["slot_ps"], BK * (g - 3) if not isinstance(s, int) or s >= 2 else 0)
                nc.scalar.activation(ex[:, u, c, k, :, :], lg[:, k, :, :], ACT.Exp).then_inc(q["ex"], 1)

        def slots(s, ks):
            for k in ks:
                wait(act, q["slot_ps"], BK * (C * s + 1) + k + 1)
                wait(act, q["ys_ps"], BK * (s - 1) + k + 1 if not isinstance(s, int) or s else 0)
                nc.scalar.activation(slot_s[:, :, k, :, :], sl[:, k, :, :].rearrange("p b (j n) -> p j b n", j=XB),
                                     ACT.Copy).then_inc(q["slot"], 1)

        def outputs(s, u, r, ks):
            for k in ks:
                wait(act, q["ys_ps"], BK * s + k + 1)
                if k == 0:
                    wait(act, y_stored[u], 16 * BB * r)
                nc.scalar.activation(ys[:, u, k, :, :], sl[:, k, :, :], ACT.Copy).then_inc(q["ys"], 1)

        act.wait_ge(ready, READY)
        nc.scalar.activation(id_r[:], id_f[:], ACT.Copy).then_inc(id_half, 1)

        def block_of(r, u):
            s = 2 * r + u
            known = isinstance(s, int)
            if not known or s >= 2:
                outputs(s - 2, u, r - 1, (0, 1))
                slots(s - 2, (2, 3))
            exps(s, u, 0)
            if not known or s >= 2:
                outputs(s - 2, u, r - 1, (2, 3))
            exps(s, u, 1)
            if not known or s >= 1:
                slots(s - 1, (0, 1))

        for r in range(2):
            for u in range(2):
                block_of(r, u)
        with act.Fori(2, SB // 2) as pair:
            for u in range(2):
                block_of(pair, u)
        r = SB // 2 - 1
        outputs(SB - 2, 0, r, (0, 1))
        slots(SB - 2, (2, 3))
        outputs(SB - 2, 0, r, (2, 3))
        slots(SB - 1, range(BK))
        outputs(SB - 1, 1, r, range(BK))

    @block.vector
    def _(dve):
        V = nc.vector

        def greatest(g):
            for k in range(BK):
                wait(dve, q["lg_ps"], BK * g + k + 1)
                if k == 0:
                    wait(dve, q["max"], 3 * g)
                V.tensor_reduce(mp[:, k, :], lg[:, k, :, :].rearrange("p b s -> p s b"), AX.X, ALU.max
                                ).then_inc(q["part"], 1)
            wait(dve, q["part"], BK * (g + 1))
            V.tensor_reduce(mxb[:], mp[:].rearrange("p k s -> p s k"), AX.X, ALU.max).then_inc(q["max"], 1)
            wait(dve, q["max"], 3 * g + 1)
            wait(dve, q["sub_ps"], BK * g)
            V.tensor_scalar(nH[:], mxb[:], -1.0, None, ALU.mult).then_inc(q["max"], 1)
            wait(dve, q["max"], 3 * g + 2)
            V.scalar_tensor_tensor(nL[:], mxb[:], -1.0, nH[:].bitcast(F32), ALU.mult, ALU.subtract
                                   ).then_inc(q["max"], 1)

        def scaled(g, u, c):
            wait(dve, q["ex"], BK * (g + 1))
            wait(dve, q["mult"], g)
            V.tensor_reduce(sm[:], ex[:, u, c, :, :, :].rearrange("p k b s -> p s (k b)"), AX.X, ALU.add
                            ).then_inc(q["sum"], 1)
            wait(dve, q["sum"], 2 * g + 1)
            V.reciprocal(sr[:], sm[:]).then_inc(q["sum"], 1)
            wait(dve, q["sum"], 2 * g + 2)
            e = ex[:, u, c, :, :, :].rearrange("p k b s -> p (k b) s")
            V.tensor_tensor(e, e, sr[:].unsqueeze(1).to_broadcast([P, NB, P]), ALU.mult).then_inc(q["mult"], 1)

        def block_of(s, u):
            greatest(C * s)
            if not isinstance(s, int) or s:
                scaled(C * s - 1, 1 - u, 1)
            greatest(C * s + 1)
            scaled(C * s, u, 0)

        block_of(0, 0)
        block_of(1, 1)
        with dve.Fori(1, SB // 2) as pair:
            for u in range(2):
                block_of(2 * pair + u, u)
        scaled(C * SB - 1, 1, 1)

    @block.gpsimd
    def _(pool):
        def bias(s, u):
            for k in range(BK):
                pool.compute_val(BK * s + k + 1)
            pool.compute_val(s * XB * D)
            for k in range(BK):
                pool.wait_ge(late, 32)
                wait(pool, q["ys"], BK * s + k + 1)
                y = ys[:, u, k, :, :].rearrange("p j e -> p (j e)")
                pool.tensor_tensor(y, y, bx[:, bass.ds(s * XB * D, XB * D)], ALU.add).then_inc(q["y"], 1)

        pool.wait_ge(late, 32)
        bias(0, 0)
        bias(1, 1)
        with pool.Fori(1, SB // 2) as pair:
            for u in range(2):
                bias(2 * pair + u, u)


def combine(nc, ctx, kept, x3_dram, x3T_dram, phi, ident, y_dram, out):
    def sb(name, shape, dt=F32):
        return ctx.enter_context(nc.sbuf_tensor(name, [P] + shape, dt))

    def sem(name):
        return kept.enter_context(nc.semaphore(name))

    id_f = sb("e_id", [P])
    phf = sb("e_phf", [S])
    phH = sb("e_phH", [S], F32R)
    phL = sb("e_phL", [S], F32R)
    xtf = sb("e_xtf", [2, L])
    xtH = sb("e_xtH", [2, L], F32R)
    xtL = sb("e_xtL", [2, L], F32R)
    xs = sb("e_xs", [2, C, D])
    yb = sb("e_yb", [2, SB, D])
    mxt = sb("e_mxt", [1])
    nmx = sb("e_nmx", [1])
    pr = sb("e_pr", [2, SB, P])
    prT = sb("e_prT", [SB, P])
    rs = sb("e_rs", [2])
    rr = sb("e_rr", [2])
    rx = sb("e_rx", [C, D])
    stt = sb("e_st", [C, 6])
    mv = sb("e_mv", [C, 2])
    v, h, y, t = (sb(f"e_n{k}", [C]) for k in range(4))
    xo = sb("e_xo", [2, C, D])

    lg = ctx.enter_context(nc.psum_tensor("e_lg", [P, 4, 512], F32))
    tp = [ctx.enter_context(nc.psum_tensor(f"e_tp{k}", [P, 512], F32)) for k in range(3)]
    po = ctx.enter_context(nc.psum_tensor("e_po", [P, 512], F32))

    ready = sem("e_ready")
    halves = sem("e_halves")
    halves_act = sem("e_halves_act")
    b_in = [sem(f"e_b_in{u}") for u in range(2)]
    stored = [sem(f"e_stored{u}") for u in range(2)]
    q = {n: sem("e_" + n) for n in "xh xl lg_ps max pr tp_ps tp out_ps inv res moments rstd rows".split()}
    block = ctx.enter_context(nc.Block())
    READY = 32
    LOADS = 16 * (2 + XB)

    def wait_apart(eng, *waits):
        for _, value in waits:
            eng.compute_val(value)
        eng.wait_ge(ready, READY)
        for s, value in waits:
            wait(eng, s, value)

    @block.sync
    def _(sp):
        sp.dma_start(phf[:], phi).then_inc(ready, 16)
        sp.dma_start(id_f[:], ident).then_inc(ready, 16)

        def load(b, u):
            for value in (C * (b - 1), b * L) + tuple(b * (XB * D) + j * D for j in range(XB)):
                sp.compute_val(value)
            sp.wait_ge(ready, READY)
            wait(sp, q["res"], C * (b - 1))
            sp.dma_start(xtf[:, u, :], x3T_dram[:, bass.ds(b * L, L)]).then_inc(b_in[u], 16)
            sp.dma_start(xs[:, u, :, :], x3_dram[bass.ds(b * L, L), :].rearrange("(c p) d -> p c d", p=P)
                         ).then_inc(b_in[u], 16)
            for j in range(XB):
                y_j = y_dram.rearrange("(k n) w -> n k w", n=NS)[:, :, bass.ds(b * (XB * D) + j * D, D)]
                sp.dma_start(yb[j * NS:(j + 1) * NS, u, :, :], y_j).then_inc(b_in[u], 16)

        def store(b, u):
            for value in (C * (b + 1), b * L):
                sp.compute_val(value)
            sp.wait_ge(ready, READY)
            wait(sp, q["rows"], C * (b + 1))
            sp.dma_start(out[bass.ds(b * L, L), :].rearrange("(c p) d -> p c d", p=P), xo[:, u, :, :]
                         ).then_inc(stored[u], 16)

        load(0, 0)
        load(1, 1)
        with sp.Fori(1, NB // 2) as pair:
            for u in range(2):
                load(2 * pair + u, u)
                store(2 * pair + u - 2, u)
        for u in range(2):
            store(NB - 2 + u, u)
        for u in range(2):
            sp.wait_ge(stored[u], 16 * (NB // 2))

    @block.tensor
    def _(pe):
        def logits(b, u, c):
            n = C * b + c
            wait(pe, q["xl"], b + 1)
            wait(pe, q["pr"], n)
            cols = slice(c * P, (c + 1) * P)
            for k in range(4):
                part = slice(k * 512, (k + 1) * 512)
                pe.matmul(lg[:, k, :], xtH[:, u, cols], phH[:, part], start=True, stop=False, skip_group_check=True)
                pe.matmul(lg[:, k, :], xtH[:, u, cols], phL[:, part], start=False, stop=False,
                          skip_group_check=True)
                last = pe.matmul(lg[:, k, :], xtL[:, u, cols], phH[:, part], start=False, stop=True,
                                 skip_group_check=True)
            last.then_inc(q["lg_ps"], 1)

        def weigh(n, u, c):
            wait(pe, q["pr"], n + 1)
            for k in range(4):
                if k < 3:
                    wait(pe, q["tp"], 4 * (n - 1) + k + 2 if k < 2 else 4 * n)
                else:
                    wait(pe, q["tp"], 4 * n + 1)
                for j in range(4):
                    last = pe.transpose(tp[k % 3][:, j * P:(j + 1) * P], pr[:, c, 4 * k + j, :], id_f[:])
                last.then_inc(q["tp_ps"], 1)
            wait(pe, q["res"], n)
            for k in range(4):
                wait(pe, q["tp"], 4 * n + k + 1)
                for j in range(4):
                    s = 4 * k + j
                    last = pe.matmul(po[:, 0:D], prT[:, s, :], yb[:, u, s, :], start=(s == 0), stop=(s == SB - 1),
                                     skip_group_check=True)
            last.then_inc(q["out_ps"], 1)

        pe.wait_ge(ready, READY)
        pe.wait_ge(halves, 1)
        pe.wait_ge(halves_act, 1)

        def batch(r, u, first=False):
            b = 2 * r + u
            logits(b, u, 0)
            if not first:
                weigh(C * b - 1, 1 - u, 1)
            logits(b, u, 1)
            pe.wait_ge(b_in[u], LOADS * (r + 1))
            weigh(C * b, u, 0)

        batch(0, 0, True)
        batch(0, 1)
        with pe.Fori(1, NB // 2) as pair:
            for u in range(2):
                batch(pair, u)
        weigh(TT - 1, 1, 1)

    @block.scalar
    def _(act):
        def split(b, u, r):
            wait(act, b_in[u], LOADS * (r + 1))
            wait(act, q["lg_ps"], C * (b - 1))
            nc.scalar.activation(xtH[:, u, :], xtf[:, u, :], ACT.Copy).then_inc(q["xh"], 1)

        def exps(n, c):
            wait(act, q["max"], 2 * (n + 1))
            wait(act, q["tp_ps"], 4 * (n - 1))
            wait(act, q["inv"], n - 1)
            nc.scalar.activation(pr[:, c, :, :].rearrange("p a s -> p (a s)"), lg[:].rearrange("p a s -> p (a s)"),
                                 ACT.Exp, bias=nmx[:], accum_out=rs[:, c:c + 1]).then_inc(q["pr"], 1)

        def turned(n, ks):
            for k in ks:
                wait(act, q["tp_ps"], 4 * n + k + 1)
                wait(act, q["out_ps"], n)
                nc.scalar.activation(prT[:, 4 * k:4 * k + 4, :].rearrange("p a s -> p (a s)"), tp[k % 3][:],
                                     ACT.Copy).then_inc(q["tp"], 1)

        act.wait_ge(ready, READY)
        nc.scalar.activation(phH[:], phf[:], ACT.Copy).then_inc(halves_act, 1)

        def batch(r, u, first=False):
            b = 2 * r + u
            split(b, u, r)
            if not first:
                turned(C * b - 1, range(4))
            exps(C * b, 0)
            turned(C * b, range(4))
            exps(C * b + 1, 1)

        batch(0, 0, True)
        batch(0, 1)
        with act.Fori(1, NB // 2) as pair:
            for u in range(2):
                batch(pair, u)
        turned(TT - 1, range(4))

    @block.vector
    def _(dve):
        V = nc.vector

        def split(b, u):
            wait(dve, q["xh"], b + 1)
            wait(dve, q["lg_ps"], C * (b - 1))
            V.tensor_tensor(xtL[:, u, :], xtf[:, u, :], xtH[:, u, :].bitcast(F32), ALU.subtract
                            ).then_inc(q["xl"], 1)

        def greatest(n):
            wait(dve, q["lg_ps"], n + 1)
            wait(dve, q["max"], 2 * n)
            V.tensor_reduce(mxt[:], lg[:].rearrange("p a s -> p (a s)"), AX.X, ALU.max).then_inc(q["max"], 1)
            wait(dve, q["max"], 2 * n + 1)
            wait(dve, q["pr"], n)
            V.tensor_scalar(nmx[:], mxt[:], -1.0, None, ALU.mult).then_inc(q["max"], 1)

        def residual(n, u, c):
            wait(dve, q["pr"], n + 1)
            V.reciprocal(rr[:, c:c + 1], rs[:, c:c + 1]).then_inc(q["inv"], 1)
            wait(dve, q["inv"], n + 1)
            wait(dve, q["out_ps"], n + 1)
            V.scalar_tensor_tensor(rx[:, c, :], po[:, 0:D], rr[:, c:c + 1], xs[:, u, c, :], ALU.mult, ALU.add
                                   ).then_inc(q["res"], 1)
            wait(dve, q["res"], n + 1)
            V.bn_stats(stt[:, c, :], rx[:, c, :]).then_inc(q["moments"], 1)
            wait_apart(dve, (q["moments"], 2 * n + 1))
            V.bn_aggr(mv[:, c, :], stt[:, c, :]).then_inc(q["moments"], 1)

        def norm(b, u, r):
            wait(dve, q["rstd"], RSQRT_OPS * (b + 1))
            wait(dve, stored[u], 16 * r)
            for c in range(C):
                V.tensor_scalar(xo[:, u, c, :], rx[:, c, :], mv[:, c, 0:1], y[:, c:c + 1], ALU.subtract, ALU.mult
                                ).then_inc(q["rows"], 1)

        dve.wait_ge(halves_act, 1)
        V.tensor_tensor(phL[:], phf[:], phH[:].bitcast(F32), ALU.subtract).then_inc(halves, 1)

        def batch(r, u, first=False):
            b = 2 * r + u
            split(b, u)
            greatest(C * b)
            if not first:
                residual(C * b - 1, 1 - u, 1)
            greatest(C * b + 1)
            if not first:
                norm(b - 1, 1 - u, r if u else r - 1)
            residual(C * b, u, 0)

        batch(0, 0, True)
        batch(0, 1)
        with dve.Fori(1, NB // 2) as pair:
            for u in range(2):
                batch(pair, u)
        residual(TT - 1, 1, 1)
        norm(NB - 1, 1, NB // 2 - 1)

    @block.gpsimd
    def _(pool):
        pool.wait_ge(ready, READY)

        def batch(b):
            newton(pool, wait_apart, q["rstd"], RSQRT_OPS * b, (q["moments"], 2 * C * (b + 1)),
                   mv[:, :, 1], 1.0, EPS, v, h, y, t)

        batch(0)
        batch(1)
        with pool.Fori(1, NB // 2) as pair:
            for u in range(2):
                batch(2 * pair + u)


def constants():
    import numpy as np

    f = np.float32
    i = np.arange(P)
    ident = np.eye(P, dtype=f)
    causal = (i[:, None] <= i[None, :]).astype(f)
    neg = np.zeros((P, 3, P), f)
    later = i[None, :] > i[:, None]
    neg[:, 0][later] = NEG
    neg[:, 2][later] = NEG
    strict = (i[:, None] > i[None, :]).astype(f)
    head_of = (i[:, None] // WL == i[None, :] // WL).astype(f)
    rot = np.zeros((P, P), f)
    rot[i[1::2], i[0::2]] = -1.0
    rot[i[0::2], i[1::2]] = 1.0
    inv = (f(1.0) / np.power(f(10000.0), np.arange(0, D, 2, dtype=f) / f(D))).astype(f)
    ang = (np.arange(L, dtype=f)[:, None] * inv).astype(f)
    cosT = np.repeat(np.cos(ang.astype(np.float64)).astype(f).T, 2, axis=0)
    sinT = np.repeat(np.sin(ang.astype(np.float64)).astype(f).T, 2, axis=0)
    w8 = np.broadcast_to(np.arange(NE, 0, -1).astype(f), (P, NE))
    return dict(ident=ident, causal=causal, neg_blocks=neg, strict_low=strict, upper=causal, head_of=head_of,
                rot=rot, cosT=cosT, sinT=sinT, w8=w8)


def layout(d):
    import numpy as np

    x = np.asarray(d["L0_attn_x"]).reshape(NB * L, D)
    wq, wk, wv = (np.asarray(d[f"L1_attn_W{n}"]).T for n in "qkv")
    a = dict(
        x=x, xT=x.T, in_wT=np.asarray(d["L0_attn_in_proj_w"]).T,
        conv_w=np.asarray(d["L0_attn_conv_w"]).reshape(NCH, P, TAPS).transpose(1, 0, 2),
        conv_b=np.asarray(d["L0_attn_conv_b"]).reshape(NCH, P).T,
        dt_bias=d["L0_attn_dt_bias"], A_log=d["L0_attn_A_log"], Dh=d["L0_attn_D"],
        norm_w=np.asarray(d["L0_attn_norm_w"]).reshape(2, P).T,
        out_wT=np.asarray(d["L0_attn_out_proj_w"]).T.reshape(2, P, D).transpose(1, 0, 2),
        ln_w=d["L0_attn_ln_w"], ln_b=d["L0_attn_ln_b"],
        w_q=d["L0_ffn_w_q"], w_k=d["L0_ffn_w_k"], w_gate=d["L0_ffn_w_gate"],
        v_exp=np.asarray(d["L0_ffn_value_experts"]).transpose(2, 0, 1, 3).reshape(D, NE * HB * DH),
        o_exp=np.asarray(d["L0_ffn_output_experts"]).reshape(NE, HP, 2, DH, D).transpose(2, 3, 1, 0, 4)
        .reshape(P, HP, NE, D),
        WqkvT=np.concatenate([wq, wk, wv], axis=1),
        bq=d["L1_attn_bq"], bk=d["L1_attn_bk"], bv=d["L1_attn_bv"],
        gamma=d["L1_attn_gamma"], beta=d["L1_attn_beta"],
        phi=np.asarray(d["L1_ffn_phi"]).reshape(D, S),
        W=np.asarray(d["L1_ffn_W"]).transpose(1, 0, 2), b_exp=np.asarray(d["L1_ffn_b"]).reshape(-1),
    )
    a.update(constants())
    return {k: np.ascontiguousarray(v) for k, v in a.items()}


def kernel(**inputs):
    import numpy as np
    import concourse.bacc as bacc
    from concourse.bass_utils import run_bass_kernel_spmd

    nc = bacc.Bacc("TRN2", target_bir_lowering=False, num_devices=1)
    arrays = layout(inputs)
    aps = {k: nc.dram_tensor(k, v.shape, mybir.dt.from_np(v.dtype), kind="ExternalInput").ap()
           for k, v in arrays.items()}
    out = nc.dram_tensor("out", (NB * L, D), F32, kind="ExternalOutput").ap()
    build(nc, out=out, **aps)
    r = run_bass_kernel_spmd(nc, [arrays], core_ids=[0])
    return np.asarray(r.results[0]["out"]).reshape(NB, L, D)
```

```python
from contextlib import ExitStack

import concourse.bass as bass
from concourse import mybir

F32 = mybir.dt.float32
F32R = mybir.dt.float32r
BF16 = mybir.dt.bfloat16
I32 = mybir.dt.int32
ALU = mybir.AluOpType
ACT = mybir.ActivationFunctionType
AX = mybir.AxisListType

NB, L, D = 16, 256, 128
P = 128
C = L // P
NH, HD = 4, 64
DI = NH * HD
NCH = (DI + 2 * D) // P
TAPS = 4
EPS = 1e-5
HB, DH, NE = 8, 64, 8
HP = HB // 2
SCALE = DH ** -0.5
NEG = -3.0e38
SCB = 3
HL = 16
WL = D // HL
SHIFT = 0.21
NX, NS = 64, 32
S = NX * NS
SB = S // P
XB = P // NS
TT = NB * C
BK, BB = 4, NB // 4

RSQRT_SEED = float(0x5F3759DF)
RSQRT_STEPS = 3
RSQRT_OPS = 3 + 4 * RSQRT_STEPS
LOG1P_TERMS = 7


def wait(eng, sem, value):
    if not isinstance(value, int) or value > 0:
        eng.wait_ge(sem, value)


def newton(pool, wait_apart, done, k, source, var, scale, eps, v, h, y, t):
    wait_apart(pool, source)
    pool.tensor_scalar(v[:], var, scale, eps, ALU.mult, ALU.add).then_inc(done, 1)
    wait_apart(pool, (done, k + 1))
    pool.tensor_scalar(h[:], v[:], -0.5, None, ALU.mult).then_inc(done, 1)
    pool.tensor_scalar(y[:].bitcast(I32), v[:].bitcast(I32), -0.5, RSQRT_SEED,
                       ALU.mult, ALU.add).then_inc(done, 1)
    for s in range(RSQRT_STEPS):
        wait(pool, done, k + 3 + 4 * s)
        pool.tensor_tensor(t[:], y[:], y[:], ALU.mult).then_inc(done, 1)
        wait(pool, done, k + 4 + 4 * s)
        pool.tensor_tensor(t[:], t[:], h[:], ALU.mult).then_inc(done, 1)
        wait_apart(pool, (done, k + 5 + 4 * s))
        pool.tensor_scalar(t[:], t[:], 1.5, None, ALU.add).then_inc(done, 1)
        wait(pool, done, k + 6 + 4 * s)
        pool.tensor_tensor(y[:], y[:], t[:], ALU.mult).then_inc(done, 1)


def build(nc, x, xT, in_wT, conv_w, conv_b, dt_bias, A_log, Dh, norm_w, out_wT, ln_w, ln_b,
          w_q, w_k, w_gate, v_exp, o_exp, WqkvT, bq, bk, bv, gamma, beta, phi, W, b_exp,
          ident, causal, neg_blocks, strict_low, upper, head_of, rot, cosT, sinT, w8,
          out):
    x3_dram = nc.dram_tensor("x3_tok", (NB * L, D), F32, kind="Internal").ap()
    x3T_dram = nc.dram_tensor("x3_T", (D, NB * L), F32, kind="Internal").ap()
    ctx = ExitStack()
    with ctx:
        x3_stored = ctx.enter_context(nc.semaphore("x3_stored"))
        token_blocks(nc, ctx, x, xT, in_wT, conv_w, conv_b, dt_bias, A_log, Dh, norm_w, out_wT, ln_w, ln_b,
                     w_q, w_k, w_gate, v_exp, o_exp, WqkvT, bq, bk, bv, gamma, beta,
                     ident, causal, neg_blocks, strict_low, upper, head_of, rot, cosT, sinT, w8,
                     x3_dram, x3T_dram, x3_stored)
        soft_experts(nc, ctx, x3_dram, x3T_dram, x3_stored, phi, W, b_exp, ident, out)


def row(ap, n):
    return ap.rearrange("(a n) -> a n", a=1).to_broadcast([P, n])


def token_blocks(nc, kept, x, xT, in_wT, conv_w, conv_b, dt_bias, A_log, Dh, norm_w, out_wT, ln_w, ln_b,
                 w_q, w_k, w_gate, v_exp, o_exp, WqkvT, bq, bk, bv, gamma, beta,
                 ident, causal, neg_blocks, strict_low, upper, head_of, rot, cosT, sinT, w8,
                 x3_dram, x3T_dram, x3_stored):
    with ExitStack() as ctx:
        def sb(name, shape, dt=F32):
            return ctx.enter_context(nc.sbuf_tensor(name, [P] + shape, dt))

        def sem(name):
            return kept.enter_context(nc.semaphore(name))

        id_f = sb("id_f", [P])
        id_b = sb("id_b", [P], BF16)
        causal_s = sb("causal_s", [P])
        negb_f = sb("negb_f", [3, P])
        negb = sb("negb", [3, P], BF16)
        low_s = sb("low_s", [P])
        upp_s = sb("upp_s", [P])
        hof = sb("hof", [P])
        hof_n = sb("hof_n", [P])
        h16 = sb("h16", [HL])
        rot_s = sb("rot_s", [P])
        cos_s = sb("cos_s", [L])
        sin_s = sb("sin_s", [L])
        w8_s = sb("w8_s", [NE])
        in_w = sb("in_w", [2 * DI + 2 * D + NH])
        out_w0 = sb("out_w0", [2, D])
        out_w = sb("out_w", [2, D])
        cw0 = sb("cw0", [NCH, TAPS])
        cb0 = sb("cb0", [NCH])
        cw = sb("cw", [NCH, TAPS])
        cb = sb("cb", [NCH])
        nw = sb("nw", [2])
        dtb = sb("dtb", [NH])
        alog = sb("alog", [NH])
        d_h = sb("d_h", [NH])
        lnw = sb("lnw", [D])
        lnb = sb("lnb", [D])
        wq_f = sb("wq_f", [HB * DH])
        wk_f = sb("wk_f", [HB * DH])
        wg_f = sb("wg_f", [HB * NE])
        wqH = sb("wqH", [HB * DH], F32R)
        wqL = sb("wqL", [HB * DH], F32R)
        wkH = sb("wkH", [HB * DH], F32R)
        wkL = sb("wkL", [HB * DH], F32R)
        wgH = sb("wgH", [HB * NE], F32R)
        wgL = sb("wgL", [HB * NE], F32R)
        ve_f = sb("ve_f", [NE * HB * DH])
        veH = sb("veH", [NE, HB * DH], F32R)
        veL = sb("veL", [NE, HB * DH], F32R)
        oe = sb("oe", [HP, NE, D])
        x_all = oe[:, :, :, :].rearrange("p a e d -> p (a e d)")
        idfold = sb("idfold", [HB * NE])
        numbers = sb("numbers", [HB, NE])
        number = sb("number", [HB])
        pick = sb("pick", [HP, 2, DH], BF16)
        wl = sb("wl", [3 * D])
        bq_s = sb("bq_s", [1])
        bk_s = sb("bk_s", [1])
        bv_s = sb("bv_s", [D])
        gam = sb("gam", [D])
        bet = sb("bet", [D])

        sv = sb("sv", [TT, NH])
        sa = sb("sa", [TT, NH])
        su = sb("su", [TT, NH])
        sd = sb("sd", [TT, NH])
        s2 = sb("s2", [TT, NH])
        sp = sb("sp", [TT, NH])
        ea = sb("ea", [NH])
        dt_all = sb("dt_all", [TT, NH])
        a_all = sb("a_all", [TT, NH])

        xt_in = sb("xt_in", [2, L])
        x_in = sb("x_in", [2, C, D])
        dt_b = sb("dt_b", [C, NH])
        a_b = sb("a_b", [C, NH])
        cin = sb("cin", [NCH, L + TAPS - 1])
        cacc = sb("cacc", [NCH, L])
        xbc = sb("xbc", [NCH, L])
        xd = sb("xd", [C, NH, HD])
        xD = sb("xD", [C, NH, HD])
        btok = sb("btok", [P])
        gm = sb("gm", [C, P])
        am = sb("am", [C, NH, P])
        lx = sb("lx", [C, NH, P])
        mx = sb("mx", [C, NH, P])
        ep = sb("ep", [NH])
        xst = sb("xst", [NH, HD])
        st = sb("st", [DI])
        inter = sb("inter", [NH, HD])
        tz = sb("tz", [C, DI])
        sz = sb("sz", [C, DI])
        ya = sb("ya", [C, DI])
        yg = sb("yg", [C, DI])
        sq = sb("sq", [DI])
        ssq = sb("ssq", [C])
        yT = sb("yT", [2, L])
        ra = sb("ra", [C, D])
        na = sb("na", [C, D])
        xb = sb("xb", [C, D])
        x1 = sb("x1", [2, C, D])
        x1H = sb("x1H", [2, L], F32R)
        x1L = sb("x1L", [2, L], F32R)

        eg = sb("eg", [C, HB, NE])
        g = sb("g", [C, HB, NE])
        gx = sb("gx", [C, HB])
        geq = sb("geq", [C, HB, NE])
        g2 = sb("g2", [C, HB])
        oh = sb("oh", [C, HB, NE])
        ohT = sb("ohT", [P], BF16)
        qk = sb("qk", [HP, 2, L])
        vals = sb("vals", [C, HB, DH])
        r3 = sb("r3", [SCB, 3])
        n3 = sb("n3", [SCB, 3])
        pr = ve_f[:, 2048:2816].rearrange("p (s a n) -> p s a n", s=2, a=3)
        pt = ve_f[:, 2816:3584].rearrange("p (s a n) -> p s a n", s=2, a=3)
        rs = sb("rs", [C, HB])
        rg = sb("rg", [C, HB])
        on = sb("on", [C, HB * DH])
        oT = sb("oT", [C, HP, P])
        mo = ve_f[:, 0:2 * HP * L].rearrange("p (s c a n) -> p s c a n", s=2, c=C, a=HP)
        oa = sb("oa", [L])
        rb = sb("rb", [C, D])
        x2 = sb("x2", [2, C, D])
        x2T = sb("x2T", [2, L])

        gl = wk_f[:, :].rearrange("p (a n) -> p a n", a=2)
        ks = sb("ks", [1])
        km = sb("km", [1])
        kmh = sb("kmh", [HL])
        ql = sb("ql", [2, L])
        t1 = ve_f[:, 3584:4096].rearrange("p (a n) -> p a n", a=2)
        t2 = wq_f[:, :].rearrange("p (a n) -> p a n", a=2)
        qr = sb("qr", [2, L])
        vl = sb("vl", [C, D])
        kr = sb("kr", [C, D])
        kv = sb("kv", [D])
        zd = sb("zd", [C, HL])
        zr = sb("zr", [C, HL])
        rc = sb("rc", [C, HL, WL])
        rc2 = sb("rc2", [C, D])
        ncn = sb("ncn", [C, D])
        n2 = sb("n2", [C, D])
        xc = sb("xc", [C, D])
        x3 = sb("x3", [C, D])
        x3T = sb("x3T", [L])

        bank = [ctx.enter_context(nc.psum_tensor(f"bk{i}", [P, C, 512], F32)) for i in (0, 2)]
        ps_v = bank
        ps_s = [bank[k // 2][:, k % 2, :] for k in range(SCB)]
        ps_o = ctx.enter_context(nc.psum_tensor("ps_o", [P, C, 512], F32))
        ps_a = ctx.enter_context(nc.psum_tensor("ps_a", [P, 512], F32))
        ps_c = ctx.enter_context(nc.psum_tensor("ps_c", [P, 512], F32))

        ready = sem("ready")
        x_all_in = sem("x_all_in")
        experts_in = sem("experts_in")
        prep = sem("prep")
        prep_act = sem("prep_act")
        dt_ps = sem("dt_ps")
        soft = sem("soft")
        soft_act = sem("soft_act")
        x_in_sem = [sem(f"x_in_sem{u}") for u in range(2)]

        names = """a_step a_xbc_ps a_cin a_conv a_th a_xbc a_z_ps a_tz a_sz a_am a_seg_ps a_lx a_mx a_xt_ps a_xd
            a_bg_ps a_btok a_ep a_gm a_xst a_st_ps a_st a_int_ps a_int a_y_ps a_y a_yg a_sq a_yt_ps a_yt
            a_op_ps a_r a_xb a_n a_x1t_ps a_x1h a_x1l a_x1
            b_g_ps b_eg b_gate b_oht_ps b_oht b_qk_ps b_qk b_v_ps b_v0 b_v b_vg b_s_ps b_max b_p b_pt_ps b_pt
            b_pv b_rg b_on b_ot_ps b_ot b_m_ps b_mo b_oe b_oa b_oat_ps b_r b_x2t_ps b_x2t
            c_qk_ps c_g c_km c_q c_v_ps c_v c_rot_ps c_qr c_t2 c_krt_ps c_kr c_kv_ps c_kv c_out_ps c_z c_res c_n
            c_x3t_ps c_x3t c_x3""".split()
        q = {n: sem(n) for n in names}
        norms = {n: {k: sem(f"{n}_{k}") for k in ("moments", "rstd", "rows")}
                 for n in ("rms", "ln1", "ln2", "lnB", "lnC", "lnD")}
        nbuf = {n: (sb(f"{n}_st", [C, 6]), sb(f"{n}_mv", [C, 2]), sb(f"{n}_v", [C]), sb(f"{n}_h", [C]),
                    sb(f"{n}_y", [C]), sb(f"{n}_t", [C])) for n in norms}

        CONSTS = [(id_f, ident), (causal_s, causal), (negb_f, neg_blocks), (low_s, strict_low), (upp_s, upper),
                  (hof, head_of), (rot_s, rot), (cos_s, cosT), (sin_s, sinT), (w8_s, w8),
                  (out_w0, out_wT), (cw0, conv_w), (cb0, conv_b), (nw, norm_w),
                  (wq_f, w_q), (wk_f, w_k), (wg_f, w_gate), (wl, WqkvT)]
        ROWS = [(dtb, dt_bias, NH), (alog, A_log, NH), (d_h, Dh, NH), (lnw, ln_w, D), (lnb, ln_b, D),
                (bv_s, bv, D), (gam, gamma, D), (bet, beta, D)]
        COLS = [(bq_s, bq), (bk_s, bk)]
        READY = 16 * (len(CONSTS) + len(ROWS) + len(COLS))
        PREP = 17
        PREP_ACT = 5

        def wait_apart(eng, *waits):
            for _, v in waits:
                eng.compute_val(v)
            eng.wait_ge(ready, READY)
            for s, v in waits:
                wait(eng, s, v)

        def var_of(n):
            return nbuf[n][1][:, :, 1] if n != "rms" else ssq[:]

        def rstd_of(n):
            return nbuf[n][4]

        def stats(dve, n, src, b):
            stt, mv = nbuf[n][0], nbuf[n][1]
            for c in range(C):
                dve.bn_stats(stt[:, c, :], src[:, c, :]).then_inc(norms[n]["moments"], 1)
            for c in range(C):
                wait_apart(dve, (norms[n]["moments"], 2 * C * b + c + 1))
                dve.bn_aggr(mv[:, c, :], stt[:, c, :]).then_inc(norms[n]["moments"], 1)

        def rsqrt(pool, n, b, scale, eps, source, per):
            _, _, v, h, y, t = nbuf[n]
            newton(pool, wait_apart, norms[n]["rstd"], RSQRT_OPS * b, (source, per * b + per), var_of(n), scale, eps,
                   v, h, y, t)

        def scale_rows(dve, n, src, dst, b):
            wait(dve, norms[n]["rstd"], RSQRT_OPS * (b + 1))
            for c in range(C):
                dve.tensor_scalar(dst[:, c, :], src[:, c, :], nbuf[n][1][:, c, 0:1], rstd_of(n)[:, c:c + 1],
                                  ALU.subtract, ALU.mult).then_inc(norms[n]["rows"], 1)

        block = ctx.enter_context(nc.Block())

        @block.sync
        def _(sp):
            sp.dma_start(in_w[:], in_wT).then_inc(x_all_in, 16)
            sp.dma_start(x_all, xT).then_inc(x_all_in, 16)
            for dst, src in CONSTS:
                sp.dma_start(dst[:], src).then_inc(ready, 16)
            for dst, src, n in ROWS:
                sp.dma_start(dst[:], row(src, n)).then_inc(ready, 16)
            for dst, src in COLS:
                sp.dma_start(dst[:], src.rearrange("(p a) -> p a", a=1)).then_inc(ready, 16)

            def load(b, u):
                for v in (b - 1, C * (b - 1), b * L):
                    sp.compute_val(v)
                sp.wait_ge(x_all_in, 32)
                wait(sp, q["a_xb"], b - 1)
                wait(sp, q["a_z_ps"], b - 1)
                wait(sp, q["a_r"], C * (b - 1))
                sp.dma_start(xt_in[:, u, :], xT[:, bass.ds(b * L, L)]).then_inc(x_in_sem[u], 16)
                sp.dma_start(x_in[:, u, :, :], x[bass.ds(b * L, L), :].rearrange("(c p) d -> p c d", p=P)
                             ).then_inc(x_in_sem[u], 16)

            def store(b):
                for v in (b + 1, b * L):
                    sp.compute_val(v)
                sp.wait_ge(x_all_in, 32)
                wait(sp, q["c_x3"], b + 1)
                sp.dma_start(x3_dram[bass.ds(b * L, L), :].rearrange("(c p) d -> p c d", p=P), x3[:]
                             ).then_inc(x3_stored, 16)
                sp.wait_ge(x_all_in, 32)
                wait(sp, q["c_x3t"], b + 1)
                sp.dma_start(x3T_dram[:, bass.ds(b * L, L)], x3T[:]).then_inc(x3_stored, 16)

            load(0, 0)
            load(1, 1)
            sp.dma_start(ve_f[:], v_exp).then_inc(experts_in, 16)
            sp.wait_ge(dt_ps, 1)
            sp.dma_start(oe[:], o_exp).then_inc(experts_in, 16)
            load(2, 0)
            with sp.Fori(1, NB // 2 - 1) as pair:
                for u in range(2):
                    load(2 * pair + u + 1, 1 - u)
                    store(2 * pair + u - 2)
            load(NB - 1, 1)
            for b in range(NB - 4, NB):
                store(b)
            sp.wait_ge(x3_stored, 32 * NB)

        @block.tensor
        def _(pe):
            def mm3(ps, lh, ll, rh, rl, first=True, last=True):
                pe.matmul(ps, lh, rh, start=first, stop=False, skip_group_check=True)
                pe.matmul(ps, lh, rl, start=False, stop=False, skip_group_check=True)
                return pe.matmul(ps, ll, rh, start=False, stop=last, skip_group_check=True)

            def a_xbc(b, u, r, half):
                if half == 0:
                    wait(pe, x_in_sem[u], 32 * (r + 1))
                    wait(pe, q["a_y"], b)
                else:
                    wait(pe, q["a_cin"], 2 * b + 1)
                for j in range(2):
                    ch = DI + (2 * half + j) * P
                    last = pe.matmul(ps_a[:, j * L:(j + 1) * L], in_w[:, ch:ch + P], xt_in[:, u, :],
                                     start=True, stop=True, skip_group_check=True)
                last.then_inc(q["a_xbc_ps"], 1)

            def a_z(b, u):
                wait(pe, q["a_cin"], 2 * b + 2)
                wait(pe, q["a_r"], C * b)
                for c in range(C):
                    last = pe.matmul(ps_a[:, c * DI:(c + 1) * DI], xt_in[:, u, c * P:(c + 1) * P], in_w[:, 0:DI],
                                     start=True, stop=True, skip_group_check=True)
                last.then_inc(q["a_z_ps"], 1)

            def a_seg(b, c):
                if c == 0:
                    wait(pe, q["a_sz"], b + 1)
                    wait(pe, q["a_x1h"], b)
                    wait(pe, q["a_x1l"], b)
                else:
                    wait(pe, q["a_lx"], C * b + 1)
                wait(pe, q["a_am"], C * b + c + 1)
                pe.matmul(ps_a[:, :], low_s[:], am[:, c, :, :].rearrange("p h t -> p (h t)"),
                          start=True, stop=True, skip_group_check=True).then_inc(q["a_seg_ps"], 1)

            def a_xt(b):
                wait(pe, q["a_xbc"], b + 1)
                wait(pe, q["a_lx"], C * b + 2)
                for c in range(C):
                    for j in range(2):
                        last = pe.transpose(ps_a[:, c * DI + j * P:c * DI + (j + 1) * P],
                                            xbc[:, j, c * P:(c + 1) * P], id_f[:])
                last.then_inc(q["a_xt_ps"], 1)

            def a_bg(b):
                wait(pe, q["a_xd"], 2 * b + 2)
                pe.transpose(ps_a[:, 0:P], xbc[:, 2, 0:P], id_f[:])
                for c in range(C):
                    pe.matmul(ps_a[:, (c + 1) * P:(c + 2) * P], xbc[:, 2, c * P:(c + 1) * P],
                              xbc[:, 3, c * P:(c + 1) * P], start=True, stop=True, skip_group_check=True)
                pe.matmul(ps_a[:, 3 * P:3 * P + NH], upp_s[:], a_b[:, 1, :], start=True, stop=True,
                          skip_group_check=True).then_inc(q["a_bg_ps"], 1)

            def a_state(b):
                wait(pe, q["a_gm"], b + 1)
                wait(pe, q["a_ep"], b + 1)
                wait(pe, q["a_btok"], b + 1)
                wait(pe, q["a_xst"], b + 1)
                pe.matmul(ps_a[:, 0:DI], btok[:], xst[:].rearrange("p h d -> p (h d)"),
                          start=True, stop=True, skip_group_check=True).then_inc(q["a_st_ps"], 1)

            def a_inter(b):
                wait(pe, q["a_st"], b + 1)
                pe.matmul(ps_a[:, DI:2 * DI], xbc[:, 3, P:2 * P], st[:],
                          start=True, stop=True, skip_group_check=True).then_inc(q["a_int_ps"], 1)

            def a_y(b):
                wait(pe, q["a_mx"], C * b + C)
                wait(pe, q["a_int"], 2 * b + 1)
                for c in range(C):
                    for h in range(NH):
                        last = pe.matmul(ps_a[:, c * DI + h * HD:c * DI + (h + 1) * HD], mx[:, c, h, :],
                                         xd[:, c, h, :], start=True, stop=True, skip_group_check=True)
                last.then_inc(q["a_y_ps"], 1)

            def a_yt(b, more):
                wait(pe, q["a_yg"], b + 1)
                if more:
                    wait(pe, q["a_cin"], 2 * b + 4)
                for j in range(2):
                    for c in range(C):
                        last = pe.transpose(ps_a[:, j * L + c * P:j * L + (c + 1) * P],
                                            yg[:, c, j * P:(j + 1) * P], id_f[:])
                last.then_inc(q["a_yt_ps"], 1)

            def a_op(b):
                wait(pe, q["a_yt"], b + 1)
                for c in range(C):
                    for j in range(2):
                        last = pe.matmul(ps_a[:, c * D:(c + 1) * D], yT[:, j, c * P:(c + 1) * P], out_w[:, j, :],
                                         start=(j == 0), stop=(j == 1), skip_group_check=True)
                last.then_inc(q["a_op_ps"], 1)

            def a_x1t(b, u, more):
                wait(pe, q["a_x1"], b + 1)
                if more:
                    wait(pe, q["a_sz"], b + 2)
                for c in range(C):
                    last = pe.transpose(ps_a[:, c * P:(c + 1) * P], x1[:, u, c, :], id_f[:])
                last.then_inc(q["a_x1t_ps"], 1)

            def b_gates(b, u):
                wait(pe, q["b_r"], b)
                for c in range(C):
                    cols = slice(c * P, (c + 1) * P)
                    last = mm3(ps_o[:, 1, c * 64:c * 64 + 64], x1H[:, u, cols], x1L[:, u, cols], wgH[:], wgL[:])
                last.then_inc(q["b_g_ps"], 1)

            def b_qk(b, u, hp):
                if hp == 0:
                    wait(pe, q["a_x1h"], b + 1)
                    wait(pe, q["a_x1l"], b + 1)
                wait(pe, q["b_mo"], (NE + 1) * b)
                bankq = ps_v[hp // 2][:, hp % 2, :]
                pe_cols = slice(hp * P, (hp + 1) * P)
                mm3(bankq[:, 0:L], wqH[:, pe_cols], wqL[:, pe_cols], x1H[:, u, :], x1L[:, u, :])
                mm3(bankq[:, L:2 * L], wkH[:, pe_cols], wkL[:, pe_cols], x1H[:, u, :], x1L[:, u, :]
                    ).then_inc(q["b_qk_ps"], 1)

            def b_values(b, u, e):
                if e < 2:
                    wait(pe, q["b_qk"], HP * b + 2 * e + 2)
                elif e == 2:
                    wait(pe, q["b_v0"], b + 1)
                else:
                    wait(pe, q["b_v"], (NE - 1) * b + e - 2)
                for c in range(C):
                    cols = slice(c * P, (c + 1) * P)
                    last = mm3(ps_v[e % 2][:, c, :], x1H[:, u, cols], x1L[:, u, cols], veH[:, e, :], veL[:, e, :])
                last.then_inc(q["b_v_ps"], 1)

            def b_oht(b):
                wait(pe, q["b_gate"], 7 * b + 7)
                wait(pe, q["b_x2t"], b)
                pe.transpose(ps_o[:, 1, P:2 * P], oh[:].rearrange("p c h e -> p (c h e)"), id_f[:]
                             ).then_inc(q["b_oht_ps"], 1)

            def b_scores(b, h):
                if h < SCB:
                    wait(pe, q["b_v"], (NE - 1) * (b + 1))
                else:
                    wait(pe, q["b_p"], 2 * HB * b + 2 * (h - SCB + 1))
                sc = ps_s[h % SCB]
                half = slice(64 * (h % 2), 64 * (h % 2) + 64)
                pe.matmul(sc[:, 0:3 * P].rearrange("p (a b) -> p a b", a=3)[:, 0:3:2, :], id_b[:], negb[:, 0:3:2, :],
                          start=True, stop=False, skip_group_check=True)
                pe.matmul(sc[:, 0:P], qk[half, h // 2, 0, 0:P], qk[half, h // 2, 1, 0:P],
                          start=False, stop=False, skip_group_check=True)
                pe.matmul(sc[:, P:3 * P], qk[half, h // 2, 0, P:L], qk[half, h // 2, 1, :],
                          start=False, stop=True, skip_group_check=True).then_inc(q["b_s_ps"], 1)

            def b_turn(b, h):
                wait(pe, q["b_p"], 2 * HB * b + 2 * h + 2)
                if h >= 1:
                    wait(pe, q["b_pt"], HB * b + h)
                for k in range(3):
                    last = pe.transpose(ps_v[1][:, 1, k * P:(k + 1) * P], pr[:, h % 2, k, :], id_f[:])
                last.then_inc(q["b_pt_ps"], 1)

            def b_pv(b, h):
                wait(pe, q["b_pt"], HB * b + h + 1)
                if h == 0:
                    wait(pe, q["b_vg"], C * (b + 1))
                    wait(pe, q["b_oht"], b + 1)
                cols = slice(h * DH, (h + 1) * DH)
                pe.matmul(ps_o[:, 0, cols], pt[:, h % 2, 0, :], vals[:, 0, h, :],
                          start=True, stop=True, skip_group_check=True)
                pe.matmul(ps_o[:, 1, cols], pt[:, h % 2, 1, :], vals[:, 0, h, :],
                          start=True, stop=False, skip_group_check=True)
                pe.matmul(ps_o[:, 1, cols], pt[:, h % 2, 2, :], vals[:, 1, h, :],
                          start=False, stop=True, skip_group_check=True).then_inc(q["b_pv"], 1)

            def b_ot(b):
                for c in range(C):
                    wait(pe, q["b_on"], C * b + c + 1)
                    for hp in range(HP):
                        last = pe.transpose(ps_v[0][:, c, hp * P:(hp + 1) * P],
                                            on[:, c, hp * P:(hp + 1) * P], id_f[:])
                last.then_inc(q["b_ot_ps"], 1)

            def b_choice(b):
                wait(pe, q["b_pt"], HB * (b + 1))
                for hp in range(HP):
                    for c in range(C):
                        rows = slice(64 * c, 64 * c + 64)
                        last = pe.matmul(ps_v[1][:, c, hp * P:(hp + 1) * P],
                                         pick[rows, hp, :, :].rearrange("p a k -> p (a k)"), ohT[rows, :],
                                         start=True, stop=True, skip_group_check=True)
                last.then_inc(q["b_m_ps"], 1)

            def b_out(b, e):
                parts = [slice(c, c + 1) for c in range(C)] if e == 0 else [slice(0, C)]
                for n, part in enumerate(parts):
                    wait(pe, q["b_mo"], (NE + 1) * b + (e + 2 if e else n + 1))
                    for hp in range(HP):
                        last = pe.matmul(ps_o[:, 0, part.start * P:part.stop * P], oe[:, hp, e, :],
                                         mo[:, e % 2, part, hp, :],
                                         start=(e == 0 and n == 0 and hp == 0), stop=(e == NE - 1 and hp == HP - 1),
                                         skip_group_check=True)
                last.then_inc(q["b_oe"], 1)

            def b_oat(b):
                wait(pe, q["b_oa"], b + 1)
                for c in range(C):
                    last = pe.transpose(ps_o[:, 1, c * P:(c + 1) * P], oa[:, c * P:(c + 1) * P], id_f[:])
                last.then_inc(q["b_oat_ps"], 1)

            def b_x2t(b, u, more):
                wait(pe, norms["lnB"]["rows"], C * (b + 1))
                if more:
                    wait(pe, q["b_eg"], b + 2)
                for c in range(C):
                    last = pe.transpose(ps_o[:, 1, L + c * P:L + (c + 1) * P], x2[:, u, c, :], id_f[:])
                last.then_inc(q["b_x2t_ps"], 1)

            def c_qk(b, u):
                wait(pe, q["b_x2t"], b + 1)
                wait(pe, q["c_x3t"], b)
                for j in range(2):
                    last = pe.matmul(ps_c[:, j * L:(j + 1) * L], wl[:, j * D:(j + 1) * D], x2T[:, u, :],
                                     start=True, stop=True, skip_group_check=True)
                last.then_inc(q["c_qk_ps"], 1)

            def c_v(b, u):
                wait(pe, q["c_g"], 2 * (b + 1))
                for c in range(C):
                    last = pe.matmul(ps_c[:, c * D:(c + 1) * D], x2T[:, u, c * P:(c + 1) * P], wl[:, 2 * D:3 * D],
                                     start=True, stop=True, skip_group_check=True)
                last.then_inc(q["c_v_ps"], 1)

            def c_rot(b):
                wait(pe, q["c_q"], b + 1)
                wait(pe, q["c_v"], b + 1)
                pe.matmul(ps_c[:, :], rot_s[:], ql[:].rearrange("p a n -> p (a n)"),
                          start=True, stop=True, skip_group_check=True).then_inc(q["c_rot_ps"], 1)

            def c_krt(b):
                wait(pe, q["c_qr"], 2 * b + 2)
                for c in range(C):
                    last = pe.transpose(ps_c[:, c * P:(c + 1) * P], qr[:, 1, c * P:(c + 1) * P], id_f[:])
                last.then_inc(q["c_krt_ps"], 1)

            def c_kv(b):
                wait(pe, q["c_kr"], b + 1)
                for c in range(C):
                    last = pe.matmul(ps_c[:, L:L + D], kr[:, c, :], vl[:, c, :], start=(c == 0), stop=(c == C - 1),
                                     skip_group_check=True)
                last.then_inc(q["c_kv_ps"], 1)

            def c_out(b):
                wait(pe, q["c_kv"], b + 1)
                wait(pe, q["c_km"], 2 * (b + 1))
                for c in range(C):
                    pe.matmul(ps_c[:, c * D:(c + 1) * D], qr[:, 0, c * P:(c + 1) * P], kv[:],
                              start=True, stop=True, skip_group_check=True)
                    last = pe.matmul(ps_c[:, 2 * D + c * HL:2 * D + (c + 1) * HL], ql[:, 0, c * P:(c + 1) * P], kmh[:],
                                     start=True, stop=True, skip_group_check=True)
                last.then_inc(q["c_out_ps"], 1)

            def c_x3t(b):
                wait(pe, q["c_x3"], b + 1)
                for c in range(C):
                    last = pe.transpose(ps_c[:, c * P:(c + 1) * P], x3[:, c, :], id_f[:])
                last.then_inc(q["c_x3t_ps"], 1)

            pe.wait_ge(x_all_in, 32)
            for n in range(TT):
                last = pe.matmul(ps_a[:, n * NH:(n + 1) * NH], x_all[:, n * P:(n + 1) * P],
                                 in_w[:, 2 * DI + 2 * D:2 * DI + 2 * D + NH], start=True, stop=True,
                                 skip_group_check=True)
            last.then_inc(dt_ps, 1)
            pe.wait_ge(ready, READY)
            pe.wait_ge(prep, PREP - 1)
            pe.wait_ge(prep_act, PREP_ACT - 1)
            pe.wait_ge(soft, 1)

            def slot(r, u, a, b, c, more):
                t = 2 * r + u
                r1 = r + u
                for k in range(HP):
                    if b:
                        b_qk(t - 1, 1 - u, k)
                    if c and k == 0:
                        b_oat(t - 2)
                    if b and k == 1:
                        b_gates(t - 1, 1 - u)
                for e in range(NE):
                    if b:
                        b_values(t - 1, 1 - u, e)
                    if a and e == 0:
                        a_seg(t, 0)
                    if c and e == 1:
                        b_x2t(t - 2, u, b)
                    if a and e == 1:
                        a_seg(t, 1)
                    if c and e == 1:
                        c_qk(t - 2, u)
                    if a and e == 3:
                        a_xt(t)
                    if a and e == 5:
                        a_bg(t)
                    if c and e == 2:
                        c_v(t - 2, u)
                    if c and e == 4:
                        c_rot(t - 2)
                    if a and e == 7:
                        a_state(t)
                    if c and e == 7:
                        c_krt(t - 2)
                if b:
                    b_oht(t - 1)
                    b_scores(t - 1, 0)
                    b_scores(t - 1, 1)
                for h in range(HB):
                    if b and h < HB - 2:
                        b_scores(t - 1, h + 2)
                    if c and h == 0:
                        c_kv(t - 2)
                    if a and h == 2:
                        a_inter(t)
                    if a and h == 3:
                        a_y(t)
                    if more and h in (4, 6):
                        a_xbc(t + 1, 1 - u, r1, (h - 4) // 2)
                    if c and h == 3:
                        c_out(t - 2)
                    if b:
                        b_turn(t - 1, h)
                        if h >= 1:
                            b_pv(t - 1, h - 1)
                if b:
                    b_pv(t - 1, HB - 1)
                if a:
                    a_yt(t, more)
                if b:
                    b_choice(t - 1)
                if b:
                    b_ot(t - 1)
                if a:
                    a_op(t)
                for e in range(NE):
                    if b:
                        b_out(t - 1, e)
                    if more and e == 0:
                        a_z(t + 1, 1 - u)
                    if c and e == 2:
                        c_x3t(t - 2)
                    if a and e == 6:
                        a_x1t(t, u, more)

            for half in range(2):
                a_xbc(0, 0, 0, half)
            a_z(0, 0)
            slot(0, 0, True, False, False, True)
            pe.wait_ge(prep, PREP)
            pe.wait_ge(prep_act, PREP_ACT)
            pe.wait_ge(experts_in, 32)
            slot(0, 1, True, True, False, True)
            with pe.Fori(1, NB // 2 - 1) as pair:
                for u in range(2):
                    slot(pair, u, True, True, True, True)
            slot(NB // 2 - 1, 0, True, True, True, True)
            slot(NB // 2 - 1, 1, True, True, True, False)
            slot(NB // 2, 0, False, True, True, False)
            slot(NB // 2, 1, False, False, True, False)

        @block.scalar
        def _(act):
            def copy(dst, src):
                return nc.scalar.activation(dst, src, ACT.Copy)

            def a_cin(b, half):
                wait(act, q["a_xbc_ps"], 2 * b + half + 1)
                wait(act, q["a_conv"], NCH * (TAPS - 1) * b)
                if half == 0:
                    wait(act, q["a_th"], b)
                    wait(act, q["a_xbc"], b)
                for j in range(2):
                    ch = 2 * half + j
                    nc.scalar.activation(cacc[:, ch, :], ps_a[:, j * L:(j + 1) * L], ACT.Identity,
                                         scale=cw[:, ch, TAPS - 1:TAPS], bias=cb[:, ch:ch + 1])
                copy(cin[:, 2 * half:2 * half + 2, TAPS - 1:], ps_a[:].rearrange("p (j n) -> p j n", j=2)
                     ).then_inc(q["a_cin"], 1)

            def a_tz(b):
                wait(act, q["a_z_ps"], b + 1)
                wait(act, q["a_sz"], b)
                nc.scalar.activation(tz[:].rearrange("p c n -> p (c n)"), ps_a[:], ACT.Tanh, scale=0.5
                                     ).then_inc(q["a_tz"], 1)

            def a_th(b):
                wait(act, q["a_conv"], NCH * (TAPS - 1) * (b + 1))
                wait(act, q["a_y_ps"], b)
                nc.scalar.activation(xbc[:], cacc[:], ACT.Tanh).then_inc(q["a_th"], 1)

            def a_lx(b, c):
                wait(act, q["a_seg_ps"], C * b + c + 1)
                wait(act, q["a_mx"], C * b)
                wait(act, q["a_xst"], b)
                nc.scalar.activation(lx[:, c, :, :].rearrange("p h t -> p (h t)"), ps_a[:], ACT.Exp
                                     ).then_inc(q["a_lx"], 1)

            def a_btok(b):
                wait(act, q["a_bg_ps"], b + 1)
                wait(act, q["a_st_ps"], b)
                copy(btok[:], ps_a[:, 0:P]).then_inc(q["a_btok"], 1)
                wait(act, q["a_int"], 2 * b)
                nc.scalar.activation(ep[:], ps_a[:, 3 * P:3 * P + NH], ACT.Exp).then_inc(q["a_ep"], 1)

            def a_st(b):
                wait(act, q["a_st_ps"], b + 1)
                wait(act, q["a_int_ps"], b)
                copy(st[:], ps_a[:, 0:DI]).then_inc(q["a_st"], 1)

            def a_sq(b):
                wait(act, q["a_yg"], b + 1)
                for c in range(C):
                    if c == 1:
                        wait(act, q["a_sq"], C * b + 1)
                    nc.scalar.activation(sq[:], yg[:, c, :], ACT.Square, scale=0.5, accum_out=ssq[:, c:c + 1]
                                         ).then_inc(q["a_sq"], 1)

            def a_yt(b):
                wait(act, q["a_yt_ps"], b + 1)
                wait(act, q["a_op_ps"], b)
                copy(yT[:].rearrange("p j n -> p (j n)"), ps_a[:]).then_inc(q["a_yt"], 1)

            def a_x1h(b, u):
                wait(act, q["a_x1t_ps"], b + 1)
                wait(act, q["b_v_ps"], NE * (b - 1))
                copy(x1H[:, u, :], ps_a[:, 0:L]).then_inc(q["a_x1h"], 1)

            def b_eg(b):
                wait(act, q["b_g_ps"], b + 1)
                wait(act, q["b_gate"], 7 * b)
                nc.scalar.activation(eg[:].rearrange("p c h e -> p (c h e)"), ps_o[:, 1, 0:P], ACT.Exp, scale=-1.0
                                     ).then_inc(q["b_eg"], 1)

            def b_qk(b, hp):
                wait(act, q["b_qk_ps"], HP * b + hp + 1)
                wait(act, q["b_s_ps"], HB * b)
                copy(qk[:, hp, :, :].rearrange("p a n -> p (a n)"), ps_v[hp // 2][:, hp % 2, :]
                     ).then_inc(q["b_qk"], 1)

            def b_v0(b):
                wait(act, q["b_v_ps"], NE * b + 1)
                wait(act, q["b_pv"], HB * b)
                copy(vals[:].rearrange("p c h k -> p c (h k)"), ps_v[0][:]).then_inc(q["b_v0"], 1)

            def b_oht(b):
                wait(act, q["b_oht_ps"], b + 1)
                wait(act, q["b_m_ps"], b)
                copy(ohT[:], ps_o[:, 1, P:2 * P]).then_inc(q["b_oht"], 1)

            def b_probs(b, h):
                wait(act, q["b_max"], 3 * HB * b + 3 * h + 3)
                if h >= 2:
                    wait(act, q["b_pt_ps"], HB * b + h - 1)
                else:
                    wait(act, q["b_rg"], 2 * b)
                sc = ps_s[h % SCB]
                nc.scalar.activation(pr[:, h % 2, 0, :], sc[:, 0:P], ACT.Exp, bias=n3[:, h % SCB, 0:1], scale=SCALE,
                                     accum_out=rs[:, 0, h:h + 1]).then_inc(q["b_p"], 1)
                nc.scalar.activation(pr[:, h % 2, 1:3, :].rearrange("p a b -> p (a b)"), sc[:, P:3 * P], ACT.Exp,
                                     bias=n3[:, h % SCB, 1:2], scale=SCALE,
                                     accum_out=rs[:, 1, h:h + 1]).then_inc(q["b_p"], 1)

            def b_pt(b, h):
                wait(act, q["b_pt_ps"], HB * b + h + 1)
                if h >= 2:
                    wait(act, q["b_pv"], HB * b + h - 1)
                copy(pt[:, h % 2, :, :].rearrange("p a b -> p (a b)"), ps_v[1][:, 1, 0:3 * P]
                     ).then_inc(q["b_pt"], 1)

            def b_ot(b):
                wait(act, q["b_ot_ps"], b + 1)
                wait(act, q["b_mo"], (NE + 1) * b)
                for c in range(C):
                    copy(oT[:, c, :, :].rearrange("p a n -> p (a n)"), ps_v[0][:, c, :]).then_inc(q["b_ot"], 1)

            def b_oa(b):
                wait(act, q["b_oe"], NE * (b + 1))
                copy(oa[:], ps_o[:, 0, 0:L]).then_inc(q["b_oa"], 1)

            def b_x2t(b, u):
                wait(act, q["b_x2t_ps"], b + 1)
                copy(x2T[:, u, :], ps_o[:, 1, L:2 * L]).then_inc(q["b_x2t"], 1)

            def c_gelu(b):
                wait(act, q["c_qk_ps"], b + 1)
                wait(act, q["c_q"], b)
                wait(act, q["c_km"], 2 * b)
                nc.scalar.activation(gl[:, 0, :], ps_c[:, 0:L], ACT.Gelu, bias=bq_s[:]).then_inc(q["c_g"], 1)
                nc.scalar.activation(gl[:, 1, :], ps_c[:, L:2 * L], ACT.Gelu, bias=bk_s[:],
                                     accum_out=ks[:]).then_inc(q["c_g"], 1)

            def c_kr(b):
                wait(act, q["c_krt_ps"], b + 1)
                copy(kr[:].rearrange("p c d -> p (c d)"), ps_c[:, 0:L]).then_inc(q["c_kr"], 1)

            def c_x3t(b):
                wait(act, q["c_x3t_ps"], b + 1)
                wait(act, x3_stored, 32 * b)
                copy(x3T[:], ps_c[:, 0:L]).then_inc(q["c_x3t"], 1)

            act.wait_ge(ready, READY)
            copy(wqH[:], wq_f[:]).then_inc(prep_act, 1)
            copy(wkH[:], wk_f[:]).then_inc(prep_act, 1)
            copy(wgH[:], wg_f[:]).then_inc(prep_act, 1)
            nc.scalar.activation(ea[:], alog[:], ACT.Exp).then_inc(prep_act, 1)
            act.wait_ge(soft, 2)
            nc.scalar.activation(su[:], sa[:], ACT.Exp, scale=-1.0).then_inc(soft_act, 1)

            def slot(r, u, a, b, c, more):
                t = 2 * r + u
                if c:
                    b_oa(t - 2)
                for k in range(HP):
                    if b:
                        b_qk(t - 1, k)
                    if b and k == 1:
                        b_eg(t - 1)
                    if a and k == 1:
                        a_th(t)
                for e in range(NE):
                    if b and e == 0:
                        b_v0(t - 1)
                    if a and e == 0:
                        a_lx(t, 0)
                    if c and e == 0:
                        b_x2t(t - 2, u)
                    if c and e == 0:
                        c_gelu(t - 2)
                    if a and e == 1:
                        a_lx(t, 1)
                    if a and e == 5:
                        a_btok(t)
                    if c and e == 6:
                        c_kr(t - 2)
                if b:
                    b_oht(t - 1)
                if b:
                    b_probs(t - 1, 0)
                for h in range(HB):
                    if b and h < HB - 1:
                        b_probs(t - 1, h + 1)
                    if b:
                        b_pt(t - 1, h)
                    if a and h == 0:
                        a_st(t)
                    if more and h in (4, 7):
                        a_cin(t + 1, (h - 4) // 3)
                    if a and h == 4:
                        a_sq(t)
                if a:
                    a_yt(t)
                if b:
                    b_ot(t - 1)
                if more:
                    a_tz(t + 1)
                if c:
                    c_x3t(t - 2)
                if a:
                    a_x1h(t, u)

            for half in range(2):
                a_cin(0, half)
            a_tz(0)
            act.wait_ge(experts_in, 32)
            copy(veH[:].rearrange("p e n -> p (e n)"), ve_f[:]).then_inc(prep_act, 1)
            slot(0, 0, True, False, False, True)
            slot(0, 1, True, True, False, True)
            with act.Fori(1, NB // 2 - 1) as pair:
                for u in range(2):
                    slot(pair, u, True, True, True, True)
            slot(NB // 2 - 1, 0, True, True, True, True)
            slot(NB // 2 - 1, 1, True, True, True, False)
            slot(NB // 2, 0, False, True, True, False)
            slot(NB // 2, 1, False, False, True, False)

        @block.vector
        def _(dve):
            V = nc.vector

            def a_steps(b):
                wait_apart(dve, (q["a_xd"], 2 * b), (q["a_bg_ps"], b), (q["a_am"], C * b))
                V.tensor_copy(dt_b[:], dt_all[:, bass.ds(b * C, C), :]).then_inc(q["a_step"], 1)
                V.tensor_copy(a_b[:], a_all[:, bass.ds(b * C, C), :]).then_inc(q["a_step"], 1)

            def a_conv(b, half, taps=range(1, TAPS)):
                wait(dve, q["a_cin"], 2 * b + half + 1)
                n0 = (TAPS - 1) * (NCH * b + 2 * half)
                for k in taps:
                    for j in range(2):
                        ch = 2 * half + j
                        tap = TAPS - 1 - k
                        if k > 1:
                            wait(dve, q["a_conv"], n0 + 2 * (k - 2) + j + 1)
                        V.scalar_tensor_tensor(cacc[:, ch, :], cin[:, ch, tap:tap + L], cw[:, ch, tap:tap + 1],
                                               cacc[:, ch, :], ALU.mult, ALU.add).then_inc(q["a_conv"], 1)

            def a_sz(b):
                wait(dve, q["a_tz"], b + 1)
                wait(dve, q["a_yg"], b)
                V.scalar_tensor_tensor(sz[:].rearrange("p c n -> p (c n)"), tz[:].rearrange("p c n -> p (c n)"), 1.0,
                                       ps_a[:], ALU.add, ALU.mult).then_inc(q["a_sz"], 1)

            def a_xbc(b):
                wait(dve, q["a_th"], b + 1)
                V.scalar_tensor_tensor(xbc[:], xbc[:], 1.0, cacc[:], ALU.add, ALU.mult).then_inc(q["a_xbc"], 1)

            def a_xd(b):
                wait(dve, q["a_xt_ps"], b + 1)
                wait(dve, q["a_step"], 2 * (b + 1))
                ps = ps_a[:].rearrange("p (c h d) -> p c h d", c=C, h=NH)
                V.tensor_tensor(xd[:], ps, dt_b[:].unsqueeze(3).to_broadcast([P, C, NH, HD]), ALU.mult
                                ).then_inc(q["a_xd"], 1)
                V.tensor_tensor(xD[:], ps, d_h[:].unsqueeze(1).unsqueeze(3).to_broadcast([P, C, NH, HD]), ALU.mult
                                ).then_inc(q["a_xd"], 1)

            def a_xst(b):
                wait(dve, q["a_lx"], C * b + 1)
                wait(dve, q["a_xd"], 2 * b + 2)
                wait(dve, q["a_st_ps"], b)
                V.tensor_tensor(xst[:], xd[:, 0, :, :], lx[:, 0, :, P - 1:P].to_broadcast([P, NH, HD]), ALU.mult
                                ).then_inc(q["a_xst"], 1)

            def a_gm(b):
                wait(dve, q["a_ep"], b + 1)
                wait(dve, q["a_mx"], C * b)
                V.tensor_tensor(gm[:], ps_a[:, P:3 * P].rearrange("p (c t) -> p c t", c=C),
                                causal_s[:].unsqueeze(1).to_broadcast([P, C, P]), ALU.mult).then_inc(q["a_gm"], 1)

            def a_int(b):
                wait(dve, q["a_int_ps"], b + 1)
                wait(dve, q["a_ep"], b + 1)
                V.tensor_tensor(inter[:], ps_a[:, DI:2 * DI].rearrange("p (h d) -> p h d", h=NH),
                                ep[:].unsqueeze(2).to_broadcast([P, NH, HD]), ALU.mult).then_inc(q["a_int"], 1)
                wait(dve, q["a_int"], 2 * b + 1)
                V.tensor_tensor(xD[:, 1, :, :], xD[:, 1, :, :], inter[:], ALU.add).then_inc(q["a_int"], 1)

            def a_y(b):
                wait(dve, q["a_y_ps"], b + 1)
                wait(dve, q["a_int"], 2 * b + 2)
                V.tensor_tensor(ya[:].rearrange("p c n -> p (c n)"), ps_a[:], xD[:].rearrange("p c h d -> p (c h d)"),
                                ALU.add).then_inc(q["a_y"], 1)
                wait(dve, q["a_y"], b + 1)
                wait(dve, q["a_sq"], C * b)
                wait(dve, q["a_yt_ps"], b)
                V.tensor_tensor(yg[:], ya[:], sz[:], ALU.mult).then_inc(q["a_yg"], 1)

            def a_res(b, u):
                V_r = rstd_of("rms")
                wait(dve, norms["rms"]["rstd"], RSQRT_OPS * (b + 1))
                wait(dve, q["a_op_ps"], b + 1)
                V.tensor_scalar(V_r[:], V_r[:], 0.5, None, ALU.mult).then_inc(norms["rms"]["rows"], 1)
                wait(dve, norms["rms"]["rows"], b + 1)
                for c in range(C):
                    V.scalar_tensor_tensor(ra[:, c, :], ps_a[:, c * D:(c + 1) * D], V_r[:, c:c + 1], x_in[:, u, c, :],
                                           ALU.mult, ALU.add).then_inc(q["a_r"], 1)
                wait(dve, q["a_r"], C * (b + 1))
                stats(dve, "ln1", ra, b)

            def a_ln1(b):
                scale_rows(dve, "ln1", ra, na, b)
                wait(dve, norms["ln1"]["rows"], C * (b + 1))
                V.tensor_tensor(na[:], na[:], lnw[:].unsqueeze(1).to_broadcast([P, C, D]), ALU.mult
                                ).then_inc(q["a_n"], 1)
                wait(dve, q["a_n"], 2 * b + 1)
                wait(dve, q["a_xb"], b + 1)
                V.tensor_tensor(na[:], na[:], xb[:], ALU.add).then_inc(q["a_n"], 1)
                wait(dve, q["a_n"], 2 * b + 2)
                stats(dve, "ln2", na, b)

            def a_ln2(b, u):
                wait(dve, norms["lnB"]["rows"], C * (b - 1))
                wait(dve, norms["ln2"]["rstd"], RSQRT_OPS * (b + 1))
                for c in range(C):
                    ins = V.tensor_scalar(x1[:, u, c, :], na[:, c, :], nbuf["ln2"][1][:, c, 0:1],
                                          rstd_of("ln2")[:, c:c + 1], ALU.subtract, ALU.mult)
                ins.then_inc(q["a_x1"], 1)

            def a_x1l(b, u):
                wait(dve, q["a_x1h"], b + 1)
                V.tensor_tensor(x1L[:, u, :], ps_a[:, 0:L], x1H[:, u, :].bitcast(F32), ALU.subtract
                                ).then_inc(q["a_x1l"], 1)

            def b_gate(b):
                k = 7 * b
                n = q["b_gate"]
                wait(dve, q["b_eg"], b + 1)
                V.tensor_scalar(eg[:], eg[:], 1.0, None, ALU.add).then_inc(n, 1)
                wait(dve, n, k + 1)
                V.reciprocal(g[:], eg[:]).then_inc(n, 1)
                wait(dve, n, k + 2)
                V.tensor_reduce(gx[:], g[:], AX.X, ALU.max).then_inc(n, 1)
                wait(dve, n, k + 3)
                V.tensor_tensor(geq[:], g[:], gx[:].unsqueeze(3).to_broadcast([P, C, HB, NE]), ALU.is_equal
                                ).then_inc(n, 1)
                wait(dve, n, k + 4)
                V.tensor_tensor(geq[:], geq[:], w8_s[:].unsqueeze(1).unsqueeze(1).to_broadcast([P, C, HB, NE]),
                                ALU.mult).then_inc(n, 1)
                wait(dve, n, k + 5)
                V.tensor_reduce(g2[:], geq[:], AX.X, ALU.max).then_inc(n, 1)
                wait(dve, n, k + 6)
                V.tensor_tensor(oh[:], geq[:], g2[:].unsqueeze(3).to_broadcast([P, C, HB, NE]), ALU.is_equal
                                ).then_inc(n, 1)

            def b_v(b, e):
                if e == 1:
                    wait_apart(dve, (q["b_v_ps"], NE * b + 2), (q["b_v0"], b + 1), (q["b_gate"], 7 * b + 7))
                else:
                    wait_apart(dve, (q["b_v_ps"], NE * b + e + 1), (q["b_v"], (NE - 1) * b + e - 1))
                for c in range(C):
                    ins = V.copy_predicated(vals[:, c, :, :],
                                            oh[:, c, :, e:e + 1].bitcast(I32).to_broadcast([P, HB, DH]),
                                            ps_v[e % 2][:, c, :].rearrange("p (h k) -> p h k", h=HB))
                ins.then_inc(q["b_v"], 1)

            def b_vg(b):
                wait(dve, q["b_v"], (NE - 1) * (b + 1))
                for c in range(C):
                    V.tensor_tensor(vals[:, c, :, :], vals[:, c, :, :],
                                    gx[:, c, :].unsqueeze(2).to_broadcast([P, HB, DH]), ALU.mult
                                    ).then_inc(q["b_vg"], 1)

            def b_max(b, h):
                n, k = q["b_max"], 3 * HB * b + 3 * h
                wait(dve, q["b_s_ps"], HB * b + h + 1)
                if h >= SCB:
                    wait(dve, q["b_p"], 2 * HB * b + 2 * (h - SCB + 1))
                V.tensor_reduce(r3[:, h % SCB, :], ps_s[h % SCB][:, 0:3 * P].rearrange("p (a b) -> p a b", a=3),
                                AX.X, ALU.max).then_inc(n, 1)
                wait(dve, n, k + 1)
                V.tensor_scalar(n3[:, h % SCB, :], r3[:, h % SCB, :], -SCALE, None, ALU.mult).then_inc(n, 1)
                wait(dve, n, k + 2)
                V.tensor_tensor(n3[:, h % SCB, 1:2], n3[:, h % SCB, 1:2], n3[:, h % SCB, 2:3], ALU.min).then_inc(n, 1)

            def b_on(b):
                wait(dve, q["b_p"], 2 * HB * (b + 1))
                V.reciprocal(rg[:], rs[:]).then_inc(q["b_rg"], 1)
                wait(dve, q["b_rg"], 2 * b + 1)
                V.tensor_tensor(rg[:], rg[:], gx[:], ALU.mult).then_inc(q["b_rg"], 1)
                wait(dve, q["b_rg"], 2 * b + 2)
                wait(dve, q["b_pv"], HB * (b + 1))
                for c in range(C):
                    V.tensor_tensor(on[:, c, :].rearrange("p (h k) -> p h k", h=HB),
                                    ps_o[:, c, :].rearrange("p (h k) -> p h k", h=HB),
                                    rg[:, c, :].unsqueeze(2).to_broadcast([P, HB, DH]), ALU.mult
                                    ).then_inc(q["b_on"], 1)

            def b_mo(b, e):
                parts = [slice(c, c + 1) for c in range(C)] if e == 0 else [slice(0, C)]
                for n, part in enumerate(parts):
                    if e == 0:
                        wait(dve, q["b_m_ps"], b + 1)
                        wait(dve, q["b_ot"], C * b + n + 1)
                        wait(dve, q["b_oe"], NE * b)
                    elif e >= 2:
                        wait(dve, q["b_oe"], NE * b + e - 1)
                    V.scalar_tensor_tensor(mo[:, e % 2, part, :, :].rearrange("p c a n -> p (c a n)"),
                                           ps_v[1][:, part, :].rearrange("p c n -> p (c n)"), float(NE - e),
                                           oT[:, part, :, :].rearrange("p c a n -> p (c a n)"),
                                           ALU.is_equal, ALU.mult).then_inc(q["b_mo"], 1)

            def b_res(b, u):
                wait(dve, q["b_oat_ps"], b + 1)
                V.tensor_tensor(rb[:].rearrange("p c d -> p (c d)"), ps_o[:, 1, 0:L],
                                x1[:, u, :, :].rearrange("p c d -> p (c d)"), ALU.add).then_inc(q["b_r"], 1)
                wait(dve, q["b_r"], b + 1)
                stats(dve, "lnB", rb, b)

            def b_x2(b, u):
                scale_rows(dve, "lnB", rb, x2[:, u, :, :], b)

            def c_q(b):
                wait(dve, q["c_g"], 2 * (b + 1))
                wait(dve, q["c_out_ps"], b)
                V.tensor_scalar(ql[:], gl[:], SHIFT, None, ALU.add).then_inc(q["c_q"], 1)

            def c_v(b):
                wait(dve, q["c_v_ps"], b + 1)
                wait(dve, q["c_kv_ps"], b)
                V.tensor_tensor(vl[:], ps_c[:, 0:L].rearrange("p (c d) -> p c d", c=C),
                                bv_s[:].unsqueeze(1).to_broadcast([P, C, D]), ALU.add).then_inc(q["c_v"], 1)

            def c_qr(b):
                n, k = q["c_qr"], 2 * b
                wait(dve, q["c_rot_ps"], b + 1)
                V.tensor_tensor(t1[:], ps_c[:].rearrange("p (a n) -> p a n", a=2),
                                sin_s[:].unsqueeze(1).to_broadcast([P, 2, L]), ALU.mult).then_inc(n, 1)
                wait(dve, n, k + 1)
                wait(dve, q["c_t2"], b + 1)
                wait(dve, q["c_out_ps"], b)
                V.tensor_tensor(qr[:], t1[:], t2[:], ALU.add).then_inc(n, 1)

            def c_kv(b):
                wait(dve, q["c_kv_ps"], b + 1)
                wait(dve, q["c_out_ps"], b)
                V.tensor_tensor(kv[:], ps_c[:, L:L + D], hof_n[:], ALU.mult).then_inc(q["c_kv"], 1)

            def c_res(b, u):
                wait(dve, q["c_out_ps"], b + 1)
                V.tensor_scalar(zd[:].rearrange("p c h -> p (c h)"), ps_c[:, 2 * D:2 * D + C * HL], 1e-6, None, ALU.add
                                ).then_inc(q["c_z"], 1)
                wait(dve, q["c_z"], 2 * b + 1)
                V.reciprocal(zr[:], zd[:]).then_inc(q["c_z"], 1)
                wait(dve, q["c_z"], 2 * b + 2)
                V.tensor_tensor(rc[:], ps_c[:, 0:L].rearrange("p (c h e) -> p c h e", c=C, h=HL),
                                zr[:].unsqueeze(3).to_broadcast([P, C, HL, WL]), ALU.mult).then_inc(q["c_res"], 1)
                wait(dve, q["c_res"], 2 * b + 1)
                V.tensor_tensor(rc2[:], rc[:].rearrange("p c h e -> p c (h e)"), x2[:, u, :, :], ALU.add
                                ).then_inc(q["c_res"], 1)
                wait(dve, q["c_res"], 2 * b + 2)
                stats(dve, "lnC", rc2, b)
                V.tensor_tensor(xc[:], x2[:, u, :, :], bet[:].unsqueeze(1).to_broadcast([P, C, D]), ALU.add
                                ).then_inc(q["c_n"], 1)

            def c_ln(b):
                scale_rows(dve, "lnC", rc2, ncn, b)
                wait(dve, norms["lnC"]["rows"], C * (b + 1))
                V.tensor_tensor(n2[:], ncn[:], gam[:].unsqueeze(1).to_broadcast([P, C, D]), ALU.mult
                                ).then_inc(q["c_n"], 1)
                wait(dve, q["c_n"], 3 * b + 2)
                V.tensor_tensor(n2[:], n2[:], xc[:], ALU.add).then_inc(q["c_n"], 1)
                wait(dve, q["c_n"], 3 * b + 3)
                stats(dve, "lnD", n2, b)

            def c_x3(b):
                wait(dve, norms["lnD"]["rstd"], RSQRT_OPS * (b + 1))
                wait(dve, x3_stored, 32 * b)
                for c in range(C):
                    ins = V.tensor_scalar(x3[:, c, :], n2[:, c, :], nbuf["lnD"][1][:, c, 0:1],
                                          rstd_of("lnD")[:, c:c + 1], ALU.subtract, ALU.mult)
                ins.then_inc(q["c_x3"], 1)

            dve.wait_ge(ready, READY)
            V.tensor_copy(id_b[:], id_f[:]).then_inc(prep, 1)
            V.tensor_copy(negb[:], negb_f[:]).then_inc(prep, 1)
            V.tensor_scalar(hof_n[:], hof[:], 1.0 / L, None, ALU.mult).then_inc(prep, 1)
            V.tensor_copy(h16[:], hof[:].rearrange("p (h e) -> p h e", h=HL)[:, :, 0]).then_inc(prep, 1)
            V.tensor_scalar(cw[:], cw0[:], 0.5, None, ALU.mult).then_inc(prep, 1)
            V.tensor_scalar(cb[:], cb0[:], 0.5, None, ALU.mult).then_inc(prep, 1)
            for j in range(2):
                V.tensor_scalar(out_w[:, j, :], out_w0[:, j, :], nw[:, j:j + 1], None, ALU.mult).then_inc(prep, 1)
            V.memset(cin[:, :, 0:TAPS - 1], 0.0).then_inc(prep, 1)
            V.tensor_tensor(idfold[:], id_f[:, 0:64], id_f[:, 64:128], ALU.add).then_inc(prep, 1)
            dve.wait_ge(prep, 10)
            V.tensor_tensor(numbers[:], idfold[:].rearrange("p (h e) -> p h e", h=HB),
                            w8_s[:].unsqueeze(1).to_broadcast([P, HB, NE]), ALU.mult).then_inc(prep, 1)
            dve.wait_ge(prep, 11)
            V.tensor_reduce(number[:], numbers[:], AX.X, ALU.add).then_inc(prep, 1)
            dve.wait_ge(prep, 12)
            V.tensor_copy(pick[:], number[:].rearrange("p (a b) -> p a b", a=HP).unsqueeze(3)
                          .to_broadcast([P, HP, 2, DH])).then_inc(prep, 1)
            for n, (lo, full, hi) in enumerate(((wqL, wq_f, wqH), (wkL, wk_f, wkH), (wgL, wg_f, wgH))):
                dve.wait_ge(prep_act, n + 1)
                V.tensor_tensor(lo[:], full[:], hi[:].bitcast(F32), ALU.subtract).then_inc(prep, 1)

            dve.wait_ge(dt_ps, 1)
            V.tensor_tensor(sv[:], ps_a[:, 0:TT * NH].rearrange("p (n h) -> p n h", h=NH),
                            dtb[:].unsqueeze(1).to_broadcast([P, TT, NH]), ALU.add).then_inc(soft, 1)
            dve.wait_ge(soft, 1)
            V.scalar_tensor_tensor(sa[:], sv[:], -1.0, sv[:], ALU.mult, ALU.max).then_inc(soft, 1)
            dve.wait_ge(soft_act, 1)
            V.tensor_scalar(sd[:], su[:], 2.0, None, ALU.add).then_inc(soft, 1)
            dve.wait_ge(soft, 3)
            V.reciprocal(sd[:], sd[:]).then_inc(soft, 1)
            dve.wait_ge(soft, 4)
            V.tensor_tensor(sd[:], sd[:], su[:], ALU.mult).then_inc(soft, 1)
            dve.wait_ge(soft, 5)
            V.tensor_tensor(s2[:], sd[:], sd[:], ALU.mult).then_inc(soft, 1)
            dve.wait_ge(soft, 6)
            V.tensor_scalar(sp[:], s2[:], 1.0 / (2 * LOG1P_TERMS + 1), None, ALU.mult).then_inc(soft, 1)
            at = 7
            for k in range(LOG1P_TERMS - 1, 0, -1):
                dve.wait_ge(soft, at)
                V.scalar_tensor_tensor(sp[:], sp[:], 1.0 / (2 * k + 1), s2[:], ALU.add, ALU.mult).then_inc(soft, 1)
                at += 1
            dve.wait_ge(soft, at)
            V.scalar_tensor_tensor(sp[:], sp[:], 1.0, sd[:], ALU.add, ALU.mult).then_inc(soft, 1)
            V.tensor_scalar(sv[:], sv[:], 0.0, None, ALU.max).then_inc(soft, 1)
            dve.wait_ge(soft, at + 2)
            V.scalar_tensor_tensor(dt_all[:], sp[:], 2.0, sv[:], ALU.mult, ALU.add).then_inc(soft, 1)
            dve.wait_ge(soft, at + 3)
            dve.wait_ge(prep_act, PREP_ACT - 1)
            V.scalar_tensor_tensor(a_all[:], dt_all[:], -1.0, ea[:].unsqueeze(1).to_broadcast([P, TT, NH]),
                                   ALU.mult, ALU.mult).then_inc(soft, 1)
            dve.wait_ge(soft, at + 4)

            def slot(r, u, a, b, c, more):
                t = 2 * r + u
                if c:
                    b_res(t - 2, u)
                if b:
                    b_gate(t - 1)
                if c:
                    b_x2(t - 2, u)
                if a:
                    a_xbc(t)
                if isinstance(t, int) and t == 0:
                    dve.wait_ge(prep_act, PREP_ACT)
                    V.tensor_tensor(veL[:].rearrange("p e n -> p (e n)"), ve_f[:],
                                    veH[:].rearrange("p e n -> p (e n)").bitcast(F32), ALU.subtract).then_inc(prep, 1)
                for e in range(NE):
                    if b and e >= 1:
                        b_v(t - 1, e)
                    if a and e == 4:
                        a_xd(t)
                        a_xst(t)
                    if a and e == 6:
                        a_gm(t)
                    if c and e == 2:
                        c_q(t - 2)
                    if c and e == 3:
                        c_v(t - 2)
                    if c and e == 5:
                        c_qr(t - 2)
                if b:
                    b_max(t - 1, 0)
                    b_max(t - 1, 1)
                    b_vg(t - 1)
                for h in range(HB):
                    if b and h < HB - 2:
                        b_max(t - 1, h + 2)
                    if c and h == 0:
                        c_kv(t - 2)
                    if a and h == 2:
                        a_int(t)
                    if a and h == 3:
                        a_y(t)
                    if c and h == 3:
                        c_res(t - 2, u)
                    if more and h == 5:
                        a_conv(t + 1, 0, (1,))
                    if more and h == 6:
                        a_conv(t + 1, 0, (2, 3))
                    if c and h == 7:
                        c_ln(t - 2)
                if b:
                    b_on(t - 1)
                for e in range(NE):
                    if b:
                        b_mo(t - 1, e)
                    if a and e == 0:
                        a_res(t, u)
                    if c and e == 1:
                        c_x3(t - 2)
                    if more and e == 2:
                        a_conv(t + 1, 1, (1,))
                    if a and e == 3:
                        a_ln1(t)
                    if more and e == 5:
                        a_sz(t + 1)
                        a_steps(t + 1)
                    if a and e == 6:
                        a_ln2(t, u)
                if more:
                    a_conv(t + 1, 1, (2,))
                if a:
                    a_x1l(t, u)
                if more:
                    a_conv(t + 1, 1, (3,))

            a_steps(0)
            a_conv(0, 0)
            a_sz(0)
            a_conv(0, 1)
            slot(0, 0, True, False, False, True)
            slot(0, 1, True, True, False, True)
            with dve.Fori(1, NB // 2 - 1) as pair:
                for u in range(2):
                    slot(pair, u, True, True, True, True)
            slot(NB // 2 - 1, 0, True, True, True, True)
            slot(NB // 2 - 1, 1, True, True, True, False)
            slot(NB // 2, 0, False, True, True, False)
            slot(NB // 2, 1, False, False, True, False)

        @block.gpsimd
        def _(pool):
            G = nc.gpsimd

            def a_am(b):
                for c in range(C):
                    wait_apart(pool, (q["a_step"], 2 * (b + 1)), (q["a_seg_ps"], C * b))
                    G.affine_select(out=am[:, c, :, :], in_=a_b[:, c, :].unsqueeze(2).to_broadcast([P, NH, P]),
                                    compare_op=ALU.is_ge, fill=0.0, base=0, pattern=[[0, NH], [1, P]],
                                    channel_multiplier=-1).then_inc(q["a_am"], 1)

            def a_mx(b):
                wait(pool, q["a_gm"], b + 1)
                wait(pool, q["a_lx"], C * (b + 1))
                wait(pool, q["a_y_ps"], b)
                for c in range(C):
                    G.tensor_tensor(mx[:, c, :, :], lx[:, c, :, :], gm[:, c, :].unsqueeze(1).to_broadcast([P, NH, P]),
                                    ALU.mult).then_inc(q["a_mx"], 1)

            def a_xb(b, u):
                wait(pool, q["a_n"], 2 * b)
                G.tensor_tensor(xb[:], x_in[:, u, :, :], lnb[:].unsqueeze(1).to_broadcast([P, C, D]), ALU.add
                                ).then_inc(q["a_xb"], 1)

            def c_turn(b):
                wait(pool, q["c_q"], b + 1)
                wait(pool, q["c_qr"], 2 * b)
                G.tensor_tensor(t2[:], ql[:], cos_s[:].unsqueeze(1).to_broadcast([P, 2, L]), ALU.mult
                                ).then_inc(q["c_t2"], 1)

            def c_km(b):
                wait_apart(pool, (q["c_g"], 2 * (b + 1)), (q["c_out_ps"], b))
                G.tensor_scalar(km[:], ks[:], 1.0 / L, SHIFT, ALU.mult, ALU.add).then_inc(q["c_km"], 1)
                wait_apart(pool, (q["c_km"], 2 * b + 1))
                G.tensor_scalar(kmh[:], h16[:], km[:], None, ALU.mult).then_inc(q["c_km"], 1)

            pool.wait_ge(ready, READY)
            pool.wait_ge(prep, PREP - 1)

            def slot(r, u, a, b, c, more):
                t = 2 * r + u
                if c:
                    rsqrt(pool, "lnB", t - 2, 1.0, EPS, norms["lnB"]["moments"], 2 * C)
                if c:
                    c_km(t - 2)
                    c_turn(t - 2)
                if a:
                    a_mx(t)
                    a_xb(t, u)
                if c:
                    rsqrt(pool, "lnC", t - 2, 1.0, 1e-12, norms["lnC"]["moments"], 2 * C)
                if a:
                    rsqrt(pool, "rms", t, 1.0 / DI, EPS, q["a_sq"], C)
                if c:
                    rsqrt(pool, "lnD", t - 2, 1.0, EPS, norms["lnD"]["moments"], 2 * C)
                if a:
                    rsqrt(pool, "ln1", t, 1.0, EPS, norms["ln1"]["moments"], 2 * C)
                    rsqrt(pool, "ln2", t, 1.0, EPS, norms["ln2"]["moments"], 2 * C)
                if more:
                    a_am(t + 1)

            a_am(0)
            slot(0, 0, True, False, False, True)
            slot(0, 1, True, True, False, True)
            with pool.Fori(1, NB // 2 - 1) as pair:
                for u in range(2):
                    slot(pair, u, True, True, True, True)
            slot(NB // 2 - 1, 0, True, True, True, True)
            slot(NB // 2 - 1, 1, True, True, True, False)
            slot(NB // 2, 0, False, True, True, False)
            slot(NB // 2, 1, False, False, True, False)


def soft_experts(nc, kept, x3_dram, x3T_dram, x3_stored, phi, W, b_exp, ident, out):
    y_dram = nc.dram_tensor("y_slots", (SB * NS, NB * XB * D), F32, kind="Internal").ap()
    y_stored = [kept.enter_context(nc.semaphore(f"y_stored{u}")) for u in range(2)]
    with ExitStack() as outer:
        def sb(name, shape, dt=F32):
            return outer.enter_context(nc.sbuf_tensor(name, [P] + shape, dt))

        shared = dict(id_f=sb("d_id", [P]), phf=sb("d_phf", [S]), phH=sb("d_phH", [S], F32R),
                      phL=sb("d_phL", [S], F32R), xtf=sb("e_xtf", [2, L]),
                      xt_in=[kept.enter_context(nc.semaphore(f"e_xt_in{u}")) for u in range(2)])
        with ExitStack() as ctx:
            dispatch(nc, ctx, kept, shared, x3_dram, x3T_dram, phi, W, b_exp, ident, y_dram, y_stored)
        with ExitStack() as ctx:
            combine(nc, ctx, kept, shared, x3_dram, x3T_dram, y_dram, out)


def dispatch(nc, ctx, kept, shared, x3_dram, x3T_dram, phi, W, b_exp, ident, y_dram, y_stored):
    def sb(name, shape, dt=F32):
        return ctx.enter_context(nc.sbuf_tensor(name, [P] + shape, dt))

    def sem(name):
        return kept.enter_context(nc.semaphore(name))

    id_f, phf = shared["id_f"], shared["phf"]
    id_r = sb("d_idr", [P], F32R)
    xtf = sb("d_xtf", [NB, C, P])
    xs = sb("d_xs", [TT, D])
    w = sb("d_w", [2, XB, D])
    bx = sb("d_bx", [SB * XB * D])
    mp = sb("d_mp", [BK, P])
    mxb = sb("d_mxb", [P])
    nH = sb("d_nH", [P], F32R)
    nL = sb("d_nL", [P], F32R)
    ex = sb("d_ex", [2, C, BK, BB, P])
    sm = sb("d_sm", [P])
    sr = sb("d_sr", [P])
    slot_s = sb("d_slot", [XB, BK, BB, NS])
    ys = sb("d_ys", [2, BK, XB, D])

    lg = ctx.enter_context(nc.psum_tensor("d_lg", [P, BK, BB, P], F32))
    sl = ctx.enter_context(nc.psum_tensor("d_sl", [P, BK, BB, P], F32))

    ready = sem("d_ready")
    late = sem("d_late")
    bx_in = sem("d_bx_in")
    x_in = [sem(f"d_x_in{c}") for c in range(C)]
    id_half = sem("d_id_half")
    w_in = [sem(f"d_w_in{u}") for u in range(2)]
    names = "lg_ps part max sub_ps ex sum mult slot_ps slot ys_ps ys y".split()
    q = {n: sem("d_" + n) for n in names}
    block = ctx.enter_context(nc.Block())
    READY = 16 * 2

    @block.sync
    def _(sp):
        sp.dma_start(phf[:, 0:P], phi[:, 0:P]).then_inc(ready, 16)
        sp.dma_start(id_f[:], ident).then_inc(ready, 16)
        for c in range(C):
            sp.dma_start(xtf[:, :, c, :], x3T_dram.rearrange("p (b c t) -> p b c t", c=C, t=P)[:, :, c, :]
                         ).then_inc(x_in[c], 16)
        sp.dma_start(phf[:, P:], phi[:, P:]).then_inc(late, 16)

        def load(s, u):
            for v in (BK * (s - 1), s * XB):
                sp.compute_val(v)
            sp.wait_ge(ready, READY)
            wait(sp, q["ys_ps"], BK * (s - 1))
            sp.dma_start(w[:, u, :, :], W[:, bass.ds(s * XB, XB), :]).then_inc(w_in[u], 16)

        def store(s, u):
            for v in (BK * (s + 1), s * NS):
                sp.compute_val(v)
            sp.wait_ge(ready, READY)
            wait(sp, q["y"], BK * (s + 1))
            for i in range(BB):
                batches = slice(i * BK * XB * D, (i + 1) * BK * XB * D)
                sp.dma_start(y_dram[bass.ds(s * NS, NS), batches],
                             ys[i * NS:(i + 1) * NS, u, :, :, :].rearrange("n k j e -> n (k j e)")
                             ).then_inc(y_stored[u], 16)

        load(0, 0)
        load(1, 1)
        sp.dma_start(xs[:], x3_dram.rearrange("(n p) d -> p n d", p=P)).then_inc(late, 16)
        sp.dma_start(bx[:], row(b_exp, S * D // NS)).then_inc(bx_in, 16)
        for u in range(2):
            sp.dma_start(shared["xtf"][:, u, :], x3T_dram[:, u * L:(u + 1) * L]).then_inc(shared["xt_in"][u], 16)
        with sp.Fori(1, SB // 2) as pair:
            for u in range(2):
                load(2 * pair + u, u)
                store(2 * pair + u - 2, u)
        for u in range(2):
            store(SB - 2 + u, u)
        for u in range(2):
            sp.wait_ge(y_stored[u], 16 * BB * (SB // 2))

    @block.tensor
    def _(pe):
        def logits(s, c):
            g = C * s + c
            cols = bass.ds(s * P, P)
            for k in range(BK):
                wait(pe, q["ex"], BK * (g - 1) + k + 1 if not isinstance(g, int) or g else 0)
                for i in range(BB):
                    b = BK * i + k
                    last = pe.matmul(lg[:, k, i, :], xtf[:, b, c, :], phf[:, cols], start=(i == 0), stop=False,
                                     skip_group_check=True)
                last.then_inc(q["lg_ps"], 1)

        def subtract(s, c):
            wait(pe, q["max"], 3 * (C * s + c) + 3)
            for k in range(BK):
                pe.matmul(lg[:, k, :, :], id_r[:], nH[:].unsqueeze(1).to_broadcast([P, BB, P]), start=False,
                          stop=False, skip_group_check=True)
                pe.matmul(lg[:, k, :, :], id_r[:], nL[:].unsqueeze(1).to_broadcast([P, BB, P]), start=False,
                          stop=True, skip_group_check=True).then_inc(q["sub_ps"], 1)

        def slots(s, u, c, ks):
            wait(pe, q["mult"], C * s + c + 1)
            for k in ks:
                if c == 0:
                    wait(pe, q["ys"], BK * (s - 1) + k + 1 if not isinstance(s, int) or s else 0)
                for i in range(BB):
                    last = pe.matmul(sl[:, k, i, :], xs[:, (BK * i + k) * C + c, :], ex[:, u, c, k, i, :],
                                     start=(c == 0 and i == 0), stop=(c == C - 1), skip_group_check=True)
                last.then_inc(q["slot_ps"], 1)

        def experts(s, u, r, ks):
            wait(pe, w_in[u], 16 * (r + 1))
            for k in ks:
                wait(pe, q["slot"], BK * s + k + 1)
                for j in range(XB):
                    last = pe.matmul(sl[:, k, j, :], slot_s[:, j, k, :, :], w[:, u, j, :], start=(j == 0), stop=True,
                                     skip_group_check=True)
                last.then_inc(q["ys_ps"], 1)

        def block_of(r, u):
            s = 2 * r + u
            known = isinstance(s, int)
            logits(s, 0)
            if not known or s >= 2:
                experts(s - 2, u, r - 1, (0, 1))
                slots(s - 2, u, 1, (2, 3))
            subtract(s, 0)
            if not known or s >= 2:
                experts(s - 2, u, r - 1, (2, 3))
            if not known or s >= 1:
                slots(s - 1, 1 - u, 0, (0, 1))
            if known and s == 0:
                pe.wait_ge(x_in[1], 16)
            logits(s, 1)
            if not known or s >= 1:
                slots(s - 1, 1 - u, 0, (2, 3))
            subtract(s, 1)
            if not known or s >= 1:
                slots(s - 1, 1 - u, 1, (0, 1))

        pe.wait_ge(ready, READY)
        pe.wait_ge(id_half, 1)
        pe.wait_ge(x_in[0], 16)
        block_of(0, 0)
        pe.wait_ge(late, 32)
        block_of(0, 1)
        with pe.Fori(1, SB // 2) as pair:
            for u in range(2):
                block_of(pair, u)
        r = SB // 2 - 1
        experts(SB - 2, 0, r, (0, 1))
        slots(SB - 2, 0, 1, (2, 3))
        experts(SB - 2, 0, r, (2, 3))
        slots(SB - 1, 1, 0, range(BK))
        slots(SB - 1, 1, 1, range(BK))
        experts(SB - 1, 1, r, range(BK))

    @block.scalar
    def _(act):
        def exps(s, u, c):
            g = C * s + c
            for k in range(BK):
                wait(act, q["sub_ps"], BK * g + k + 1)
                if k == 0:
                    wait(act, q["slot_ps"], BK * (g - 3) if not isinstance(s, int) or s >= 2 else 0)
                nc.scalar.activation(ex[:, u, c, k, :, :], lg[:, k, :, :], ACT.Exp).then_inc(q["ex"], 1)

        def slots(s, ks):
            for k in ks:
                wait(act, q["slot_ps"], BK * (C * s + 1) + k + 1)
                wait(act, q["ys_ps"], BK * (s - 1) + k + 1 if not isinstance(s, int) or s else 0)
                nc.scalar.activation(slot_s[:, :, k, :, :], sl[:, k, :, :].rearrange("p b (j n) -> p j b n", j=XB),
                                     ACT.Copy).then_inc(q["slot"], 1)

        def outputs(s, u, r, ks):
            for k in ks:
                wait(act, q["ys_ps"], BK * s + k + 1)
                if k == 0:
                    wait(act, y_stored[u], 16 * BB * r)
                nc.scalar.activation(ys[:, u, k, :, :], sl[:, k, :, :], ACT.Copy).then_inc(q["ys"], 1)

        act.wait_ge(ready, READY)
        nc.scalar.activation(id_r[:], id_f[:], ACT.Copy).then_inc(id_half, 1)

        def block_of(r, u):
            s = 2 * r + u
            known = isinstance(s, int)
            if not known or s >= 2:
                outputs(s - 2, u, r - 1, (0, 1))
                slots(s - 2, (2, 3))
            exps(s, u, 0)
            if not known or s >= 2:
                outputs(s - 2, u, r - 1, (2, 3))
            exps(s, u, 1)
            if not known or s >= 1:
                slots(s - 1, (0, 1))

        block_of(0, 0)
        act.wait_ge(late, 32)
        nc.scalar.activation(shared["phH"][:], phf[:], ACT.Copy).then_inc(id_half, 1)
        block_of(0, 1)
        for u in range(2):
            block_of(1, u)
        with act.Fori(2, SB // 2) as pair:
            for u in range(2):
                block_of(pair, u)
        r = SB // 2 - 1
        outputs(SB - 2, 0, r, (0, 1))
        slots(SB - 2, (2, 3))
        outputs(SB - 2, 0, r, (2, 3))
        slots(SB - 1, range(BK))
        outputs(SB - 1, 1, r, range(BK))

    @block.vector
    def _(dve):
        V = nc.vector

        def greatest(g):
            for k in range(BK):
                wait(dve, q["lg_ps"], BK * g + k + 1)
                if k == 0:
                    wait(dve, q["max"], 3 * g)
                V.tensor_reduce(mp[:, k, :], lg[:, k, :, :].rearrange("p b s -> p s b"), AX.X, ALU.max
                                ).then_inc(q["part"], 1)
            wait(dve, q["part"], BK * (g + 1))
            V.tensor_reduce(mxb[:], mp[:].rearrange("p k s -> p s k"), AX.X, ALU.max).then_inc(q["max"], 1)
            wait(dve, q["max"], 3 * g + 1)
            wait(dve, q["sub_ps"], BK * g)
            V.tensor_scalar(nH[:], mxb[:], -1.0, None, ALU.mult).then_inc(q["max"], 1)
            wait(dve, q["max"], 3 * g + 2)
            V.scalar_tensor_tensor(nL[:], mxb[:], -1.0, nH[:].bitcast(F32), ALU.mult, ALU.subtract
                                   ).then_inc(q["max"], 1)

        def scaled(g, u, c):
            wait(dve, q["ex"], BK * (g + 1))
            wait(dve, q["mult"], g)
            V.tensor_reduce(sm[:], ex[:, u, c, :, :, :].rearrange("p k b s -> p s (k b)"), AX.X, ALU.add
                            ).then_inc(q["sum"], 1)
            wait(dve, q["sum"], 2 * g + 1)
            V.reciprocal(sr[:], sm[:]).then_inc(q["sum"], 1)
            wait(dve, q["sum"], 2 * g + 2)
            e = ex[:, u, c, :, :, :].rearrange("p k b s -> p (k b) s")
            V.tensor_tensor(e, e, sr[:].unsqueeze(1).to_broadcast([P, NB, P]), ALU.mult).then_inc(q["mult"], 1)

        def block_of(s, u):
            greatest(C * s)
            if not isinstance(s, int) or s:
                scaled(C * s - 1, 1 - u, 1)
            greatest(C * s + 1)
            scaled(C * s, u, 0)

        block_of(0, 0)
        dve.wait_ge(id_half, 2)
        V.tensor_tensor(shared["phL"][:], phf[:], shared["phH"][:].bitcast(F32), ALU.subtract).then_inc(id_half, 1)
        block_of(1, 1)
        with dve.Fori(1, SB // 2) as pair:
            for u in range(2):
                block_of(2 * pair + u, u)
        scaled(C * SB - 1, 1, 1)

    @block.gpsimd
    def _(pool):
        def bias(s, u):
            for k in range(BK):
                pool.compute_val(BK * s + k + 1)
            pool.compute_val(s * XB * D)
            for k in range(BK):
                pool.wait_ge(bx_in, 16)
                wait(pool, q["ys"], BK * s + k + 1)
                y = ys[:, u, k, :, :].rearrange("p j e -> p (j e)")
                pool.tensor_tensor(y, y, bx[:, bass.ds(s * XB * D, XB * D)], ALU.add).then_inc(q["y"], 1)

        pool.wait_ge(bx_in, 16)
        bias(0, 0)
        bias(1, 1)
        with pool.Fori(1, SB // 2) as pair:
            for u in range(2):
                bias(2 * pair + u, u)


def combine(nc, ctx, kept, shared, x3_dram, x3T_dram, y_dram, out):
    def sb(name, shape, dt=F32):
        return ctx.enter_context(nc.sbuf_tensor(name, [P] + shape, dt))

    def sem(name):
        return kept.enter_context(nc.semaphore(name))

    id_f, phH, phL, xtf, xt_in = shared["id_f"], shared["phH"], shared["phL"], shared["xtf"], shared["xt_in"]
    xtH = sb("e_xtH", [2, L], F32R)
    xtL = sb("e_xtL", [2, L], F32R)
    xs = sb("e_xs", [2, C, D])
    yb = sb("e_yb", [2, SB, D])
    mxt = sb("e_mxt", [1])
    nmx = sb("e_nmx", [1])
    pr = sb("e_pr", [2, SB, P])
    prT = sb("e_prT", [SB, P])
    rs = sb("e_rs", [2])
    rr = sb("e_rr", [2])
    rx = sb("e_rx", [C, D])
    stt = sb("e_st", [C, 6])
    mv = sb("e_mv", [C, 2])
    v, h, y, t = (sb(f"e_n{k}", [C]) for k in range(4))
    xo = sb("e_xo", [2, C, D])

    lg = ctx.enter_context(nc.psum_tensor("e_lg", [P, 4, 512], F32))
    tp = [ctx.enter_context(nc.psum_tensor(f"e_tp{k}", [P, 512], F32)) for k in range(3)]
    po = ctx.enter_context(nc.psum_tensor("e_po", [P, 512], F32))

    b_in = [sem(f"e_b_in{u}") for u in range(2)]
    stored = [sem(f"e_stored{u}") for u in range(2)]
    q = {n: sem("e_" + n) for n in "xh xl lg_ps max pr tp_ps tp out_ps inv res moments rstd rows".split()}
    block = ctx.enter_context(nc.Block())
    LOADS = 16 * (1 + XB)

    def wait_apart(eng, *waits):
        for _, value in waits:
            eng.compute_val(value)
        eng.wait_ge(xt_in[0], 16)
        for s, value in waits:
            wait(eng, s, value)

    @block.sync
    def _(sp):
        def rows(b):
            return x3_dram[bass.ds(b * L, L), :].rearrange("(c p) d -> p c d", p=P)


        def load_xt(b, u):
            for value in (C * (b - 1), b * L):
                sp.compute_val(value)
            sp.wait_ge(xt_in[0], 16)
            wait(sp, q["lg_ps"], C * (b - 1))
            sp.dma_start(xtf[:, u, :], x3T_dram[:, bass.ds(b * L, L)]).then_inc(xt_in[u], 16)

        def load(b, u):
            for value in (C * (b - 1), b * L) + tuple(b * (XB * D) + j * D for j in range(XB)):
                sp.compute_val(value)
            sp.wait_ge(xt_in[0], 16)
            wait(sp, q["res"], C * (b - 1))
            sp.dma_start(xs[:, u, :, :], rows(b)).then_inc(b_in[u], 16)
            for j in range(XB):
                y_j = y_dram.rearrange("(k n) w -> n k w", n=NS)[:, :, bass.ds(b * (XB * D) + j * D, D)]
                sp.dma_start(yb[j * NS:(j + 1) * NS, u, :, :], y_j).then_inc(b_in[u], 16)

        def store(b, u):
            for value in (C * (b + 1), b * L):
                sp.compute_val(value)
            sp.wait_ge(xt_in[0], 16)
            wait(sp, q["rows"], C * (b + 1))
            sp.dma_start(out[bass.ds(b * L, L), :].rearrange("(c p) d -> p c d", p=P), xo[:, u, :, :]
                         ).then_inc(stored[u], 16)

        load(0, 0)
        load(1, 1)
        with sp.Fori(1, NB // 2) as pair:
            for u in range(2):
                load_xt(2 * pair + u, u)
                load(2 * pair + u, u)
                store(2 * pair + u - 2, u)
        for u in range(2):
            store(NB - 2 + u, u)
        for u in range(2):
            sp.wait_ge(stored[u], 16 * (NB // 2))

    @block.tensor
    def _(pe):
        def logits(b, u, c):
            n = C * b + c
            wait(pe, q["xl"], b + 1)
            wait(pe, q["pr"], n)
            cols = slice(c * P, (c + 1) * P)
            for k in range(4):
                part = slice(k * 512, (k + 1) * 512)
                pe.matmul(lg[:, k, :], xtH[:, u, cols], phH[:, part], start=True, stop=False, skip_group_check=True)
                pe.matmul(lg[:, k, :], xtH[:, u, cols], phL[:, part], start=False, stop=False,
                          skip_group_check=True)
                last = pe.matmul(lg[:, k, :], xtL[:, u, cols], phH[:, part], start=False, stop=True,
                                 skip_group_check=True)
            last.then_inc(q["lg_ps"], 1)

        def weigh(n, u, c):
            wait(pe, q["pr"], n + 1)
            for k in range(4):
                if k < 3:
                    wait(pe, q["tp"], 4 * (n - 1) + k + 2 if k < 2 else 4 * n)
                else:
                    wait(pe, q["tp"], 4 * n + 1)
                for j in range(4):
                    last = pe.transpose(tp[k % 3][:, j * P:(j + 1) * P], pr[:, c, 4 * k + j, :], id_f[:])
                last.then_inc(q["tp_ps"], 1)
            wait(pe, q["res"], n)
            for k in range(4):
                wait(pe, q["tp"], 4 * n + k + 1)
                for j in range(4):
                    s = 4 * k + j
                    last = pe.matmul(po[:, 0:D], prT[:, s, :], yb[:, u, s, :], start=(s == 0), stop=(s == SB - 1),
                                     skip_group_check=True)
            last.then_inc(q["out_ps"], 1)

        def batch(r, u, first=False):
            b = 2 * r + u
            logits(b, u, 0)
            if not first:
                weigh(C * b - 1, 1 - u, 1)
            logits(b, u, 1)
            pe.wait_ge(b_in[u], LOADS * (r + 1))
            weigh(C * b, u, 0)

        batch(0, 0, True)
        batch(0, 1)
        with pe.Fori(1, NB // 2) as pair:
            for u in range(2):
                batch(pair, u)
        weigh(TT - 1, 1, 1)

    @block.scalar
    def _(act):
        def split(b, u, r):
            wait(act, xt_in[u], 16 * (r + 1))
            wait(act, q["lg_ps"], C * (b - 1))
            nc.scalar.activation(xtH[:, u, :], xtf[:, u, :], ACT.Copy).then_inc(q["xh"], 1)

        def exps(n, c):
            wait(act, q["max"], 2 * (n + 1))
            wait(act, q["tp_ps"], 4 * (n - 1))
            wait(act, q["inv"], n - 1)
            nc.scalar.activation(pr[:, c, :, :].rearrange("p a s -> p (a s)"), lg[:].rearrange("p a s -> p (a s)"),
                                 ACT.Exp, bias=nmx[:], accum_out=rs[:, c:c + 1]).then_inc(q["pr"], 1)

        def turned(n, ks):
            for k in ks:
                wait(act, q["tp_ps"], 4 * n + k + 1)
                wait(act, q["out_ps"], n)
                nc.scalar.activation(prT[:, 4 * k:4 * k + 4, :].rearrange("p a s -> p (a s)"), tp[k % 3][:],
                                     ACT.Copy).then_inc(q["tp"], 1)

        def batch(r, u, first=False, more=True):
            b = 2 * r + u
            if not first:
                turned(C * b - 1, range(4))
            exps(C * b, 0)
            if more:
                split(b + 1, 1 - u, r + u)
            turned(C * b, range(4))
            exps(C * b + 1, 1)

        split(0, 0, 0)
        batch(0, 0, True)
        batch(0, 1)
        with act.Fori(1, NB // 2 - 1) as pair:
            for u in range(2):
                batch(pair, u)
        batch(NB // 2 - 1, 0)
        batch(NB // 2 - 1, 1, more=False)
        turned(TT - 1, range(4))

    @block.vector
    def _(dve):
        V = nc.vector

        def split(b, u):
            wait(dve, q["xh"], b + 1)
            wait(dve, q["lg_ps"], C * (b - 1))
            V.tensor_tensor(xtL[:, u, :], xtf[:, u, :], xtH[:, u, :].bitcast(F32), ALU.subtract
                            ).then_inc(q["xl"], 1)

        def greatest(n):
            wait(dve, q["lg_ps"], n + 1)
            wait(dve, q["max"], 2 * n)
            V.tensor_reduce(mxt[:], lg[:].rearrange("p a s -> p (a s)"), AX.X, ALU.max).then_inc(q["max"], 1)
            wait(dve, q["max"], 2 * n + 1)
            wait(dve, q["pr"], n)
            V.tensor_scalar(nmx[:], mxt[:], -1.0, None, ALU.mult).then_inc(q["max"], 1)

        def residual(n, u, c):
            wait(dve, q["pr"], n + 1)
            V.reciprocal(rr[:, c:c + 1], rs[:, c:c + 1]).then_inc(q["inv"], 1)
            wait(dve, q["inv"], n + 1)
            wait(dve, q["out_ps"], n + 1)
            V.scalar_tensor_tensor(rx[:, c, :], po[:, 0:D], rr[:, c:c + 1], xs[:, u, c, :], ALU.mult, ALU.add
                                   ).then_inc(q["res"], 1)
            wait(dve, q["res"], n + 1)
            V.bn_stats(stt[:, c, :], rx[:, c, :]).then_inc(q["moments"], 1)
            wait_apart(dve, (q["moments"], 2 * n + 1))
            V.bn_aggr(mv[:, c, :], stt[:, c, :]).then_inc(q["moments"], 1)

        def norm(b, u, r):
            wait(dve, q["rstd"], RSQRT_OPS * (b + 1))
            wait(dve, stored[u], 16 * r)
            for c in range(C):
                V.tensor_scalar(xo[:, u, c, :], rx[:, c, :], mv[:, c, 0:1], y[:, c:c + 1], ALU.subtract, ALU.mult
                                ).then_inc(q["rows"], 1)

        def batch(r, u, first=False, more=True):
            b = 2 * r + u
            greatest(C * b)
            if more:
                split(b + 1, 1 - u)
            if not first:
                residual(C * b - 1, 1 - u, 1)
            greatest(C * b + 1)
            if not first:
                norm(b - 1, 1 - u, r if u else r - 1)
            residual(C * b, u, 0)

        split(0, 0)
        batch(0, 0, True)
        batch(0, 1)
        with dve.Fori(1, NB // 2 - 1) as pair:
            for u in range(2):
                batch(pair, u)
        batch(NB // 2 - 1, 0)
        batch(NB // 2 - 1, 1, more=False)
        residual(TT - 1, 1, 1)
        norm(NB - 1, 1, NB // 2 - 1)

    @block.gpsimd
    def _(pool):
        pool.wait_ge(xt_in[0], 16)

        def batch(b):
            newton(pool, wait_apart, q["rstd"], RSQRT_OPS * b, (q["moments"], 2 * C * (b + 1)),
                   mv[:, :, 1], 1.0, EPS, v, h, y, t)

        batch(0)
        batch(1)
        with pool.Fori(1, NB // 2) as pair:
            for u in range(2):
                batch(2 * pair + u)


def constants():
    import numpy as np

    f = np.float32
    i = np.arange(P)
    ident = np.eye(P, dtype=f)
    causal = (i[:, None] <= i[None, :]).astype(f)
    neg = np.zeros((P, 3, P), f)
    later = i[None, :] > i[:, None]
    neg[:, 0][later] = NEG
    neg[:, 2][later] = NEG
    strict = (i[:, None] > i[None, :]).astype(f)
    head_of = (i[:, None] // WL == i[None, :] // WL).astype(f)
    rot = np.zeros((P, P), f)
    rot[i[1::2], i[0::2]] = -1.0
    rot[i[0::2], i[1::2]] = 1.0
    inv = (f(1.0) / np.power(f(10000.0), np.arange(0, D, 2, dtype=f) / f(D))).astype(f)
    ang = (np.arange(L, dtype=f)[:, None] * inv).astype(f)
    cosT = np.repeat(np.cos(ang.astype(np.float64)).astype(f).T, 2, axis=0)
    sinT = np.repeat(np.sin(ang.astype(np.float64)).astype(f).T, 2, axis=0)
    w8 = np.broadcast_to(np.arange(NE, 0, -1).astype(f), (P, NE))
    return dict(ident=ident, causal=causal, neg_blocks=neg, strict_low=strict, upper=causal, head_of=head_of,
                rot=rot, cosT=cosT, sinT=sinT, w8=w8)


def layout(d):
    import numpy as np

    x = np.asarray(d["L0_attn_x"]).reshape(NB * L, D)
    wq, wk, wv = (np.asarray(d[f"L1_attn_W{n}"]).T for n in "qkv")
    a = dict(
        x=x, xT=x.T, in_wT=np.asarray(d["L0_attn_in_proj_w"]).T,
        conv_w=np.asarray(d["L0_attn_conv_w"]).reshape(NCH, P, TAPS).transpose(1, 0, 2),
        conv_b=np.asarray(d["L0_attn_conv_b"]).reshape(NCH, P).T,
        dt_bias=d["L0_attn_dt_bias"], A_log=d["L0_attn_A_log"], Dh=d["L0_attn_D"],
        norm_w=np.asarray(d["L0_attn_norm_w"]).reshape(2, P).T,
        out_wT=np.asarray(d["L0_attn_out_proj_w"]).T.reshape(2, P, D).transpose(1, 0, 2),
        ln_w=d["L0_attn_ln_w"], ln_b=d["L0_attn_ln_b"],
        w_q=d["L0_ffn_w_q"], w_k=d["L0_ffn_w_k"], w_gate=d["L0_ffn_w_gate"],
        v_exp=np.asarray(d["L0_ffn_value_experts"]).transpose(2, 0, 1, 3).reshape(D, NE * HB * DH),
        o_exp=np.asarray(d["L0_ffn_output_experts"]).reshape(NE, HP, 2, DH, D).transpose(2, 3, 1, 0, 4)
        .reshape(P, HP, NE, D),
        WqkvT=np.concatenate([wq, wk, wv], axis=1),
        bq=d["L1_attn_bq"], bk=d["L1_attn_bk"], bv=d["L1_attn_bv"],
        gamma=d["L1_attn_gamma"], beta=d["L1_attn_beta"],
        phi=np.asarray(d["L1_ffn_phi"]).reshape(D, S),
        W=np.asarray(d["L1_ffn_W"]).transpose(1, 0, 2), b_exp=np.asarray(d["L1_ffn_b"]).reshape(-1),
    )
    a.update(constants())
    return {k: np.ascontiguousarray(v) for k, v in a.items()}


def kernel(**inputs):
    import numpy as np
    import concourse.bacc as bacc
    from concourse.bass_utils import run_bass_kernel_spmd

    nc = bacc.Bacc("TRN2", target_bir_lowering=False, num_devices=1)
    arrays = layout(inputs)
    aps = {k: nc.dram_tensor(k, v.shape, mybir.dt.from_np(v.dtype), kind="ExternalInput").ap()
           for k, v in arrays.items()}
    out = nc.dram_tensor("out", (NB * L, D), F32, kind="ExternalOutput").ap()
    build(nc, out=out, **aps)
    r = run_bass_kernel_spmd(nc, [arrays], core_ids=[0])
    return np.asarray(r.results[0]["out"]).reshape(NB, L, D)
```
